# Optimizing a Trainium2 kernel written in Bass

```python
import numpy as np
import jax
import jax.numpy as jnp

def _softmax(x, axis=-1):
    return jax.nn.softmax(x, axis=axis)

def _gelu(x):
    return jax.nn.gelu(x, approximate=True)

def _silu(x):
    return jax.nn.silu(x)

def _sigmoid(x):
    return jax.nn.sigmoid(x)

def _layernorm(x, axis=-1, eps=1e-05):
    m = jnp.mean(x, axis=axis, keepdims=True)
    v = jnp.var(x, axis=axis, keepdims=True)
    return (x - m) / jnp.sqrt(v + eps)

def _scatter_add(tgt, idx, src, axis=0):
    return tgt.at[idx].add(src)

def _segment_sum(src, seg, n):
    return jax.ops.segment_sum(src, seg, n)
kernel_name = 'mk_audio_tower_d1_tok_audfeat1024_r4_c34dae'

def setup_inputs(seed: int=0):
    np.random.seed(seed)
    _w = jnp.asarray

    def _rec_inputs():
        import jax
        import jax.numpy as jnp
        _rk = jax.random.key(seed)
        x = -7.10856e-05 + 0.999911 * jax.random.normal(jax.random.fold_in(_rk, 1), (16, 750, 256), jnp.float32)
        return x
    x = _rec_inputs()

    def _L0_tok_setup():
        import jax, jax.numpy as jnp
        import numpy as np

        def _layernorm(x, gamma, beta, eps=1e-05):
            mu = jnp.mean(x, axis=-1, keepdims=True)
            var = jnp.mean(jnp.square(x - mu), axis=-1, keepdims=True)
            return (x - mu) * jax.lax.rsqrt(var + eps) * gamma + beta
        key = jax.random.key(seed)
        ks = jax.random.split(key, 4)
        B, T, C = (16, 1024, 256)
        x = jax.random.normal(ks[0], (B, T, C), dtype=jnp.float32)
        fan_in = C * 2
        bound = 1.0 / np.sqrt(fan_in)
        conv_w = jax.random.uniform(ks[1], (C, C, 2), jnp.float32, -bound, bound)
        conv_b = jax.random.uniform(ks[2], (C,), jnp.float32, -bound, bound)
        fusion_ln_w = jnp.ones((C,), jnp.float32)
        fusion_ln_b = jnp.zeros((C,), jnp.float32)
        final_ln_w = jnp.ones((C,), jnp.float32)
        final_ln_b = jnp.zeros((C,), jnp.float32)
        return {'x': x, 'conv_w': conv_w, 'conv_b': conv_b, 'fusion_ln_w': fusion_ln_w, 'fusion_ln_b': fusion_ln_b, 'final_ln_w': final_ln_w, 'final_ln_b': final_ln_b}
    _L0_tok_all = _L0_tok_setup()
    _L0_tok_in = {k: v for k, v in _L0_tok_all.items() if k in ('conv_w', 'conv_b', 'fusion_ln_w', 'fusion_ln_b', 'final_ln_w', 'final_ln_b')}
    del _L0_tok_all

    def _L0_attn_setup():
        import jax, jax.numpy as jnp
        import numpy as np
        INIT_L = 512.0
        EPS = 1e-06
        N_HEAD = 16

        def fire_bias(T, w1, b1, w2, b2, c, L_multiplier):
            pos = jnp.arange(T, dtype=jnp.float32)
            rel = pos[:, None] - pos[None, :]
            threshold = jnp.abs(L_multiplier * INIT_L)
            pos_norm = jnp.maximum(pos, threshold)[:, None]
            rel = jnp.log(jnp.abs(c * rel) + 1.0)
            pos_norm = jnp.log(jnp.abs(c * pos_norm) + 1.0) + EPS
            nd = rel / pos_norm
            h = jax.nn.relu(nd[..., None] * w1[0] + b1)
            bias = jnp.einsum('tsw,wh->hts', h, w2) + b2[:, None, None]
            causal = jnp.tril(jnp.ones((T, T), dtype=bool))
            bias = jnp.where(causal[None], bias, -jnp.inf)
            return bias[None]
        key = jax.random.key(seed)
        ks = jax.random.split(key, 8)
        B, T, C, H, W = (2, 512, 256, 16, 32)
        s = 0.02
        return {'x': jax.random.normal(ks[0], (B, T, C), jnp.float32), 'Wqkv': jax.random.normal(ks[1], (C, 3 * C), jnp.float32) * s, 'bqkv': jnp.zeros((3 * C,), jnp.float32), 'Wproj': jax.random.normal(ks[2], (C, C), jnp.float32) * s, 'bproj': jnp.zeros((C,), jnp.float32), 'w1': jax.random.normal(ks[3], (1, W), jnp.float32), 'b1': jnp.zeros((W,), jnp.float32), 'w2': jax.random.normal(ks[4], (W, H), jnp.float32) * 0.1, 'b2': jnp.zeros((H,), jnp.float32), 'c_param': jnp.float32(0.1), 'L_multiplier': jnp.float32(1.0)}
    _L0_attn_all = _L0_attn_setup()
    _L0_attn_in = {k: v for k, v in _L0_attn_all.items() if k in ('Wqkv', 'bqkv', 'Wproj', 'bproj', 'w1', 'b1', 'w2', 'b2', 'c_param', 'L_multiplier')}
    del _L0_attn_all

    def _L0_ffn_setup():
        import jax, jax.numpy as jnp
        import numpy as np
        B, T, D, H, E, K = (2, 256, 256, 16, 8, 2)
        HS = D // H
        FF = 4 * D

        def layernorm(x, g, b, eps=1e-05):
            m = jnp.mean(x, axis=-1, keepdims=True)
            v = jnp.mean((x - m) ** 2, axis=-1, keepdims=True)
            return (x - m) * jax.lax.rsqrt(v + eps) * g + b
        key = jax.random.key(seed)
        ks = jax.random.split(key, 10)
        s = 0.02
        return {'x': jax.random.normal(ks[0], (B, T, D), jnp.float32), 'Wq': jax.random.normal(ks[1], (H, D, HS), jnp.float32) * s, 'Wk': jax.random.normal(ks[2], (H, D, HS), jnp.float32) * s, 'Wv': jax.random.normal(ks[3], (H, D, HS), jnp.float32) * s, 'gate_W': jax.random.normal(ks[4], (D, E), jnp.float32) * s, 'W1': jax.random.normal(ks[5], (E, D, FF), jnp.float32) * s, 'b1': jnp.zeros((E, FF), jnp.float32), 'W2': jax.random.normal(ks[6], (E, FF, D), jnp.float32) * s, 'b2': jnp.zeros((E, D), jnp.float32), 'ln1_g': jnp.ones((D,), jnp.float32), 'ln1_b': jnp.zeros((D,), jnp.float32), 'ln2_g': jnp.ones((D,), jnp.float32), 'ln2_b': jnp.zeros((D,), jnp.float32)}
    _L0_ffn_all = _L0_ffn_setup()
    _L0_ffn_in = {k: v for k, v in _L0_ffn_all.items() if k in ('Wq', 'Wk', 'Wv', 'gate_W', 'W1', 'b1', 'W2', 'b2', 'ln1_g', 'ln1_b', 'ln2_g', 'ln2_b')}
    del _L0_ffn_all
    return {'x': x, 'L0_tok_conv_w': _L0_tok_in['conv_w'], 'L0_tok_conv_b': _L0_tok_in['conv_b'], 'L0_tok_fusion_ln_w': _L0_tok_in['fusion_ln_w'], 'L0_tok_fusion_ln_b': _L0_tok_in['fusion_ln_b'], 'L0_tok_final_ln_w': _L0_tok_in['final_ln_w'], 'L0_tok_final_ln_b': _L0_tok_in['final_ln_b'], 'L0_attn_Wqkv': _L0_attn_in['Wqkv'], 'L0_attn_bqkv': _L0_attn_in['bqkv'], 'L0_attn_Wproj': _L0_attn_in['Wproj'], 'L0_attn_bproj': _L0_attn_in['bproj'], 'L0_attn_w1': _L0_attn_in['w1'], 'L0_attn_b1': _L0_attn_in['b1'], 'L0_attn_w2': _L0_attn_in['w2'], 'L0_attn_b2': _L0_attn_in['b2'], 'L0_attn_c_param': _L0_attn_in['c_param'], 'L0_attn_L_multiplier': _L0_attn_in['L_multiplier'], 'L0_ffn_Wq': _L0_ffn_in['Wq'], 'L0_ffn_Wk': _L0_ffn_in['Wk'], 'L0_ffn_Wv': _L0_ffn_in['Wv'], 'L0_ffn_gate_W': _L0_ffn_in['gate_W'], 'L0_ffn_W1': _L0_ffn_in['W1'], 'L0_ffn_b1': _L0_ffn_in['b1'], 'L0_ffn_W2': _L0_ffn_in['W2'], 'L0_ffn_b2': _L0_ffn_in['b2'], 'L0_ffn_ln1_g': _L0_ffn_in['ln1_g'], 'L0_ffn_ln1_b': _L0_ffn_in['ln1_b'], 'L0_ffn_ln2_g': _L0_ffn_in['ln2_g'], 'L0_ffn_ln2_b': _L0_ffn_in['ln2_b']}

def reference(x, L0_tok_conv_w, L0_tok_conv_b, L0_tok_fusion_ln_w, L0_tok_fusion_ln_b, L0_tok_final_ln_w, L0_tok_final_ln_b, L0_attn_Wqkv, L0_attn_bqkv, L0_attn_Wproj, L0_attn_bproj, L0_attn_w1, L0_attn_b1, L0_attn_w2, L0_attn_b2, L0_attn_c_param, L0_attn_L_multiplier, L0_ffn_Wq, L0_ffn_Wk, L0_ffn_Wv, L0_ffn_gate_W, L0_ffn_W1, L0_ffn_b1, L0_ffn_W2, L0_ffn_b2, L0_ffn_ln1_g, L0_ffn_ln1_b, L0_ffn_ln2_g, L0_ffn_ln2_b):
    import jax
    import jax.numpy as jnp

    def _L0_tok_ref(x, conv_w, conv_b, fusion_ln_w, fusion_ln_b, final_ln_w, final_ln_b):
        import jax, jax.numpy as jnp
        import numpy as np

        def _layernorm(x, gamma, beta, eps=1e-05):
            mu = jnp.mean(x, axis=-1, keepdims=True)
            var = jnp.mean(jnp.square(x - mu), axis=-1, keepdims=True)
            return (x - mu) * jax.lax.rsqrt(var + eps) * gamma + beta
        B, T, C = x.shape
        xp = x.reshape(B, T // 2, 2, C)
        x_fused = jnp.einsum('btkc,ock->bto', xp, conv_w) + conv_b
        x_fused = _layernorm(x_fused, fusion_ln_w, fusion_ln_b)
        x_skip = jnp.mean(xp, axis=2)
        out = jax.nn.gelu(x_fused + x_skip, approximate=False)
        return _layernorm(out, final_ln_w, final_ln_b)

    def _L0_attn_ref(x, Wqkv, bqkv, Wproj, bproj, w1, b1, w2, b2, c_param, L_multiplier):
        import jax, jax.numpy as jnp
        import numpy as np
        INIT_L = 512.0
        EPS = 1e-06
        N_HEAD = 16

        def fire_bias(T, w1, b1, w2, b2, c, L_multiplier):
            pos = jnp.arange(T, dtype=jnp.float32)
            rel = pos[:, None] - pos[None, :]
            threshold = jnp.abs(L_multiplier * INIT_L)
            pos_norm = jnp.maximum(pos, threshold)[:, None]
            rel = jnp.log(jnp.abs(c * rel) + 1.0)
            pos_norm = jnp.log(jnp.abs(c * pos_norm) + 1.0) + EPS
            nd = rel / pos_norm
            h = jax.nn.relu(nd[..., None] * w1[0] + b1)
            bias = jnp.einsum('tsw,wh->hts', h, w2) + b2[:, None, None]
            causal = jnp.tril(jnp.ones((T, T), dtype=bool))
            bias = jnp.where(causal[None], bias, -jnp.inf)
            return bias[None]
        B, T, C = x.shape
        H = N_HEAD
        hd = C // H
        qkv = x @ Wqkv + bqkv
        q, k, v = jnp.split(qkv, 3, axis=-1)
        q = q.reshape(B, T, H, hd).transpose(0, 2, 1, 3)
        k = k.reshape(B, T, H, hd).transpose(0, 2, 1, 3)
        v = v.reshape(B, T, H, hd).transpose(0, 2, 1, 3)
        bias = fire_bias(T, w1, b1, w2, b2, c_param, L_multiplier)
        scale = 1.0 / jnp.sqrt(jnp.float32(hd))
        att = jnp.einsum('bhqd,bhkd->bhqk', q, k) * scale + bias
        att = jax.nn.softmax(att, axis=-1)
        y = jnp.einsum('bhqk,bhkd->bhqd', att, v)
        y = y.transpose(0, 2, 1, 3).reshape(B, T, C)
        return y @ Wproj + bproj

    def _L0_ffn_ref(x, Wq, Wk, Wv, gate_W, W1, b1, W2, b2, ln1_g, ln1_b, ln2_g, ln2_b):
        import jax, jax.numpy as jnp
        import numpy as np
        B, T, D, H, E, K = (2, 256, 256, 16, 8, 2)
        HS = D // H
        FF = 4 * D

        def layernorm(x, g, b, eps=1e-05):
            m = jnp.mean(x, axis=-1, keepdims=True)
            v = jnp.mean((x - m) ** 2, axis=-1, keepdims=True)
            return (x - m) * jax.lax.rsqrt(v + eps) * g + b
        b, t, d = x.shape
        q = jnp.einsum('btd,hdf->bhtf', x, Wq)
        k = jnp.einsum('btd,hdf->bhtf', x, Wk)
        v = jnp.einsum('btd,hdf->bhtf', x, Wv)
        wei = jnp.einsum('bhtf,bhsf->bhts', q, k) * d ** (-0.5)
        mask = jnp.tril(jnp.ones((t, t), bool))
        wei = jnp.where(mask, wei, -jnp.inf)
        wei = jax.nn.softmax(wei, axis=-1)
        attn = jnp.einsum('bhts,bhsf->bhtf', wei, v)
        attn = attn.transpose(0, 2, 1, 3).reshape(b, t, d)
        y = x + layernorm(attn, ln1_g, ln1_b)
        flat = y.reshape(-1, d)
        logits = flat @ gate_W
        topv, topi = jax.lax.top_k(logits, K)
        w = jax.nn.softmax(topv, axis=-1)
        combine = jnp.sum(jax.nn.one_hot(topi, E, dtype=flat.dtype) * w[..., None], axis=1)
        h = jax.nn.relu(jnp.einsum('nd,edf->enf', flat, W1) + b1[:, None, :])
        eo = jnp.einsum('enf,efd->end', h, W2) + b2[:, None, :]
        moe = jnp.einsum('ne,end->nd', combine, eo)
        out = y + layernorm(moe.reshape(b, t, d), ln2_g, ln2_b)
        return out
    h = _L0_tok_ref(x, L0_tok_conv_w, L0_tok_conv_b, L0_tok_fusion_ln_w, L0_tok_fusion_ln_b, L0_tok_final_ln_w, L0_tok_final_ln_b)
    h = h + _L0_attn_ref(_layernorm(h, axis=-1), L0_attn_Wqkv, L0_attn_bqkv, L0_attn_Wproj, L0_attn_bproj, L0_attn_w1, L0_attn_b1, L0_attn_w2, L0_attn_b2, L0_attn_c_param, L0_attn_L_multiplier)
    h = h + _L0_ffn_ref(_layernorm(h, axis=-1), L0_ffn_Wq, L0_ffn_Wk, L0_ffn_Wv, L0_ffn_gate_W, L0_ffn_W1, L0_ffn_b1, L0_ffn_W2, L0_ffn_b2, L0_ffn_ln1_g, L0_ffn_ln1_b, L0_ffn_ln2_g, L0_ffn_ln2_b)
    return h

_drawn_inputs = setup_inputs


def setup_inputs(seed=0):
    import zlib

    import numpy as np

    out = dict(_drawn_inputs(seed))
    spreads = {'L0_tok_fusion_ln_w': (1.0, 0.2),
     'L0_tok_fusion_ln_b': (0.0, 0.1),
     'L0_tok_final_ln_w': (1.0, 0.2),
     'L0_tok_final_ln_b': (0.0, 0.1),
     'L0_attn_bqkv': (0.0, 0.1),
     'L0_attn_bproj': (0.0, 0.1),
     'L0_attn_b1': (0.0, 0.8),
     'L0_attn_b2': (0.0, 0.8),
     'L0_ffn_b1': (0.0, 0.1),
     'L0_ffn_b2': (0.0, 0.1),
     'L0_ffn_ln1_g': (1.0, 0.2),
     'L0_ffn_ln1_b': (0.0, 0.1),
     'L0_ffn_ln2_g': (1.0, 0.2),
     'L0_ffn_ln2_b': (0.0, 0.1)}
    factors = {'L0_attn_w1': 3.98, 'L0_attn_w2': 3.938}
    for name, (base, spread) in spreads.items():
        noise = np.random.default_rng([zlib.crc32(name.encode()), seed]).standard_normal(out[name].shape)
        drawn = base * np.exp(spread * noise) if base else spread * noise
        out[name] = jnp.asarray(drawn.astype(out[name].dtype))
    for name, factor in factors.items():
        out[name] = (out[name] * factor).astype(out[name].dtype)
    return out
```

```python
import concourse.bass as bass
from concourse import mybir
from concourse.alu_op_type import AluOpType as ALU
from contextlib import ExitStack

F32 = mybir.dt.float32
BF16 = mybir.dt.bfloat16
I32 = mybir.dt.int32
U32 = mybir.dt.uint32
ACT = mybir.ActivationFunctionType
AX_X = mybir.AxisListType.X

B, T_IN, C = 16, 750, 256
T = T_IN // 2
R = 125
NT = T // R
TILES = B * NT
KC = C // 128
H = 16
HD = C // H
W = 32
E = 8
FF = 4 * C
SEG = [R * i * (i + 1) // 2 for i in range(NT + 1)]
CAUSAL = SEG[NT]
BIG = 3.0e38
NEG = -1.0e30
INIT_L, BIAS_EPS, LN_EPS = 512.0, 1e-6, 1e-5
Q_PARTS = [0, 0, 0, 1, 1, 2]
K_PARTS = [0, 1, 2, 0, 1, 0]
STACK = len(Q_PARTS) * HD


def count(b, per, c):
    i, off = b
    const = off * per + c
    return const if i is None else i * (2 * per) + const


def wait(eng, sem, value):
    if not isinstance(value, int) or value > 0:
        eng.wait_ge(sem, value)


def wait_alone(eng, *pairs):
    pairs = [(sem, value) for sem, value in pairs if not isinstance(value, int) or value > 0]
    if any(not isinstance(value, int) for _, value in pairs):
        pairs = [(sem, value if isinstance(value, int) else eng.to_reg(value)) for sem, value in pairs]
        eng.wait_ge(pairs[0][0], 1)
    for sem, value in pairs:
        eng.wait_ge(sem, value)


def batches(eng, body, first=2, last=0):
    for n in range(first):
        body((None, n), n % 2)
    with eng.Fori(0, (B - first - last) // 2) as i:
        for par in range(2):
            body((i, first + par), par)
    for n in range(B - last, B):
        body((None, n), n % 2)


def half_count(b, per, c):
    i, off = b
    const = off // 2 * per + c
    return const if i is None else i * per + const


def before(b, n=1):
    return (b[0], b[1] - n)


def rows(b, j=0, n=1):
    at = count(b, NT, j)
    return slice(at, at + n) if isinstance(at, int) else bass.ds(at, n)


def row(b, j):
    at = count(b, NT, j)
    return at


class Memory:

    def __init__(self, nc, ctx, tag):
        self.nc, self.ctx, self.tag, self.sems = nc, ctx, tag, []
        ctx.callback(self.close)

    def close(self):
        if self.sems:
            self.nc.clear_and_free_semaphores(self.sems)
            self.nc.all_engine_barrier()

    def sb(self, name, shape, dt=F32):
        return self.ctx.enter_context(self.nc.sbuf_tensor(f"{self.tag}_{name}", shape, dt))

    def ps(self, name, shape, dt=F32):
        return self.ctx.enter_context(self.nc.psum_tensor(f"{self.tag}_{name}", shape, dt))

    def sem(self, name):
        self.sems.append(self.nc.alloc_semaphore(f"{self.tag}_{name}"))
        return self.sems[-1]


def constants(nc, mem):
    ident = mem.sb("ident", [128, 128])
    neghalf = mem.sb("neghalf", [128, NT])
    eps = mem.sb("eps", [128, NT])
    set_done, sel_done = mem.sem("set_done"), mem.sem("sel_done")
    with nc.Block() as block:

        @block.gpsimd
        def _(pool):
            pool.memset(neghalf[:, :], -0.5)
            pool.memset(eps[:, :], LN_EPS)
            pool.memset(ident[:, :], 0.0).then_inc(set_done, 1)
            pool.wait_ge(set_done, 1)
            pool.affine_select(out=ident[:, :], in_=ident[:, :], compare_op=ALU.not_equal, fill=1.0,
                               base=0, pattern=[[-1, 128]], channel_multiplier=1).then_inc(sel_done, 1)
    return ident, neghalf, eps


def tokenize(nc, ident, neghalf, eps, hid, x, conv_w, conv_b, g_fuse, b_fuse, g_fin, b_fin):
    with ExitStack() as ctx:
        m = Memory(nc, ctx, "tok")
        w_in = m.sb("w_in", [128, KC, C * 2])
        w_sb = m.sb("w", [128, 2 * KC, C])
        cb, gf, bf, gl, bl = (m.sb(n, [R, C]) for n in ("cb", "gf", "bf", "gl", "bl"))
        xin = m.sb("xin", [R, 2, NT, 2 * C])
        xT = m.sb("xT", [128, 2, 2 * KC, R])
        y = m.sb("y", [R, 2, NT, C])
        sk = m.sb("sk", [R, 2, NT, C])
        st = m.sb("st", [R, 2, NT, 6])
        mv = m.sb("mv", [R, 2, NT, 2])
        ve = m.sb("ve", [R, 2, NT])
        rs = m.sb("rs", [R, 2, NT])
        st2 = m.sb("st2", [R, 2, NT, 6])
        mv2 = m.sb("mv2", [R, 2, NT, 2])
        ve2 = m.sb("ve2", [R, 2, NT])
        rs2 = m.sb("rs2", [R, 2, NT])
        p_wt = m.ps("p_wt", [128, 512])
        p_xt = [m.ps(f"p_xt{n}", [128, 2 * KC, 128]) for n in range(2)]
        p_y = [m.ps(f"p_y{n}", [128, 512]) for n in range(2)]
        (consts_in, wt_full, wt_evac, xt_full, xt_ready, y_full, y_added, stats1, aggr1, eps1, rstd1,
         scaled1, gained1, fused, skip_sum, summed, gelu_done, stats2, aggr2, eps2, rstd2, scaled2, gained2,
         final) = (m.sem(n) for n in (
             "consts_in", "wt_full", "wt_evac", "xt_full", "xt_ready", "y_full", "y_added", "stats1", "aggr1",
             "eps1", "rstd1", "scaled1", "gained1", "fused", "skip_sum", "summed", "gelu_done", "stats2", "aggr2",
             "eps2", "rstd2", "scaled2", "gained2", "final"))
        x_in = [m.sem(f"x_in{n}") for n in range(2)]
        x_rows = x.rearrange("b t c -> (b t c)").rearrange("(g r c) -> r g c", r=R, c=2 * C)

        block = ctx.enter_context(nc.Block())

        @block.sync
        def _(sp):
            sp.dma_start(w_in[:, :, :], conv_w.rearrange("(o p) c k -> p o (c k)", p=128)).then_inc(consts_in, 16)
            for vec, sb in ((conv_b, cb), (g_fuse, gf), (b_fuse, bf), (g_fin, gl), (b_fin, bl)):
                sp.dma_start(sb[:, :], vec.rearrange("(a c) -> a c", a=1).to_broadcast([R, C])).then_inc(consts_in, 16)

            def load(b, par):
                wait_alone(sp, (xt_full, count(b, NT, -NT)),
                               (skip_sum, count(b, 1, -1)))
                sp.dma_start(xin[:, par, :, :], x_rows[:, rows(b, 0, NT), :]).then_inc(x_in[par], 16)

            batches(sp, load)

        @block.tensor
        def _(pe):
            pe.wait_ge(consts_in, 96)
            w_ck = w_in[:, :, :].rearrange("p o (c k) -> p o c k", k=2)
            for k in range(2):
                for c in range(KC):
                    n = k * KC + c
                    if n:
                        pe.wait_ge(wt_evac, n)
                    for o in range(KC):
                        mm = pe.transpose(p_wt[:, o * 128:(o + 1) * 128],
                                          w_ck[:, o, c * 128:(c + 1) * 128, k], ident[:, :])
                    mm.then_inc(wt_full, 1)
            pe.wait_ge(wt_evac, 2 * KC)

            def convolve(b, par):
                wait(pe, x_in[par], half_count(b, 16, 16))
                for j in range(NT):
                    q = (par * NT + j) % 2
                    wait(pe, xt_ready, count(b, NT, j - 1))
                    for k in range(2 * KC):
                        mm = pe.transpose(p_xt[q][:, k, 0:R], xin[:, par, j, k * 128:(k + 1) * 128],
                                          ident[0:R, 0:R])
                    mm.then_inc(xt_full, 1)
                    wait(pe, xt_ready, count(b, NT, j + 1))
                    wait(pe, y_added, count(b, NT, j - 1))
                    for k in range(2 * KC):
                        mm = pe.matmul(p_y[q][0:R, 0:C], xT[:, q, k, :], w_sb[:, k, :],
                                       start=(k == 0), stop=(k == 2 * KC - 1))
                    mm.then_inc(y_full, 1)

            batches(pe, convolve)

        @block.scalar
        def _(act):
            for n in range(2 * KC):
                act.wait_ge(wt_full, n + 1)
                act.activation(w_sb[:, n, :], p_wt[:, 0:C], ACT.Copy).then_inc(wt_evac, 1)

            def evacuate(b, par):
                for j in range(NT):
                    q = (par * NT + j) % 2
                    wait(act, xt_full, count(b, NT, j + 1))
                    wait(act, y_full, count(b, NT, j - 1))
                    act.activation(xT[:, q, :, :], p_xt[q][:, :, 0:R], ACT.Copy).then_inc(xt_ready, 1)
                wait(act, summed, count(b, 1, 1))
                act.activation(sk[:, par, :, :], sk[:, par, :, :], ACT.Gelu).then_inc(gelu_done, 1)

            batches(act, evacuate)

        @block.vector
        def _(dve):
            def norms(b, par):
                for j in range(NT):
                    q = (par * NT + j) % 2
                    wait(dve, y_full, count(b, NT, j + 1))
                    wait(dve, summed, count(b, 1, -1))
                    dve.tensor_tensor(y[:, par, j, :], p_y[q][0:R, 0:C], cb[:, :], ALU.add).then_inc(y_added, 1)
                for j in range(NT):
                    wait(dve, y_added, count(b, NT, j + 1))
                    dve.bn_stats(st[:, par, j, :], y[:, par, j, :]).then_inc(stats1, 1)
                for j in range(NT):
                    wait_alone(dve, (stats1, count(b, NT, j + 1)))
                    dve.bn_aggr(mv[:, par, j, :], st[:, par, j, :]).then_inc(aggr1, 1)
                wait(dve, x_in[par], half_count(b, 16, 16))
                wait(dve, scaled2, count(b, NT, -NT))
                dve.tensor_tensor(sk[:, par, :, :], xin[:, par, :, 0:C], xin[:, par, :, C:2 * C],
                                  ALU.add).then_inc(skip_sum, 1)
                wait(dve, rstd1, count(b, 1, 1))
                for j in range(NT):
                    dve.tensor_scalar(y[:, par, j, :], y[:, par, j, :], mv[:, par, j, 0:1], rs[:, par, j:j + 1],
                                      ALU.subtract, ALU.mult).then_inc(scaled1, 1)
                wait(dve, fused, count(b, 1, 1))
                wait(dve, skip_sum, count(b, 1, 1))
                dve.scalar_tensor_tensor(out=sk[:, par, :, :], in0=sk[:, par, :, :], scalar=0.5,
                                         in1=y[:, par, :, :], op0=ALU.mult, op1=ALU.add).then_inc(summed, 1)
                wait(dve, gelu_done, count(b, 1, 1))
                for j in range(NT):
                    dve.bn_stats(st2[:, par, j, :], sk[:, par, j, :]).then_inc(stats2, 1)
                for j in range(NT):
                    wait_alone(dve, (stats2, count(b, NT, j + 1)))
                    dve.bn_aggr(mv2[:, par, j, :], st2[:, par, j, :]).then_inc(aggr2, 1)
                wait(dve, rstd2, count(b, 1, 1))
                for j in range(NT):
                    dve.tensor_scalar(hid[:, row(b, j), :], sk[:, par, j, :], mv2[:, par, j, 0:1],
                                      rs2[:, par, j:j + 1], ALU.subtract, ALU.mult).then_inc(scaled2, 1)

            dve.wait_ge(consts_in, 96)
            batches(dve, norms)

        @block.gpsimd
        def _(pool):
            def over_tiles(v):
                return v[:, :].rearrange("p (a c) -> p a c", a=1).to_broadcast([R, NT, C])

            def gains(b, par):
                def rstd(mv, ve, rs, aggr, eps_done, rstd_done):
                    wait_alone(pool, (aggr, count(b, NT, NT)))
                    pool.tensor_tensor(ve[:, par, :], mv[:, par, :, 1], eps[0:R, :], ALU.add).then_inc(eps_done, 1)
                    wait_alone(pool, (eps_done, count(b, 1, 1)))
                    pool.tensor_tensor(rs[:, par, :], ve[:, par, :], neghalf[0:R, :], ALU.pow).then_inc(rstd_done, 1)

                rstd(mv, ve, rs, aggr1, eps1, rstd1)
                wait_alone(pool, (scaled1, count(b, NT, NT)))
                pool.tensor_tensor(y[:, par, :, :], y[:, par, :, :], over_tiles(gf), ALU.mult).then_inc(gained1, 1)
                wait_alone(pool, (gained1, count(b, 1, 1)))
                pool.tensor_tensor(y[:, par, :, :], y[:, par, :, :], over_tiles(bf), ALU.add).then_inc(fused, 1)
                rstd(mv2, ve2, rs2, aggr2, eps2, rstd2)
                wait_alone(pool, (scaled2, count(b, NT, NT)))
                hb = hid[:, rows(b, 0, NT), :]
                pool.tensor_tensor(hb, hb, over_tiles(gl), ALU.mult).then_inc(gained2, 1)
                wait_alone(pool, (gained2, count(b, 1, 1)))
                pool.tensor_tensor(hb, hb, over_tiles(bl), ALU.add).then_inc(final, 1)

            pool.wait_ge(consts_in, 96)
            batches(pool, gains)


def fire_bias(nc, bias, nd_dram, bias_dram, w1, b1, w2, b2, c_param, l_mult):
    G = 4
    PR = 128 // G
    STEP = 4
    CH = STEP * CAUSAL
    NMM = CH // 500
    with ExitStack() as ctx:
        m = Memory(nc, ctx, "bias")
        cpar = m.sb("cpar", [128, 1])
        lpar = m.sb("lpar", [128, 1])
        thr = m.sb("thr", [128, 1])
        rel = m.sb("rel", [128, CAUSAL])
        pos = m.sb("pos", [128, NT])
        nd = m.sb("nd", [128, CAUSAL])
        w1c = m.sb("w1c", [128, 1])
        b1c = m.sb("b1c", [128, 1])
        b2c = m.sb("b2c", [G * H, 1])
        w2g = m.sb("w2g", [128, G * H])
        nd_w = m.sb("nd_w", [128, 2, CH])
        hidden = m.sb("hidden", [128, 2, CH])
        outb = m.sb("outb", [G * H, 2, CH])
        pb = [m.ps(f"pb{n}", [G * H, 512]) for n in range(4)]
        (params_in, zeroed, w2_in, iota_done, rel_abs, rel_log, pos_max, pos_abs, pos_log, pos_eps, pos_inv, thr_done,
         nd_done, nd_out, hidden_done, mm_done, out_done, bias_in, masked) = (m.sem(n) for n in (
             "params_in", "zeroed", "w2_in", "iota_done", "rel_abs", "rel_log", "pos_max", "pos_abs", "pos_log",
             "pos_eps", "pos_inv", "thr_done", "nd_done", "nd_out", "hidden_done", "mm_done", "out_done", "bias_in",
             "masked"))
        nd_in = [m.sem(f"nd_in{n}") for n in range(2)]
        stored = [m.sem(f"stored{n}") for n in range(2)]
        block = ctx.enter_context(nc.Block())
        N = PR // STEP

        @block.sync
        def _(sp):
            sp.dma_start(cpar[:, :], c_param.to_broadcast([128, 1])).then_inc(params_in, 16)
            sp.dma_start(lpar[:, :], l_mult.to_broadcast([128, 1])).then_inc(params_in, 16)
            for g in range(G):
                sp.dma_start(w1c[g * W:(g + 1) * W, :], w1.rearrange("a w -> w a")).then_inc(params_in, 16)
                sp.dma_start(b1c[g * W:(g + 1) * W, :], b1.rearrange("(w a) -> w a", a=1)).then_inc(params_in, 16)
                sp.dma_start(b2c[g * H:(g + 1) * H, :], b2.rearrange("(h a) -> h a", a=1)).then_inc(params_in, 16)
            sp.wait_ge(zeroed, 1)
            for g in range(G):
                sp.dma_start(w2g[g * W:(g + 1) * W, g * H:(g + 1) * H], w2).then_inc(w2_in, 16)
            sp.wait_ge(nd_done, 3)
            sp.dma_start(nd_dram, nd[:, :]).then_inc(nd_out, 16)
            sp.wait_ge(nd_out, 16)
            for n in range(N + 1):
                if n < N:
                    if n >= 2:
                        sp.wait_ge(hidden_done, n - 1)
                    for g in range(G):
                        src = nd_dram[g * PR + n * STEP:g * PR + (n + 1) * STEP, :].rearrange("(a r) c -> a (r c)", a=1)
                        sp.dma_start(nd_w[g * W:(g + 1) * W, n % 2, :],
                                     src.to_broadcast([W, CH])).then_inc(nd_in[n % 2], 16)
                if n >= 1:
                    sp.wait_ge(out_done, NMM * n)
                    at = (n - 1) * STEP
                    for g in range(G):
                        dst = bias_dram[:, g * PR + at:g * PR + at + STEP, :].rearrange("h r c -> h (r c)")
                        sp.dma_start(dst, outb[g * H:(g + 1) * H, (n - 1) % 2, :]).then_inc(stored[(n - 1) % 2], 16)
            for n in range(2):
                sp.wait_ge(stored[n], 16 * G * N // 2)
            sp.dma_start(bias[:, :, :], bias_dram[:, 0:R, :].rearrange("h r c -> r h c")).then_inc(bias_in, 16)

        @block.gpsimd
        def _(pool):
            for i in range(NT):
                pool.iota(rel[:, SEG[i]:SEG[i + 1]], [[-1, R * (i + 1)]], base=R * i, channel_multiplier=1,
                          allow_small_or_imprecise_dtypes=True)
                pool.iota(pos[:, i:i + 1], [[0, 1]], base=R * i, channel_multiplier=1,
                          allow_small_or_imprecise_dtypes=True)
            pool.memset(w2g[:, :], 0.0).then_inc(zeroed, 1)
            pool.wait_ge(zeroed, 1)
            pool.nop().then_inc(iota_done, 1)
            pool.wait_ge(bias_in, 16)
            for i in range(NT):
                diag = bias[:, :, SEG[i] + R * i:SEG[i + 1]]
                pool.affine_select(out=diag, in_=diag, compare_op=ALU.is_ge, fill=NEG, base=0,
                                   pattern=[[0, H], [-1, R]], channel_multiplier=1).then_inc(masked, 1)

        @block.scalar
        def _(act):
            act.wait_ge(params_in, 16 * (2 + 3 * G))
            act.wait_ge(zeroed, 1)
            act.activation(thr[:, :], lpar[:, :], ACT.Abs, scale=INIT_L).then_inc(thr_done, 1)
            act.activation(rel[:, :], rel[:, :], ACT.Abs, scale=cpar[:, 0:1]).then_inc(rel_abs, 1)
            act.wait_ge(rel_abs, 1)
            act.activation(rel[:, :], rel[:, :], ACT.Ln, bias=1.0).then_inc(rel_log, 1)
            act.wait_ge(pos_max, 1)
            act.activation(pos[:, :], pos[:, :], ACT.Abs, scale=cpar[:, 0:1]).then_inc(pos_abs, 1)
            act.wait_ge(pos_abs, 1)
            act.activation(pos[:, :], pos[:, :], ACT.Ln, bias=1.0).then_inc(pos_log, 1)
            for n in range(N):
                act.wait_ge(nd_in[n % 2], 16 * G * (n // 2 + 1))
                if n >= 2:
                    act.wait_ge(mm_done, NMM * (n - 1))
                act.activation(hidden[:, n % 2, :], nd_w[:, n % 2, :], ACT.Relu, bias=b1c[:, 0:1],
                               scale=w1c[:, 0:1]).then_inc(hidden_done, 1)

        @block.vector
        def _(dve):
            dve.wait_ge(thr_done, 1)
            dve.tensor_scalar(pos[:, :], pos[:, :], thr[:, 0:1], None, ALU.max).then_inc(pos_max, 1)
            dve.wait_ge(pos_log, 1)
            dve.tensor_scalar(pos[:, :], pos[:, :], BIAS_EPS, None, ALU.add).then_inc(pos_eps, 1)
            dve.wait_ge(pos_eps, 1)
            dve.reciprocal(pos[:, :], pos[:, :]).then_inc(pos_inv, 1)
            dve.wait_ge(pos_inv, 1)
            dve.wait_ge(rel_log, 1)
            for i in range(NT):
                dve.tensor_scalar(nd[:, SEG[i]:SEG[i + 1]], rel[:, SEG[i]:SEG[i + 1]], pos[:, i:i + 1], None,
                                  ALU.mult).then_inc(nd_done, 1)
            for n in range(N):
                if n >= 2:
                    dve.wait_ge(stored[n % 2], 16 * G * (n // 2))
                for k in range(NMM):
                    u = n * NMM + k
                    dve.wait_ge(mm_done, u + 1)
                    dve.tensor_scalar(outb[:, n % 2, k * 500:(k + 1) * 500], pb[u % 4][:, 0:500], b2c[:, 0:1], None,
                                      ALU.add).then_inc(out_done, 1)

        @block.tensor
        def _(pe):
            pe.wait_ge(w2_in, 16 * G)
            for n in range(N):
                pe.wait_ge(hidden_done, n + 1)
                for k in range(NMM):
                    u = n * NMM + k
                    if u >= 4:
                        pe.wait_ge(out_done, u - 3)
                    pe.matmul(pb[u % 4][:, 0:500], w2g[:, :], hidden[:, n % 2, k * 500:(k + 1) * 500],
                              start=True, stop=True).then_inc(mm_done, 1)


def attention(nc, ident, neghalf, eps, hid, first, wq_in, wk_in, wv_in, scale, bias, tail):
    tag = "a" if first else "f"
    with ExitStack() as ctx:
        m = Memory(nc, ctx, tag)
        XW = NT * R
        wqk = m.sb("wqk", [128, KC, 2 * C])
        wv = m.sb("wv", [128, KC, C])
        wo = m.sb("wo", [128, KC, C]) if first else None
        wg = None if first else m.sb("wg", [128, KC, E])
        qkb = m.sb("qkb", [128, 2 * KC])
        vb = m.sb("vb", [R, C])
        ob = m.sb("ob", [R, C])
        ob2 = None if first else m.sb("ob2", [R, C])
        st = m.sb("st", [R, NT, 6])
        mv = m.sb("mv", [R, NT, 2])
        ve = m.sb("ve", [R, NT])
        rs = m.sb("rs", [R, NT])
        xn = m.sb("xn", [R, NT, C])
        xr = None if first else m.sb("xr", [R, 2, NT, C])
        xT = m.sb("xT", [128, KC, XW])
        f = m.sb("f", [128, 2, XW])
        w_stage = [v[:, :, :].rearrange("p a t -> p (a t)") for v in (f, xT)]
        part = [m.sb(f"part{n}", [128, 2 * KC, XW], BF16) for n in range(3)]
        qs = [m.sb(f"qs{n}", [STACK, H, XW], BF16) for n in range(2)]
        ks = [m.sb(f"ks{n}", [STACK, H, XW], BF16) for n in range(2)]
        VW = HD + 1
        OR = 32
        vx = [m.sb(f"vx{n}", [R, NT, H, VW]) for n in range(2)]
        sc = m.sb("sc", [R, 2, CAUSAL])
        nmx = m.sb("nmx", [R, 2, NT])
        pr = m.sb("pr", [R, 2, CAUSAL])
        pT = m.sb("pT", [R, 2, CAUSAL])
        oT = m.sb("oT", [128, XW])
        rden = m.sb("rden", [R, NT, 4])
        y = m.sb("y", [R, 2, NT, C])
        yT = xT if first else m.sb("yT", [128, KC, XW])
        p_s = [[m.ps(f"p_s{n}{u}", [128, 512]) for u in range(2)] for n in range(2)]
        p_t = [m.ps(f"p_t{u}", [128, 512]) for u in range(2)]
        p_o = m.ps("p_o", [128, 512])
        p_m = m.ps("p_m", [128, 512])
        S = {n: m.sem(n) for n in (
            "consts_in", "ones_set", "gaps_zeroed", "no_bias", "wqk_ready", "bias_scaled", "stats", "aggr", "eps_added", "rstd", "normed", "xt_full", "xt_ready",
            "qk_full", "f_ready", "part0", "residual1", "part1", "part2", "v_full", "v_ready", "scored", "biased",
            "exped", "pt_full", "ptx_ready", "pty_ready", "weighed", "o_evac", "o_back", "recip", "y_ready",
            "yt_full", "yt_ready", "out_full", "out_added", "tail_done")}
        S2 = {} if first else {n: m.sem(n) for n in ("stats_y", "aggr_y", "eps_y", "rstd_y", "normed_y", "gained",
                                                     "shifted", "summed", "resid_added", "wqkv_zero")}
        stacked = [m.sem(f"stacked{n}") for n in range(2)]
        y_out = [m.sem(f"y_out{n}") for n in range(2)]
        h_out = [m.sem(f"h_out{n}") for n in range(2)]
        if not first:
            y_st, y_mv = m.sb("y_st", [R, NT, 6]), m.sb("y_mv", [R, NT, 2])
            y_ve, y_rs = m.sb("y_ve", [R, NT]), m.sb("y_rs", [R, NT])

        N_CONST = tail["n_const"]
        PAIRS = [range(j, min(j + 2, NT)) for j in range(0, NT, 2)]
        NP = len(PAIRS)
        block = ctx.enter_context(nc.Block())

        @block.sync
        def _(sp):
            for k in range(KC):
                for n, w_ in enumerate((wq_in, wk_in, wv_in)):
                    dst = wv[:, k, :] if n == 2 else w_stage[k][:, n * C:(n + 1) * C]
                    if not first:
                        dst = dst.rearrange("p (h d) -> p h d", d=HD)
                    sp.dma_start(dst, w_(k)).then_inc(S["consts_in"], 16)
            tail["load"](sp, qkb, vb, ob, ob2, wo, wg, S["consts_in"])

            def stacks(b, par):
                for blk in range(2 * KC):
                    n = blk % 2
                    wait_alone(sp, (S["part2"], count(b, 2 * KC, blk + 1)),
                                   (S["scored"], count(b, 2 * H, -2 * H)))
                    to, parts = (qs, Q_PARTS) if blk < KC else (ks, K_PARTS)
                    at = blk % KC * (H // KC)
                    for r, c in enumerate(parts):
                        sp.dma_start(to[par][r * HD:(r + 1) * HD, at:at + H // KC, :],
                                     part[c][:, blk, :]).then_inc(stacked[n], 16)

            def body(b, par, prologue, epilogue):
                if prologue:
                    stacks((b[0], b[1] + 1), 1 - par)
                if epilogue and not first:
                    pb = before(b)
                    wait_alone(sp, (S2["summed"], count(pb, 1, 1)))
                    sp.dma_start(tail["y_rows"][:, rows(pb, 0, NT), :], y[:, 1 - par, :, :]).then_inc(y_out[1 - par], 16)
                    wait_alone(sp, (S2["resid_added"], count(pb, 1, 1)))
                    sp.dma_start(tail["h_rows"][:, rows(pb, 0, NT), :], hid[:, rows(pb, 0, NT), :]
                                 ).then_inc(h_out[1 - par], 16)

            run_batches(sp, lambda: stacks((None, 0), 0), body)
            if not first:
                sp.wait_ge(S2["summed"], B)
                sp.dma_start(tail["y_rows"][:, (B - 1) * NT:B * NT, :], y[:, 1, :, :]).then_inc(y_out[1], 16)
                sp.wait_ge(S2["resid_added"], B)
                sp.dma_start(tail["h_rows"][:, (B - 1) * NT:B * NT, :],
                             hid[:, (B - 1) * NT:B * NT, :]).then_inc(h_out[1], 16)
                for n in range(2):
                    sp.wait_ge(y_out[n], 16 * B // 2)
                    sp.wait_ge(h_out[n], 16 * B // 2)

        @block.tensor
        def _(pe):
            shared = {}

            def take_bank():
                if "by" in shared:
                    wait(pe, *shared["by"])

            def x_transpose(b, par, k):
                take_bank()
                wait(pe, S["normed"], count(b, NT, NT))
                wait(pe, S["v_full"], count(b, NP, 0))
                for j in range(NT):
                    mm = pe.transpose(p_m[:, j * R:(j + 1) * R], xn[:, j, k * 128:(k + 1) * 128], ident[0:R, 0:R])
                mm.then_inc(S["xt_full"], 1)
                shared["by"] = (S["xt_ready"], count(b, KC, k + 1))

            def qk_project(b, par, blk):
                take_bank()
                wait(pe, S["xt_ready"], count(b, KC, KC))
                for k in range(KC):
                    mm = pe.matmul(p_m[:, 0:XW], wqk[:, k, blk * 128:(blk + 1) * 128], xT[:, k, :],
                                   start=(k == 0), stop=(k == KC - 1))
                mm.then_inc(S["qk_full"], 1)
                shared["by"] = (S["f_ready"], count(b, 2 * KC, blk + 1))

            def v_project(b, par, p):
                take_bank()
                for n, j in enumerate(PAIRS[p]):
                    for k in range(KC):
                        mm = pe.matmul(p_m[0:R, n * C:(n + 1) * C], xT[:, k, j * R:(j + 1) * R], wv[:, k, :],
                                       start=(k == 0), stop=(k == KC - 1))
                mm.then_inc(S["v_full"], 1)
                shared["by"] = (S["v_ready"], count(b, NP, p + 1))

            def score(b, par, h):
                if h == 0:
                    for n in range(2):
                        wait(pe, stacked[n], count(b, 16 * KC * STACK // HD, 16 * KC * STACK // HD))
                for u, tiles in enumerate(((0, 1), (2,))):
                    wait(pe, S["biased"], count(b, H * NT, NT * (h - 2) + tiles[-1] + 1))
                    for i in tiles:
                        o = SEG[i] if u == 0 else 0
                        mm = pe.matmul(p_s[h % 2][u][0:R, o:o + R * (i + 1)], qs[par][:, h, i * R:(i + 1) * R],
                                       ks[par][:, h, 0:R * (i + 1)], start=True, stop=True)
                    mm.then_inc(S["scored"], 1)

            def transpose_probs(b, par, h):
                if h < 0:
                    b, par, h = before(b), 1 - par, h + H
                    if b[0] is None and b[1] < 0:
                        return
                wait(pe, S["exped"], count(b, H * NT, NT * h + NT))
                wait(pe, S["ptx_ready"], count(b, H, h))
                for i in range(NT):
                    mm = pe.transpose(p_t[0][0:R, i * R:(i + 1) * R], pr[:, h % 2, SEG[i]:SEG[i] + R], ident[0:R, 0:R])
                mm.then_inc(S["pt_full"], 1)
                wait(pe, S["pty_ready"], count(b, H, h))
                for o, (i, s) in enumerate(((1, 1), (2, 1), (2, 2))):
                    mm = pe.transpose(p_t[1][0:R, o * R:(o + 1) * R], pr[:, h % 2, SEG[i] + s * R:SEG[i] + (s + 1) * R],
                                      ident[0:R, 0:R])
                mm.then_inc(S["pt_full"], 1)

            def weigh(b, par, h):
                if h < 0:
                    b, par, h = before(b), 1 - par, h + H
                    if b[0] is None and b[1] < 0:
                        return
                q = h % 4
                if q == 0:
                    wait(pe, S["o_evac"], count(b, H // 4, h // 4))
                if h == 0:
                    wait(pe, S["v_ready"], count(b, NP, NP))
                wait(pe, S["ptx_ready"], count(b, H, h + 1))
                wait(pe, S["pty_ready"], count(b, H, h + 1))
                for s in range(NT):
                    at = (0, XW, 2 * XW - R)[s]
                    mm = pe.matmul(p_o[q * OR:q * OR + VW, s * R:XW], vx[par][:, s, h, :],
                                   pT[:, h % 2, at:at + XW - s * R], start=(s == 0), stop=(s == NT - 1))
                mm.then_inc(S["weighed"], 1)

            def outputs_back(b, par, g):
                take_bank()
                wait(pe, S["o_evac"], count(b, H // 4, g + 1))
                for j in range(NT):
                    mm = pe.transpose(p_m[0:R, j * 128:(j + 1) * 128], oT[:, j * R:(j + 1) * R], ident[:, :])
                mm.then_inc(S["o_back"], 1)
                shared["by"] = (S["y_ready"], count(b, H // 4, g + 1))

            def y_transpose(b, par, k):
                take_bank()
                if first:
                    wait(pe, S["y_ready"], count(b, H // 4, H // 4))
                else:
                    wait(pe, S2["summed"], count(b, 1, 1))
                for j in range(NT):
                    mm = pe.transpose(p_m[:, j * R:(j + 1) * R], y[:, par, j, k * 128:(k + 1) * 128], ident[0:R, 0:R])
                mm.then_inc(S["yt_full"], 1)
                shared["by"] = (S["yt_ready"], count(b, KC, k + 1))

            def out_project(b, par, p):
                take_bank()
                wait(pe, S["yt_ready"], count(b, KC, KC))
                for n, j in enumerate(PAIRS[p]):
                    for k in range(KC):
                        mm = pe.matmul(p_m[0:R, n * C:(n + 1) * C], yT[:, k, j * R:(j + 1) * R], wo[:, k, :],
                                       start=(k == 0), stop=(k == KC - 1))
                mm.then_inc(S["out_full"], 1)
                shared["by"] = (S["out_added"], count(b, NP, p + 1))

            def gate(b, par, _):
                take_bank()
                wait(pe, S["yt_ready"], count(b, KC, KC))
                for j in range(NT):
                    for k in range(KC):
                        mm = pe.matmul(p_m[0:R, j * E:(j + 1) * E], yT[:, k, j * R:(j + 1) * R], wg[:, k, :],
                                       start=(k == 0), stop=(k == KC - 1))
                mm.then_inc(S["out_full"], 1)
                shared["by"] = (S["out_added"], count(b, 1, 1))

            def own(n):
                return {6: [(outputs_back, 0)], 10: [(outputs_back, 1)], 14: [(outputs_back, 2)]}.get(n, [])

            pro = {1: [(x_transpose, 0)], 3: [(x_transpose, 1)], 4: [(qk_project, 0)], 5: [(qk_project, 1)],
                   7: [(qk_project, 2)], 8: [(qk_project, 3)], 9: [(v_project, 0)], 11: [(v_project, 1)]}
            epi = {12: [(y_transpose, 0)], 13: [(y_transpose, 1)], 15: [(out_project, 1) if first else (gate, 0)]}
            epi_early = {15: [(out_project, 0)]} if first else {}

            def body(b, par, prologue, epilogue):
                if b[0] is not None:
                    shared["by"] = (S["out_added"], count(before(b, 2), NP if first else 1, NP if first else 1))
                for n in range(H):
                    transpose_probs(b, par, n - 1)
                    if epilogue:
                        for step, arg in epi_early.get(n, []):
                            step(before(b), 1 - par, arg)
                    if n + 1 < H:
                        score(b, par, n + 1)
                    elif prologue:
                        score((b[0], b[1] + 1), 1 - par, 0)
                    weigh(b, par, n - 2)
                    if epilogue:
                        if n == 2:
                            outputs_back(before(b), 1 - par, 3)
                        for step, arg in epi.get(n, []):
                            step(before(b), 1 - par, arg)
                    for step, arg in own(n):
                        step(b, par, arg)
                    if prologue:
                        for step, arg in pro.get(n, []):
                            step((b[0], b[1] + 1), 1 - par, arg)

            def start():
                pe.wait_ge(S["consts_in"], 16 * N_CONST)
                pe.wait_ge(S["wqk_ready"], 2 * KC * KC)
                pe.wait_ge(S["gaps_zeroed"], 1)
                for n in range(H):
                    for step, arg in pro.get(n, []):
                        step((None, 0), 0, arg)
                score((None, 0), 0, 0)

            run_batches(pe, start, body)
            b, par = (None, B - 1), 1
            transpose_probs(b, par, H - 1)
            weigh(b, par, H - 2)
            weigh(b, par, H - 1)
            outputs_back(b, par, 3)
            for n in range(H):
                for step, arg in epi_early.get(n, []) + epi.get(n, []):
                    step(b, par, arg)

        @block.vector
        def _(dve):
            def norm_stats(b, par, _):
                for j in range(NT):
                    dve.bn_stats(st[:, j, :], hid[:, row(b, j), :]).then_inc(S["stats"], 1)
                for j in range(NT):
                    wait_alone(dve, (S["stats"], count(b, NT, j + 1)))
                    dve.bn_aggr(mv[:, j, :], st[:, j, :]).then_inc(S["aggr"], 1)

            def norm_scale(b, par, _):
                wait(dve, S["rstd"], count(b, 1, 1))
                wait(dve, S["xt_full"], count(b, KC, 0))
                if not first:
                    wait(dve, S2["shifted"], count(b, 1, 0))
                for j in range(NT):
                    dve.tensor_scalar(xn[:, j, :], hid[:, row(b, j), :], mv[:, j, 0:1], rs[:, j:j + 1],
                                      ALU.subtract, ALU.mult).then_inc(S["normed"], 1)

            def first_part(b, par, blk):
                n = blk % 2
                wait(dve, S["f_ready"], count(b, 2 * KC, blk + 1))
                free_part(dve, b, blk)
                dve.tensor_copy(part[0][:, blk, :], f[:, n, :]).then_inc(S["part0"], 1)

            def second_part(b, par, blk):
                n = blk % 2
                wait(dve, S["residual1"], count(b, 2 * KC, blk + 1))
                free_part(dve, b, blk)
                dve.tensor_copy(part[1][:, blk, :], f[:, n, :]).then_inc(S["part1"], 1)

            def values(b, par, p):
                wait(dve, S["v_full"], count(b, NP, p + 1))
                wait(dve, S["weighed"], count(b, H, -H))
                k = len(PAIRS[p])
                dve.tensor_tensor(vx[par][:, PAIRS[p][0]:PAIRS[p][0] + k, :, 0:HD],
                                  p_m[0:R, 0:k * C].rearrange("p (j h d) -> p j h d", h=H, d=HD),
                                  vb[:, :].rearrange("p (a h d) -> p a h d", a=1, d=HD).to_broadcast([R, k, H, HD]),
                                  ALU.add).then_inc(S["v_ready"], 1)

            def add_bias(b, par, h):
                for i in range(NT):
                    u, o = (0, SEG[i]) if i < 2 else (1, 0)
                    if i != 1:
                        wait_alone(dve, (S["scored"], count(b, 2 * H, 2 * h + u + 1)))
                    if i == 0:
                        wait_alone(dve, (S["exped"], count(b, NT * H, NT * (h - 1))))
                    dve.tensor_tensor_reduce(out=sc[:, h % 2, SEG[i]:SEG[i + 1]],
                                             in0=p_s[h % 2][u][0:R, o:o + R * (i + 1)], in1=bias(h, i),
                                             scale=-1.0, scalar=BIG, op0=ALU.add, op1=ALU.min,
                                             accum_out=nmx[:, h % 2, i:i + 1]).then_inc(S["biased"], 1)

            def probs_back(b, par, h):
                if h < 0:
                    b, par, h = before(b), 1 - par, h + H
                    if b[0] is None and b[1] < 0:
                        return
                wait(dve, S["pt_full"], count(b, 2 * H, 2 * h + 1))
                wait(dve, S["weighed"], count(b, H, h - 1))
                dve.tensor_copy(pT[:, h % 2, 0:XW], p_t[0][0:R, 0:XW]).then_inc(S["ptx_ready"], 1)

            def normalize(b, par, g):
                wait(dve, S["o_back"], count(b, H // 4, g + 1))
                o = p_m[0:R, 0:NT * 128].rearrange("p (j q v) -> p j q v", j=NT, q=4)
                wait(dve, S["y_ready"], count(b, H // 4, g))
                dve.reciprocal(rden[:, :, :], o[:, :, :, HD]).then_inc(S["recip"], 1)
                wait(dve, S["recip"], count(b, H // 4, g + 1))
                if first:
                    wait(dve, S["yt_full"], count(b, KC, -KC))
                else:
                    wait(dve, S["yt_full"], count(b, KC, -KC))
                    wait(dve, S2["resid_added"], count(b, 1, -1))
                    wait(dve, y_out[par], half_count(b, 16, 0))
                dst = y[:, par, :, g * 4 * HD:(g + 1) * 4 * HD].rearrange("p j (q d) -> p j q d", q=4)
                dve.tensor_tensor(dst, o[:, :, :, 0:HD],
                                  rden[:, :, :].rearrange("p j (q a) -> p j q a", a=1).to_broadcast([R, NT, 4, HD]),
                                  ALU.mult).then_inc(S["y_ready"], 1)

            def add_output(b, par, p):
                k = len(PAIRS[p])
                hb = hid[:, rows(b, PAIRS[p][0], k), :]
                wait(dve, S["out_full"], count(b, NP, p + 1))
                dve.tensor_tensor(hb, p_m[0:R, 0:k * C].rearrange("p (j c) -> p j c", c=C), hb,
                                  ALU.add).then_inc(S["out_added"], 1)

            def y_stats(b, par, _):
                wait(dve, S["y_ready"], count(b, H // 4, H // 4))
                for j in range(NT):
                    dve.bn_stats(y_st[:, j, :], y[:, par, j, :]).then_inc(S2["stats_y"], 1)
                for j in range(NT):
                    wait_alone(dve, (S2["stats_y"], count(b, NT, j + 1)))
                    dve.bn_aggr(y_mv[:, j, :], y_st[:, j, :]).then_inc(S2["aggr_y"], 1)

            def y_scale(b, par, _):
                wait(dve, S2["rstd_y"], count(b, 1, 1))
                for j in range(NT):
                    dve.tensor_scalar(y[:, par, j, :], y[:, par, j, :], y_mv[:, j, 0:1], y_rs[:, j:j + 1],
                                      ALU.subtract, ALU.mult).then_inc(S2["normed_y"], 1)

            def keep_logits(b, par, _):
                wait(dve, S["out_full"], count(b, 1, 1))
                dve.tensor_copy(tail["logits"][:, rows(b, 0, NT), :],
                                p_m[0:R, 0:NT * E].rearrange("p (j e) -> p j e", e=E)).then_inc(S["out_added"], 1)

            epi_start = {3: [(normalize, 3)]}
            epi_mid = {15: [(add_output, 0)]} if first else {}
            epi = {15: [(add_output, 1)]} if first else {3: [(y_stats, 0)], 5: [(y_scale, 0)], 15: [(keep_logits, 0)]}
            own = {7: [(normalize, 0)], 11: [(normalize, 1)], 15: [(normalize, 2)]}
            pro_start = {0: [(norm_stats, 0)], 1: [(norm_scale, 0)], 10: [(values, 0)], 12: [(values, 1)]}
            pro = {5: [(first_part, 0)], 6: [(second_part, 0), (first_part, 1)], 7: [(second_part, 1)],
                   8: [(first_part, 2)], 9: [(second_part, 2), (first_part, 3)], 10: [(second_part, 3)]}

            def body(b, par, prologue, epilogue):
                nxt, last = (b[0], b[1] + 1), before(b)

                def steps(table, at, p):
                    for step, arg in table:
                        step(at, p, arg)

                for n in range(H):
                    add_bias(b, par, n)
                    if prologue:
                        steps(pro_start.get(n, []), nxt, 1 - par)
                    if epilogue:
                        steps(epi_start.get(n, []), last, 1 - par)
                    steps(own.get(n, []), b, par)
                    if epilogue:
                        steps(epi_mid.get(n, []), last, 1 - par)
                    probs_back(b, par, n - 1)
                    if epilogue:
                        steps(epi.get(n, []), last, 1 - par)
                    if prologue:
                        steps(pro.get(n, []), nxt, 1 - par)

            def start():
                dve.wait_ge(S["consts_in"], 16 * N_CONST)
                for k in range(KC):
                    for n in range(2 * KC):
                        dve.tensor_copy(wqk[:, k, n * 128:(n + 1) * 128].rearrange("p (d h) -> p d h", d=HD),
                                        w_stage[k][:, n * 128:(n + 1) * 128].rearrange("p (h d) -> p d h", d=HD)
                                        ).then_inc(S["wqk_ready"], 1)
                if not first:
                    dve.wait_ge(S["no_bias"], 2)
                dve.tensor_scalar(qkb[:, 0:KC], qkb[:, 0:KC], scale, None, ALU.mult).then_inc(S["bias_scaled"], 1)
                dve.memset(p_o[:, :], 0.0).then_inc(S["gaps_zeroed"], 1)
                dve.wait_ge(S["ones_set"], 2)
                for n in range(H):
                    for step, arg in pro_start.get(n, []) + pro.get(n, []):
                        step((None, 0), 0, arg)

            def free_part(eng, b, blk):
                wait(eng, stacked[blk % 2], count(b, 16 * KC * STACK // HD, 16 * STACK // HD * (blk // 2 + 1 - KC)))

            run_batches(dve, start, body)
            b, par = (None, B - 1), 1
            probs_back(b, par, H - 1)
            for n in range(H):
                for step, arg in epi_start.get(n, []) + epi_mid.get(n, []) + epi.get(n, []):
                    step(b, par, arg)

        @block.scalar
        def _(act):
            def x_back(b, par, k):
                wait(act, S["xt_full"], count(b, KC, k + 1))
                if first:
                    wait(act, S["out_full"], count(b, NP, -2 * NP))
                wait(act, S["v_full"], count(b, NP, 0))
                act.activation(xT[:, k, :], p_m[:, 0:XW], ACT.Copy).then_inc(S["xt_ready"], 1)

            def qk_back(b, par, blk):
                n = blk % 2
                wait(act, S["qk_full"], count(b, 2 * KC, blk + 1))
                wait(act, S["part2"], count(b, 2 * KC, blk - 1))
                act.activation(f[:, n, :], p_m[:, 0:XW], ACT.Identity, bias=qkb[:, blk:blk + 1],
                               scale=(scale if blk < KC else 1.0)).then_inc(S["f_ready"], 1)

            def exponentiate(b, par, h):
                for i in range(NT):
                    wait(act, S["biased"], count(b, NT * H, NT * h + i + 1))
                    if i == 0:
                        wait(act, S["pt_full"], count(b, 2 * H, 2 * (h - 1)))
                    act.activation(pr[:, h % 2, SEG[i]:SEG[i + 1]], sc[:, h % 2, SEG[i]:SEG[i + 1]], ACT.Exp,
                                   bias=nmx[:, h % 2, i:i + 1], scale=-1.0).then_inc(S["exped"], 1)

            def probs_back(b, par, h):
                if h < 0:
                    b, par, h = before(b), 1 - par, h + H
                    if b[0] is None and b[1] < 0:
                        return
                wait(act, S["pt_full"], count(b, 2 * H, 2 * h + 2))
                wait(act, S["weighed"], count(b, H, h - 1))
                act.activation(pT[:, h % 2, XW:2 * XW], p_t[1][0:R, 0:XW], ACT.Copy).then_inc(S["pty_ready"], 1)

            def outputs_out(b, par, g):
                wait(act, S["weighed"], count(b, H, 4 * g + 4))
                wait(act, S["o_back"], count(b, H // 4, g))
                act.activation(oT[:, :], p_o[:, 0:XW], ACT.Copy).then_inc(S["o_evac"], 1)

            def y_back(b, par, k):
                wait(act, S["yt_full"], count(b, KC, k + 1))
                wait(act, S["out_full"], count(b, NP if first else 1, 0))
                if first and (b[0] is not None or b[1] < B - 2):
                    wait(act, S["v_full"], count(b, NP, 3 * NP))
                act.activation(yT[:, k, :], p_m[:, 0:XW], ACT.Copy).then_inc(S["yt_ready"], 1)

            epi = {2: [(outputs_out, 3)], 13: [(y_back, 0)], 14: [(y_back, 1)]}
            own = {6: [(outputs_out, 0)], 10: [(outputs_out, 1)], 14: [(outputs_out, 2)]}
            pro = {2: [(x_back, 0)], 4: [(x_back, 1)], 5: [(qk_back, 0)], 6: [(qk_back, 1)], 8: [(qk_back, 2)],
                   9: [(qk_back, 3)]}

            def body(b, par, prologue, epilogue):
                for n in range(H):
                    if epilogue:
                        for step, arg in epi.get(n, []):
                            step(before(b), 1 - par, arg)
                    for step, arg in own.get(n, []):
                        step(b, par, arg)
                    if prologue:
                        for step, arg in pro.get(n, []):
                            step((b[0], b[1] + 1), 1 - par, arg)
                    exponentiate(b, par, n)
                    probs_back(b, par, n - 1)

            def start():
                act.wait_ge(S["bias_scaled"], 1)
                act.wait_ge(S["wqk_ready"], 2 * KC * KC)
                for n in range(H):
                    for step, arg in pro.get(n, []):
                        step((None, 0), 0, arg)

            run_batches(act, start, body)
            b, par = (None, B - 1), 1
            probs_back(b, par, H - 1)
            for n in range(H):
                for step, arg in epi.get(n, []):
                    step(b, par, arg)

        @block.gpsimd
        def _(pool):
            def root(b, par, _):
                wait_alone(pool, (S["aggr"], count(b, NT, NT)))
                pool.tensor_tensor(ve[:, :], mv[:, :, 1], eps[0:R, :], ALU.add).then_inc(S["eps_added"], 1)
                wait_alone(pool, (S["eps_added"], count(b, 1, 1)),
                                 (S["normed"], count(b, NT, 0)))
                pool.tensor_tensor(rs[:, :], ve[:, :], neghalf[0:R, :], ALU.pow).then_inc(S["rstd"], 1)

            def residual(b, par, blk):
                n = blk % 2
                wait_alone(pool, (S["part0"], count(b, 2 * KC, blk + 1)))
                pool.tensor_tensor(f[:, n, :], f[:, n, :], part[0][:, blk, :], ALU.subtract).then_inc(S["residual1"], 1)

            def third_part(b, par, blk):
                n = blk % 2
                wait_alone(pool, (S["part1"], count(b, 2 * KC, blk + 1)),
                                 (stacked[n], count(b, 16 * KC * STACK // HD, 16 * STACK // HD * (blk // 2 + 1 - KC))))
                pool.tensor_tensor(part[2][:, blk, :], f[:, n, :], part[1][:, blk, :],
                                   ALU.subtract).then_inc(S["part2"], 1)

            def over_tiles(v):
                return v[:, :].rearrange("p (a c) -> p a c", a=1).to_broadcast([R, NT, C])

            def output_bias(b, par, _):
                wait_alone(pool, (S["out_added"], count(b, NP, NP)))
                hb = hid[:, rows(b, 0, NT), :]
                pool.tensor_tensor(hb, hb, over_tiles(ob), ALU.add).then_inc(S["tail_done"], 1)

            def root_y(b, par, _):
                wait_alone(pool, (S2["aggr_y"], count(b, NT, NT)))
                pool.tensor_tensor(y_ve[:, :], y_mv[:, :, 1], eps[0:R, :], ALU.add).then_inc(S2["eps_y"], 1)
                wait_alone(pool, (S2["eps_y"], count(b, 1, 1)),
                                 (S2["normed_y"], count(b, NT, 0)))
                pool.tensor_tensor(y_rs[:, :], y_ve[:, :], neghalf[0:R, :], ALU.pow).then_inc(S2["rstd_y"], 1)

            def shift(b, par, _):
                wait_alone(pool, (S["normed"], count(b, NT, NT)),
                                 (S2["summed"], count(b, 1, -1)))
                pool.tensor_tensor(xr[:, par, :, :], xn[:, :, :], over_tiles(ob2), ALU.add).then_inc(S2["shifted"], 1)

            def gain(b, par, _):
                yb = y[:, par, :, :]
                wait_alone(pool, (S2["normed_y"], count(b, NT, NT)))
                pool.tensor_tensor(yb, yb, over_tiles(ob), ALU.mult).then_inc(S2["gained"], 1)
                wait_alone(pool, (S2["gained"], count(b, 1, 1)))
                pool.tensor_tensor(yb, yb, xr[:, par, :, :], ALU.add).then_inc(S2["summed"], 1)

            def add_residual(b, par, _):
                wait_alone(pool, (S2["summed"], count(b, 1, 1)))
                hb = hid[:, rows(b, 0, NT), :]
                pool.tensor_tensor(hb, hb, y[:, par, :, :], ALU.add).then_inc(S2["resid_added"], 1)

            epi = {15: [(output_bias, 0)]} if first else {3: [(root_y, 0)], 10: [(gain, 0)], 12: [(add_residual, 0)]}
            pro = {0: [(root, 0)], 5: [(residual, 0)], 6: [(third_part, 0), (residual, 1)], 7: [(third_part, 1)],
                   8: [(residual, 2)], 9: [(third_part, 2), (residual, 3)], 10: [(third_part, 3)]}
            if not first:
                pro[14] = [(shift, 0)]

            def body(b, par, prologue, epilogue):
                for n in range(H):
                    if epilogue:
                        for step, arg in epi.get(n, []):
                            step(before(b), 1 - par, arg)
                    if prologue:
                        for step, arg in pro.get(n, []):
                            step((b[0], b[1] + 1), 1 - par, arg)

            def start():
                if not first:
                    pool.memset(qkb[:, :], 0.0).then_inc(S["no_bias"], 1)
                    pool.memset(vb[:, :], 0.0).then_inc(S["no_bias"], 1)
                for n in range(2):
                    pool.memset(vx[n][:, :, :, HD:VW], 1.0).then_inc(S["ones_set"], 1)
                pool.wait_ge(S["consts_in"], 16 * N_CONST)
                for n in range(H):
                    for step, arg in pro.get(n, []):
                        step((None, 0), 0, arg)

            run_batches(pool, start, body)
            for n in range(H):
                for step, arg in epi.get(n, []):
                    step((None, B - 1), 1, arg)


def run_batches(eng, start, body):
    start()
    body((None, 0), 0, True, False)
    body((None, 1), 1, True, True)
    with eng.Fori(0, (B - 4) // 2) as i:
        for par in range(2):
            body((i, 2 + par), par, True, True)
    body((None, B - 2), 0, True, True)
    body((None, B - 1), 1, False, True)


def attend(nc, ident, neghalf, eps, hid, bias, wqkv, bqkv, wproj, bproj):
    def load(sp, qkb, vb, ob, ob2, wo, wg, consts_in):
        for n in range(2 * KC):
            sp.dma_start(qkb[:, n:n + 1], bqkv[n * 128:(n + 1) * 128].rearrange("(h d a) -> d h a", d=HD, a=1),
                         allow_slow_non_contiguous=True).then_inc(consts_in, 16)
        for vec, sb in ((bqkv[2 * C:3 * C], vb), (bproj, ob)):
            sp.dma_start(sb[:, :], vec.rearrange("(a c) -> a c", a=1).to_broadcast([R, C])).then_inc(consts_in, 16)
        sp.dma_start(wo[:, :, :], wproj.rearrange("(k p) n -> p k n", p=128)).then_inc(consts_in, 16)

    cols = [lambda k, n=n: wqkv[k * 128:(k + 1) * 128, n * C:(n + 1) * C] for n in range(3)]
    attention(nc, ident, neghalf, eps, hid, True, *cols, float(HD) ** -0.5,
              lambda h, i: bias[:, h, SEG[i]:SEG[i + 1]], {"load": load, "n_const": 5 * KC + 3})


def attend_in_ffn(nc, ident, neghalf, eps, hid, logits, y_dram, h_dram, wq, wk, wv, gate_w, g1, b1):
    with ExitStack() as ctx:
        m = Memory(nc, ctx, "mask")
        mask = m.sb("mask", [R, CAUSAL])
        zeroed, masked = m.sem("zeroed"), m.sem("masked")
        with nc.Block() as block:

            @block.gpsimd
            def _(pool):
                pool.memset(mask[:, :], 0.0).then_inc(zeroed, 1)
                pool.wait_ge(zeroed, 1)
                for i in range(NT):
                    diag = mask[:, SEG[i] + R * i:SEG[i + 1]]
                    pool.affine_select(out=diag, in_=diag, compare_op=ALU.is_ge, fill=NEG, base=0,
                                       pattern=[[-1, R]], channel_multiplier=1).then_inc(masked, 1)

        def load(sp, qkb, vb, ob, ob2, wo, wg, consts_in):
            for vec, sb in ((g1, ob), (b1, ob2)):
                sp.dma_start(sb[:, :], vec.rearrange("(a c) -> a c", a=1).to_broadcast([R, C])).then_inc(consts_in, 16)
            sp.dma_start(wg[:, :, :], gate_w.rearrange("(k p) n -> p k n", p=128)).then_inc(consts_in, 16)

        cols = [lambda k, w=w: w[:, k * 128:(k + 1) * 128, :].rearrange("h p d -> p h d") for w in (wq, wk, wv)]
        attention(nc, ident, neghalf, eps, hid, False, *cols, float(C) ** -0.5,
                  lambda h, i: mask[:, SEG[i]:SEG[i + 1]],
                  {"load": load, "n_const": 3 * KC + 3, "logits": logits,
                   "y_rows": y_dram.rearrange("(g r) c -> r g c", r=R),
                   "h_rows": h_dram.rearrange("(g r) c -> r g c", r=R)})


N_TOK = B * T
SLOT = 128
SLOT_TILES = (2 * N_TOK + E * (SLOT - 1)) // SLOT
ROWW = C + 1
DUMP = 2 * N_TOK
N_RES = DUMP + SLOT_TILES * SLOT


def clear_slots(nc, slots_dram):
    CH = 17
    with ExitStack() as ctx:
        m = Memory(nc, ctx, "clr")
        empty = [m.sb(f"empty{n}", [SLOT, CH, ROWW]) for n in range(2)]
        zeroed, numbered = m.sem("zeroed"), m.sem("numbered")
        stored = [m.sem(f"stored{n}") for n in range(2)]
        chunks = [(t, min(CH, SLOT_TILES - t)) for t in range(0, SLOT_TILES, CH)]
        dst = slots_dram.rearrange("(t p) c -> p t c", p=SLOT)
        with nc.Block() as block:

            @block.vector
            def _(dve):
                for n in range(2):
                    dve.memset(empty[n][:, :, 0:C], 0.0).then_inc(zeroed, 1)

            @block.gpsimd
            def _(pool):
                for n, (t, k) in enumerate(chunks):
                    if n >= 2:
                        pool.wait_ge(stored[n % 2], 16 * (n // 2))
                    pool.iota(empty[n % 2][:, 0:k, C].bitcast(I32), [[SLOT, k]], base=DUMP + SLOT * t,
                              channel_multiplier=1).then_inc(numbered, 1)

            @block.sync
            def _(sp):
                sp.wait_ge(zeroed, 2)
                for n, (t, k) in enumerate(chunks):
                    sp.wait_ge(numbered, n + 1)
                    sp.dma_start(dst[:, t:t + k, :], empty[n % 2][:, 0:k, :]).then_inc(stored[n % 2], 16)
                for n in range(2):
                    sp.wait_ge(stored[n], 16 * ((len(chunks) + 1 - n) // 2))


def route(nc, logits, weights, expert_of, y_dram, slots_dram, load_weights):
    with ExitStack() as ctx:
        m = Memory(nc, ctx, "route")
        GE = TILES * E
        NC_ = -(-N_TOK // SLOT)
        eid = m.sb("eid", [R, TILES, E])
        upper = m.sb("upper", [R, 128])
        ones = m.sb("ones", [R, 128])
        top = m.sb("top", [R, 2, TILES])
        lg2 = m.sb("lg2", [R, TILES, E])
        eq = m.sb("eq", [R, TILES, E])
        idx = m.sb("idx", [R, 2, TILES])
        hot = m.sb("hot", [R, 2, TILES, E])
        both = m.sb("both", [R, TILES, E])
        ediff = m.sb("ediff", [R, TILES])
        esum = m.sb("esum", [R, TILES])
        total = m.sb("total", [128, TILES, E])
        incl = m.sb("incl", [128, TILES, E])
        onesg = m.sb("onesg", [128, TILES])
        steps = m.sb("steps", [128, E, NC_])
        over = m.sb("over", [128, E, NC_])
        ntile = m.sb("ntile", [128, E])
        tend = m.sb("tend", [128, E])
        base = m.sb("base", [128, E])
        slot = m.sb("slot", [R, TILES, E])
        picked = m.sb("picked", [R, TILES, E])
        slotf = m.sb("slotf", [R, 2, TILES])
        sloti = m.sb("sloti", [R, 2, TILES], U32)
        dest = m.sb("dest", [R, 2, TILES], I32)
        tid = m.sb("tid", [1, SLOT_TILES, E])
        past = m.sb("past", [1, SLOT_TILES, E])
        texp = m.sb("texp", [1, SLOT_TILES])
        NB = 4
        ybuf = [m.sb(f"ybuf{n}", [R, ROWW]) for n in range(2 * NB)]
        p_rank = m.ps("p_rank", [128, GE])
        p_total = m.ps("p_total", [128, GE])
        dve_step, pool_set, chosen, ranked, exp_done, slots_ready, dest_set = (m.sem(n) for n in (
            "dve_step", "pool_set", "chosen", "ranked", "exp_done", "slots_ready", "dest_set"))
        y_in = [m.sem(f"y_in{n}") for n in range(2 * NB)]
        sent = [m.sem(f"sent{n}") for n in range(2 * NB)]
        y_rows = y_dram.rearrange("(g r) c -> g r c", r=R)
        block = ctx.enter_context(nc.Block())

        def over_experts(v):
            return v.rearrange("p (g a) -> p g a", a=1).to_broadcast([v.shape[0], v.shape[1], E])

        @block.sync
        def _(sp):
            for g in range(TILES):
                for c in range(2):
                    n = 2 * (g % NB) + c
                    if g >= NB:
                        sp.wait_ge(sent[n], 16 * (g // NB))
                    sp.dma_start(ybuf[n][:, 0:C], y_rows[g]).then_inc(y_in[n], 16)
            load_weights(sp)

        @block.gpsimd
        def _(pool):
            pool.iota(eid[:, :, :], [[0, TILES], [1, E]], base=-E, channel_multiplier=0,
                      allow_small_or_imprecise_dtypes=True).then_inc(pool_set, 1)
            pool.memset(upper[:, :], 1.0).then_inc(pool_set, 1)
            pool.memset(ones[:, :], 1.0).then_inc(pool_set, 1)
            pool.memset(onesg[:, :], 1.0).then_inc(pool_set, 1)
            pool.iota(steps[:, :, :], [[0, E], [SLOT, NC_]], base=0, channel_multiplier=0,
                      allow_small_or_imprecise_dtypes=True).then_inc(pool_set, 1)
            pool.iota(tid[:, :, :], [[1, SLOT_TILES], [0, E]], base=0, channel_multiplier=0,
                      allow_small_or_imprecise_dtypes=True).then_inc(pool_set, 1)
            pool.iota(dest[:, :, :], [[N_TOK, 2], [R, TILES]], base=0, channel_multiplier=1).then_inc(pool_set, 1)
            pool.wait_ge(pool_set, 7)
            pool.affine_select(out=upper[:, :], in_=upper[:, :], compare_op=ALU.is_gt, fill=0.0, base=0,
                               pattern=[[1, 128]], channel_multiplier=-1).then_inc(pool_set, 1)
            pool.wait_ge(slots_ready, 1)
            for g in range(TILES):
                for c in range(2):
                    n = 2 * (g % NB) + c
                    pool.wait_ge(dest_set, 2 * g + c + 1)
                    pool.wait_ge(y_in[n], 16 * (g // NB + 1))
                    pool.indirect_dma_start(out=slots_dram, out_offset=bass.IndirectOffsetOnAxis(
                        ap=sloti[:, c, g:g + 1], axis=0), in_=ybuf[n][:, :], in_offset=None).then_inc(sent[n], 16)
            for n in range(2 * NB):
                pool.wait_ge(sent[n], 16 * (TILES // NB))

        @block.scalar
        def _(act):
            act.wait_ge(chosen, 2)
            act.activation(ediff[:, :], ediff[:, :], ACT.Exp).then_inc(exp_done, 1)

        @block.tensor
        def _(pe):
            pe.wait_ge(chosen, 1)
            pe.wait_ge(pool_set, 8)
            b2 = both[:, :, :].rearrange("p g e -> p (g e)")
            pe.matmul(p_rank[:, :], upper[:, :], b2, start=True, stop=True)
            pe.matmul(p_total[:, :], ones[:, :], b2, start=True, stop=True).then_inc(ranked, 1)

        @block.vector
        def _(dve):
            n_steps = [0]

            def step(ins):
                ins.then_inc(dve_step, 1)
                n_steps[0] += 1
                dve.wait_ge(dve_step, n_steps[0])

            dve.wait_ge(pool_set, 8)
            src = logits[:, :, :]
            for c in range(2):
                step(dve.tensor_reduce(top[:, c, :], src, axis=AX_X, op=ALU.max))
                step(dve.tensor_tensor(eq[:, :, :], src, over_experts(top[:, c, :]), ALU.is_equal))
                step(dve.tensor_tensor(eq[:, :, :], eq[:, :, :], eid[:, :, :], ALU.mult))
                step(dve.tensor_reduce(idx[:, c, :], eq[:, :, :], axis=AX_X, op=ALU.min))
                step(dve.tensor_tensor(hot[:, c, :, :], eid[:, :, :], over_experts(idx[:, c, :]), ALU.is_equal))
                if c == 0:
                    step(dve.scalar_tensor_tensor(out=lg2[:, :, :], in0=hot[:, 0, :, :], scalar=-BIG,
                                                  in1=src, op0=ALU.mult, op1=ALU.add))
                    src = lg2[:, :, :]
            dve.tensor_tensor(both[:, :, :], hot[:, 0, :, :], hot[:, 1, :, :], ALU.add).then_inc(chosen, 1)
            dve.tensor_tensor(ediff[:, :], top[:, 1, :], top[:, 0, :], ALU.subtract).then_inc(chosen, 1)
            dve.wait_ge(exp_done, 1)
            step(dve.tensor_scalar(esum[:, :], ediff[:, :], 1.0, None, ALU.add))
            step(dve.reciprocal(weights[:, 0, :], esum[:, :]))
            step(dve.tensor_tensor(weights[:, 1, :], ediff[:, :], weights[:, 0, :], ALU.mult))
            dve.wait_ge(ranked, 1)
            step(dve.tensor_copy(total[:, :, :], p_total[:, :].rearrange("p (g e) -> p g e", e=E)))
            for e in range(E):
                scan = dve.tensor_tensor_scan(incl[:, :, e], onesg[:, :], total[:, :, e], 0.0, ALU.mult, ALU.add)
            step(scan)
            step(dve.tensor_tensor(over[:, :, :], incl[:, TILES - 1, :].rearrange("p (e a) -> p e a", a=1)
                                   .to_broadcast([128, E, NC_]), steps[:, :, :], ALU.is_gt))
            step(dve.tensor_reduce(ntile[:, :], over[:, :, :], axis=AX_X, op=ALU.add))
            step(dve.tensor_tensor_scan(tend[:, :], onesg[:, 0:E], ntile[:, :], 0.0, ALU.mult, ALU.add))
            step(dve.tensor_tensor(base[:, :], tend[:, :], ntile[:, :], ALU.subtract))
            step(dve.tensor_scalar(base[:, :], base[:, :], float(SLOT), None, ALU.mult))
            step(dve.tensor_tensor(incl[:, :, :], incl[:, :, :], total[:, :, :], ALU.subtract))
            step(dve.tensor_tensor(slot[:, :, :], p_rank[0:R, :].rearrange("p (g e) -> p g e", e=E),
                                   incl[0:R, :, :], ALU.add))
            step(dve.tensor_tensor(slot[:, :, :], slot[:, :, :], base[0:R, :].rearrange("p (a e) -> p a e", a=1)
                                   .to_broadcast([R, TILES, E]), ALU.add))
            for c in range(2):
                step(dve.tensor_tensor(picked[:, :, :], hot[:, c, :, :], slot[:, :, :], ALU.mult))
                step(dve.tensor_reduce(slotf[:, c, :], picked[:, :, :], axis=AX_X, op=ALU.add))
            dve.tensor_copy(sloti[:, :, :], slotf[:, :, :]).then_inc(slots_ready, 1)
            step(dve.tensor_tensor(past[:, :, :], tid[:, :, :], tend[0:1, :].rearrange("p (a e) -> p a e", a=1)
                                   .to_broadcast([1, SLOT_TILES, E]), ALU.is_ge))
            step(dve.tensor_reduce(texp[:, :], past[:, :, :], axis=AX_X, op=ALU.add))
            step(dve.tensor_scalar(expert_of[:, :], texp[:, :], float(E - 1), None, ALU.min))
            for g in range(TILES):
                for c in range(2):
                    n = 2 * (g % NB) + c
                    if g >= NB:
                        dve.wait_ge(sent[n], 16 * (g // NB))
                    dve.tensor_copy(ybuf[n][:, C:ROWW].bitcast(I32), dest[:, c, g:g + 1]).then_inc(dest_set, 1)


def split_biases(nc, b1, b2, b1s, b2s, ones3):
    with ExitStack() as ctx:
        m = Memory(nc, ctx, "bsp")
        WID = FF + C
        raw = m.sb("raw", [E, WID])
        part = [m.sb(f"part{n}", [E, WID], BF16) for n in range(3)]
        loaded, cut, rest, ones_set, moved = (m.sem(n) for n in ("loaded", "cut", "rest", "ones_set", "moved"))
        with nc.Block() as block:

            @block.sync
            def _(sp):
                sp.dma_start(raw[:, 0:FF], b1).then_inc(loaded, 16)
                sp.dma_start(raw[:, FF:WID], b2).then_inc(loaded, 16)
                sp.wait_ge(cut, 3)
                for n in range(3):
                    sp.dma_start(b1s[n:n + 1, :], part[n][:, 0:FF]).then_inc(moved, 16)
                    sp.dma_start(b2s[n:n + 1, :], part[n][:, FF:WID]).then_inc(moved, 16)
                sp.wait_ge(moved, 96)

            @block.vector
            def _(dve):
                dve.memset(ones3[:, :], 1.0).then_inc(ones_set, 1)
                dve.wait_ge(loaded, 32)
                for n in range(3):
                    dve.tensor_copy(part[n][:, :], raw[:, :]).then_inc(cut, 1)
                    dve.wait_ge(cut, n + 1)
                    if n < 2:
                        dve.tensor_tensor(raw[:, :], raw[:, :], part[n][:, :], ALU.subtract).then_inc(rest, 1)
                        dve.wait_ge(rest, n + 1)


def slot_tiles(eng, body):
    first, last = 2, 1 + (SLOT_TILES - 3) % 2
    for n in range(first):
        body((None, n), n % 2, False)
    with eng.Fori(0, (SLOT_TILES - first - last) // 2) as i:
        for par in range(2):
            body((i, first + par), par, False)
    for n in range(SLOT_TILES - last, SLOT_TILES):
        body((None, n), n % 2, n == SLOT_TILES - 1)


def experts(nc, ident, w1, w2, b1s, b2s, ones3, expert_of, slots_dram, out_dram, weights_in, n_weights):
    FT = FF // 128
    HALF = FF // 2
    with ExitStack() as ctx:
        m = Memory(nc, ctx, "moe")
        xin = m.sb("xin", [SLOT, 2, ROWW])
        ids = m.sb("ids", [SLOT, 2], I32)
        xT = m.sb("xT", [128, 2, KC, SLOT])
        hid = m.sb("hid", [SLOT, 2, FF])
        hT = m.sb("hT", [128, 2, FT, SLOT])
        res = m.sb("res", [SLOT, 2, C])
        p_x = m.ps("p_x", [128, 512])
        p_h = [m.ps(f"p_h{n}", [128, 512]) for n in range(2)]
        p_t = [m.ps(f"p_t{n}", [128, 512]) for n in range(2)]
        p_y = [m.ps(f"p_y{n}", [128, 512]) for n in range(2)]
        xt_full, xt_ready, h_full, h_ready, ht_full, ht0_ready, ht1_ready, y_full, y_ready, ids_ready = (
            m.sem(n) for n in ("xt_full", "xt_ready", "h_full", "h_ready", "ht_full", "ht0_ready", "ht1_ready",
                               "y_full", "y_ready", "ids_ready"))
        x_in = [m.sem(f"x_in{n}") for n in range(2)]
        sent = [m.sem(f"sent{n}") for n in range(2)]
        x_rows = slots_dram.rearrange("(t p) c -> p t c", p=SLOT)
        block = ctx.enter_context(nc.Block())

        def at(b, width=1, per=1):
            v = count(b, per, 0)
            return slice(v, v + width) if isinstance(v, int) else bass.ds(v, width)

        @block.sync
        def _(sp):
            def load(t, par, is_last):
                wait_alone(sp, (xt_full, count(t, 1, -1)),
                               (ids_ready, count(t, 1, -1)))
                sp.dma_start(xin[:, par, :], x_rows[:, at(t), :]).then_inc(x_in[par], 16)

            slot_tiles(sp, load)

        @block.tensor
        def _(pe):
            def expert(t):
                return pe.value_load(expert_of[0:1, at(t)], min_val=0, max_val=E - 1)

            def transpose_x(t, par):
                wait(pe, x_in[par], half_count(t, 16, 16))
                wait(pe, xt_ready, count(t, 1, 0))
                for k in range(KC):
                    mm = pe.transpose(p_x[:, k * 128:(k + 1) * 128], xin[:, par, k * 128:(k + 1) * 128], ident[:, :])
                mm.then_inc(xt_full, 1)

            def layer1(t, par):
                e = expert(t)
                wait(pe, xt_ready, count(t, 1, 1))
                for n in range(2):
                    wait(pe, h_ready, count(t, 2, n - 1))
                    for k in range(KC):
                        pe.matmul(p_h[n][:, :], xT[:, par, k, :], w1[:, k, bass.ds(e * FF + n * HALF, HALF)],
                                  start=(k == 0), stop=False)
                    pe.matmul(p_h[n][:, :], ones3[:, :], b1s[:, bass.ds(e * FF + n * HALF, HALF)],
                              start=False, stop=True).then_inc(h_full, 1)

            def transpose_h(t, par):
                for n, evac in enumerate((ht0_ready, ht1_ready)):
                    wait(pe, h_ready, count(t, 2, n + 1))
                    wait(pe, evac, count(t, 1, 0))
                    for f in range(FT // 2):
                        at_ = (n * FT // 2 + f) * 128
                        mm = pe.transpose(p_t[n][:, f * 128:(f + 1) * 128], hid[:, par, at_:at_ + 128], ident[:, :])
                    mm.then_inc(ht_full, 1)

            def layer2(t, par):
                e = expert(t)
                wait(pe, y_ready, count(t, 1, -1))
                for f in range(FT):
                    if f == 0:
                        wait(pe, ht0_ready, count(t, 1, 1))
                    if f == FT // 2:
                        wait(pe, ht1_ready, count(t, 1, 1))
                    pe.matmul(p_y[par][:, 0:C], hT[:, par, f, :], w2[:, bass.ds((e * FT + f) * C, C)],
                              start=(f == 0), stop=False)
                pe.matmul(p_y[par][:, 0:C], ones3[:, :], b2s[:, bass.ds(e * C, C)],
                          start=False, stop=True).then_inc(y_full, 1)

            def body(t, par, is_last):
                layer1(t, par)
                if not is_last:
                    transpose_x((t[0], t[1] + 1), 1 - par)
                if t[0] is not None or t[1] > 0:
                    layer2(before(t), 1 - par)
                transpose_h(t, par)

            pe.wait_ge(weights_in, n_weights)
            transpose_x((None, 0), 0)
            slot_tiles(pe, body)
            layer2((None, SLOT_TILES - 1), (SLOT_TILES - 1) % 2)

        @block.scalar
        def _(act):
            def body(t, par, is_last):
                for n in range(2):
                    wait(act, h_full, count(t, 2, n + 1))
                    wait(act, ht_full, count(t, 2, -2))
                    act.activation(hid[:, par, n * HALF:(n + 1) * HALF], p_h[n][:, :], ACT.Relu).then_inc(h_ready, 1)
                wait(act, ht_full, count(t, 2, 2))
                wait(act, y_full, count(t, 1, -1))
                act.activation(hT[:, par, FT // 2:FT, :].rearrange("p f s -> p (f s)"), p_t[1][:, :],
                               ACT.Copy).then_inc(ht1_ready, 1)

            slot_tiles(act, body)

        @block.vector
        def _(dve):
            def keep_ids(t, par):
                wait(dve, x_in[par], half_count(t, 16, 16))
                wait(dve, sent[par], half_count(t, 16, 0))
                dve.tensor_copy(ids[:, par:par + 1], xin[:, par, C:ROWW].bitcast(I32)).then_inc(ids_ready, 1)

            def x_back(t, par):
                wait(dve, xt_full, count(t, 1, 1))
                wait(dve, h_full, count(t, 2, -2))
                dve.tensor_copy(xT[:, par, :, :].rearrange("p k s -> p (k s)"), p_x[:, 0:C]).then_inc(xt_ready, 1)

            def result(t, par):
                wait(dve, y_full, count(t, 1, 1))
                wait(dve, sent[par], half_count(t, 16, 0))
                dve.tensor_copy(res[:, par, :], p_y[par][:, 0:C]).then_inc(y_ready, 1)

            def body(t, par, is_last):
                if t[0] is not None or t[1] > 0:
                    result(before(t), 1 - par)
                if not is_last:
                    x_back((t[0], t[1] + 1), 1 - par)
                wait(dve, ht_full, count(t, 2, 1))
                wait(dve, y_full, count(t, 1, -1))
                dve.tensor_copy(hT[:, par, 0:FT // 2, :].rearrange("p f s -> p (f s)"), p_t[0][:, :]).then_inc(ht0_ready, 1)
                if not is_last:
                    keep_ids((t[0], t[1] + 1), 1 - par)

            keep_ids((None, 0), 0)
            x_back((None, 0), 0)
            slot_tiles(dve, body)
            result((None, SLOT_TILES - 1), (SLOT_TILES - 1) % 2)

        @block.gpsimd
        def _(pool):
            def send(t, par, is_last):
                wait_alone(pool, (y_ready, count(t, 1, 1)),
                                 (ids_ready, count(t, 1, 1)))
                pool.indirect_dma_start(out=out_dram, out_offset=bass.IndirectOffsetOnAxis(
                    ap=ids[:, par:par + 1].bitcast(U32), axis=0), in_=res[:, par, :], in_offset=None
                    ).then_inc(sent[par], 16)

            slot_tiles(pool, send)
            for n in range(2):
                pool.wait_ge(sent[n], 16 * ((SLOT_TILES + 1 - n) // 2))


def combine(nc, neghalf, eps, weights, moe_dram, h_dram, out, g2, b2):
    with ExitStack() as ctx:
        m = Memory(nc, ctx, "comb")
        gain, shift = m.sb("gain", [R, C]), m.sb("shift", [R, C])
        eo = m.sb("eo", [R, 2, 2, NT, C])
        hy = m.sb("hy", [R, 2, NT, C])
        acc = m.sb("acc", [R, 2, NT, C])
        st, mv = m.sb("st", [R, 2, NT, 6]), m.sb("mv", [R, 2, NT, 2])
        ve, rs = m.sb("ve", [R, 2, NT]), m.sb("rs", [R, 2, NT])
        consts_in, weighted, mixed, stats, aggr, eps_added, rstd, normed, gained, shifted, summed = (
            m.sem(n) for n in ("consts_in", "weighted", "mixed", "stats", "aggr", "eps_added", "rstd", "normed",
                               "gained", "shifted", "summed"))
        x_in = [m.sem(f"x_in{n}") for n in range(2)]
        out_done = [m.sem(f"out_done{n}") for n in range(2)]
        e_rows = moe_dram[0:2 * N_TOK, :].rearrange("(c g r) d -> r c g d", c=2, r=R)
        h_rows = h_dram.rearrange("(g r) c -> r g c", r=R)
        o_rows = out.rearrange("b t c -> (b t) c").rearrange("(g r) c -> r g c", r=R)
        block = ctx.enter_context(nc.Block())

        @block.sync
        def _(sp):
            for vec, sb in ((g2, gain), (b2, shift)):
                sp.dma_start(sb[:, :], vec.rearrange("(a c) -> a c", a=1).to_broadcast([R, C])).then_inc(consts_in, 16)

            def load(b, par):
                wait_alone(sp, (summed, count(b, 1, -1)))
                for c in range(2):
                    sp.dma_start(eo[:, par, c, :, :], e_rows[:, c, rows(b, 0, NT), :]).then_inc(x_in[par], 16)
                sp.dma_start(hy[:, par, :, :], h_rows[:, rows(b, 0, NT), :]).then_inc(x_in[par], 16)

            batches(sp, load)

        @block.scalar
        def _(act):
            def store(b, par):
                wait(act, summed, count(b, 1, 1))
                act.dma_start(o_rows[:, rows(b, 0, NT), :], acc[:, par, :, :]).then_inc(out_done[par], 16)

            batches(act, store)
            for n in range(2):
                act.wait_ge(out_done[n], 16 * B // 2)

        @block.vector
        def _(dve):
            def mix(b, par):
                wait(dve, x_in[par], half_count(b, 48, 48))
                wait(dve, out_done[par], half_count(b, 16, 0))
                for c, done in ((0, weighted), (1, mixed)):
                    for j in range(NT):
                        w = weights[:, c, row(b, j):row(b, j) + 1] if b[0] is None else weights[:, c, bass.ds(row(b, j), 1)]
                        if c == 0:
                            dve.tensor_scalar(acc[:, par, j, :], eo[:, par, 0, j, :], w, None, ALU.mult).then_inc(done, 1)
                        else:
                            wait(dve, weighted, count(b, NT, j + 1))
                            dve.scalar_tensor_tensor(out=acc[:, par, j, :], in0=eo[:, par, 1, j, :], scalar=w,
                                                     in1=acc[:, par, j, :], op0=ALU.mult, op1=ALU.add).then_inc(done, 1)
                for j in range(NT):
                    wait_alone(dve, (mixed, count(b, NT, j + 1)))
                    dve.bn_stats(st[:, par, j, :], acc[:, par, j, :]).then_inc(stats, 1)
                for j in range(NT):
                    wait_alone(dve, (stats, count(b, NT, j + 1)))
                    dve.bn_aggr(mv[:, par, j, :], st[:, par, j, :]).then_inc(aggr, 1)
                wait(dve, rstd, count(b, 1, 1))
                for j in range(NT):
                    dve.tensor_scalar(acc[:, par, j, :], acc[:, par, j, :], mv[:, par, j, 0:1], rs[:, par, j:j + 1],
                                      ALU.subtract, ALU.mult).then_inc(normed, 1)
                wait(dve, shifted, count(b, 1, 1))
                dve.tensor_tensor(acc[:, par, :, :], acc[:, par, :, :], hy[:, par, :, :], ALU.add).then_inc(summed, 1)

            batches(dve, mix)

        @block.gpsimd
        def _(pool):
            def over_tiles(v):
                return v[:, :].rearrange("p (a c) -> p a c", a=1).to_broadcast([R, NT, C])

            def affine(b, par):
                wait_alone(pool, (aggr, count(b, NT, NT)))
                pool.tensor_tensor(ve[:, par, :], mv[:, par, :, 1], eps[0:R, :], ALU.add).then_inc(eps_added, 1)
                wait_alone(pool, (eps_added, count(b, 1, 1)))
                pool.tensor_tensor(rs[:, par, :], ve[:, par, :], neghalf[0:R, :], ALU.pow).then_inc(rstd, 1)
                ab = acc[:, par, :, :]
                wait_alone(pool, (normed, count(b, NT, NT)))
                pool.tensor_tensor(ab, ab, over_tiles(gain), ALU.mult).then_inc(gained, 1)
                wait_alone(pool, (gained, count(b, 1, 1)))
                pool.tensor_tensor(ab, ab, over_tiles(shift), ALU.add).then_inc(shifted, 1)

            pool.wait_ge(consts_in, 32)
            batches(pool, affine)


def mixture(nc, ctx, ident, neghalf, eps, logits, y_dram, h_dram, slots_dram, moe_dram, out, w1, b1, w2, b2, g2, be2):
    m = Memory(nc, ctx, "mix")
    FT = FF // 128
    weights = m.sb("weights", [R, 2, TILES])
    expert_of = m.sb("expert_of", [1, SLOT_TILES], I32)
    with ExitStack() as inner:
        m = Memory(nc, inner, "mixw")
        w1s = m.sb("w1s", [128, KC, E * FF])
        w2s = m.sb("w2s", [128, E * FT * C])
        b1s = m.sb("b1s", [3, E * FF], BF16)
        b2s = m.sb("b2s", [3, E * C], BF16)
        ones3 = m.sb("ones3", [3, SLOT], BF16)
        weights_in = m.sem("weights_in")

        def load_weights(sp):
            for e in range(E):
                sp.dma_start(w1s[:, :, e * FF:(e + 1) * FF], w1[e].rearrange("(k p) f -> p k f", p=128)
                             ).then_inc(weights_in, 16)
                sp.dma_start(w2s[:, e * FT * C:(e + 1) * FT * C].rearrange("p (f c) -> p f c", c=C),
                             w2[e].rearrange("(f p) c -> p f c", p=128)).then_inc(weights_in, 16)

        split_biases(nc, b1, b2, b1s, b2s, ones3)
        route(nc, logits, weights, expert_of, y_dram, slots_dram, load_weights)
        experts(nc, ident, w1s, w2s, b1s, b2s, ones3, expert_of, slots_dram, moe_dram, weights_in, 32 * E)
    combine(nc, neghalf, eps, weights, moe_dram, h_dram, out, g2, be2)


def build(nc, x, conv_w, conv_b, fuse_w, fuse_b, fin_w, fin_b, a_wqkv, a_bqkv, a_wproj, a_bproj, a_w1, a_b1, a_w2, a_b2,
          a_c, a_l, f_wq, f_wk, f_wv, f_gate, f_w1, f_b1, f_w2, f_b2, f_g1, f_be1, f_g2, f_be2, out):
    def dram(name, shape):
        return nc.dram_tensor(name, shape, F32, kind="Internal").ap()

    nd_dram = dram("nd_scratch", (128, CAUSAL))
    bias_dram = dram("bias_scratch", (H, 128, CAUSAL))
    y_dram = dram("y_scratch", (N_TOK, C))
    h_dram = dram("h_scratch", (N_TOK, C))
    slots_dram = dram("slots_scratch", (SLOT_TILES * SLOT, ROWW))
    moe_dram = dram("moe_scratch", (N_RES, C))
    with ExitStack() as ctx:
        m = Memory(nc, ctx, "all")
        logits = m.sb("logits", [R, TILES, E])
        ident, neghalf, eps = constants(nc, m)
        with ExitStack() as held:
            hid = Memory(nc, held, "held").sb("hid", [R, TILES, C])
            clear_slots(nc, slots_dram)
            tokenize(nc, ident, neghalf, eps, hid, x, conv_w, conv_b, fuse_w, fuse_b, fin_w, fin_b)
            with ExitStack() as first:
                bias = Memory(nc, first, "held").sb("bias", [R, H, CAUSAL])
                fire_bias(nc, bias, nd_dram, bias_dram, a_w1, a_b1, a_w2, a_b2, a_c, a_l)
                attend(nc, ident, neghalf, eps, hid, bias, a_wqkv, a_bqkv, a_wproj, a_bproj)
            attend_in_ffn(nc, ident, neghalf, eps, hid, logits, y_dram, h_dram, f_wq, f_wk, f_wv, f_gate, f_g1, f_be1)
        mixture(nc, ctx, ident, neghalf, eps, logits, y_dram, h_dram, slots_dram, moe_dram, out,
                f_w1, f_b1, f_w2, f_b2, f_g2, f_be2)


_INS = ["x", "L0_tok_conv_w", "L0_tok_conv_b", "L0_tok_fusion_ln_w", "L0_tok_fusion_ln_b", "L0_tok_final_ln_w",
        "L0_tok_final_ln_b", "L0_attn_Wqkv", "L0_attn_bqkv", "L0_attn_Wproj", "L0_attn_bproj", "L0_attn_w1",
        "L0_attn_b1", "L0_attn_w2", "L0_attn_b2", "L0_attn_c_param", "L0_attn_L_multiplier", "L0_ffn_Wq", "L0_ffn_Wk",
        "L0_ffn_Wv", "L0_ffn_gate_W", "L0_ffn_W1", "L0_ffn_b1", "L0_ffn_W2", "L0_ffn_b2", "L0_ffn_ln1_g",
        "L0_ffn_ln1_b", "L0_ffn_ln2_g", "L0_ffn_ln2_b"]


def kernel(**inputs):
    import numpy as _np
    import concourse.bacc as _bacc
    from concourse import mybir as _mybir
    from concourse.bass_utils import run_bass_kernel_spmd as _run

    nc = _bacc.Bacc("TRN2", target_bir_lowering=False, num_devices=1)
    arrays, args = {}, []
    for name in _INS:
        a = _np.ascontiguousarray(inputs[name])
        if name in ("L0_attn_c_param", "L0_attn_L_multiplier"):
            a = a.reshape(1, 1)
        arrays[f"in_{name}"] = a
        args.append(nc.dram_tensor(f"in_{name}", a.shape, _mybir.dt.from_np(a.dtype), kind="ExternalInput").ap())
    args.append(nc.dram_tensor("out_0", (B, T, C), F32, kind="ExternalOutput").ap())
    build(nc, *args)
    r = _run(nc, [arrays], core_ids=[0])
    return r.results[0]["out_0"]
```

```python
import concourse.bass as bass
from concourse import mybir
from concourse.alu_op_type import AluOpType as ALU
from contextlib import ExitStack

F32 = mybir.dt.float32
BF16 = mybir.dt.bfloat16
I32 = mybir.dt.int32
U32 = mybir.dt.uint32
ACT = mybir.ActivationFunctionType
AX_X = mybir.AxisListType.X

B, T_IN, C = 16, 750, 256
T = T_IN // 2
R = 125
NT = T // R
TILES = B * NT
KC = C // 128
H = 16
HD = C // H
W = 32
E = 8
FF = 4 * C
SEG = [R * i * (i + 1) // 2 for i in range(NT + 1)]
CAUSAL = SEG[NT]
BIG = 3.0e38
NEG = -1.0e30
INIT_L, BIAS_EPS, LN_EPS = 512.0, 1e-6, 1e-5
Q_PARTS = [0, 0, 0, 1, 1, 2]
K_PARTS = [0, 1, 2, 0, 1, 0]
STACK = len(Q_PARTS) * HD


def count(b, per, c):
    i, off, ways = b
    const = off * per + c
    return const if i is None else i * (ways * per) + const


def wait(eng, sem, value):
    if not isinstance(value, int) or value > 0:
        eng.wait_ge(sem, value)


def wait_alone(eng, *pairs):
    pairs = [(sem, value) for sem, value in pairs if not isinstance(value, int) or value > 0]
    if any(not isinstance(value, int) for _, value in pairs):
        pairs = [(sem, value if isinstance(value, int) else eng.to_reg(value)) for sem, value in pairs]
        eng.wait_ge(pairs[0][0], 1)
    for sem, value in pairs:
        eng.wait_ge(sem, value)


def skewed(eng, steps, prelude=None, ways=2):
    def body(b, lane):
        for k, step in steps:
            if b[0] is not None or 0 <= b[1] - k < B:
                step(before(b, k), (lane - k) % ways)

    body((None, 0, ways), 0)
    if prelude:
        prelude()
    for n in range(1, 4):
        body((None, n, ways), n % ways)
    with eng.Fori(0, (B - 4) // ways) as i:
        for lane in range(ways):
            body((i, 4 + lane, ways), lane)
    for n in range(B, B + max(k for k, _ in steps)):
        body((None, n, ways), n % ways)


def lane_count(b, per, c):
    i, off, ways = b
    const = off // ways * per + c
    return const if i is None else i * per + const


def before(b, n=1):
    return (b[0], b[1] - n, b[2])


def after(b):
    return before(b, -1)


def rows(b, j=0, n=1):
    at = count(b, NT, j)
    return slice(at, at + n) if isinstance(at, int) else bass.ds(at, n)


def row(b, j):
    at = count(b, NT, j)
    return at


class Memory:

    def __init__(self, nc, ctx, tag):
        self.nc, self.ctx, self.tag, self.sems = nc, ctx, tag, []
        ctx.callback(self.close)

    def close(self):
        if self.sems:
            self.nc.clear_and_free_semaphores(self.sems)
            self.nc.all_engine_barrier()

    def sb(self, name, shape, dt=F32):
        return self.ctx.enter_context(self.nc.sbuf_tensor(f"{self.tag}_{name}", shape, dt))

    def ps(self, name, shape, dt=F32):
        return self.ctx.enter_context(self.nc.psum_tensor(f"{self.tag}_{name}", shape, dt))

    def sem(self, name):
        self.sems.append(self.nc.alloc_semaphore(f"{self.tag}_{name}"))
        return self.sems[-1]


def constants(nc, mem):
    ident = mem.sb("ident", [128, 128])
    neghalf = mem.sb("neghalf", [128, NT])
    eps = mem.sb("eps", [128, NT])
    set_done, sel_done = mem.sem("set_done"), mem.sem("sel_done")
    with nc.Block() as block:

        @block.gpsimd
        def _(pool):
            pool.memset(neghalf[:, :], -0.5)
            pool.memset(eps[:, :], LN_EPS)
            pool.memset(ident[:, :], 0.0).then_inc(set_done, 1)
            pool.wait_ge(set_done, 1)
            pool.affine_select(out=ident[:, :], in_=ident[:, :], compare_op=ALU.not_equal, fill=1.0,
                               base=0, pattern=[[-1, 128]], channel_multiplier=1).then_inc(sel_done, 1)
    return ident, neghalf, eps


def tokenize(nc, ident, neghalf, eps, hid, nd_dram, bias_dram, x, conv_w, conv_b, g_fuse, b_fuse, g_fin, b_fin,
             w1, b1, w2, b2, c_param, l_mult):
    G = 4
    PR = 128 // G
    STEP = PR // B
    CH = STEP * CAUSAL
    NMM = CH // 500
    with ExitStack() as ctx:
        m = Memory(nc, ctx, "tok")
        w_in = m.sb("w_in", [128, KC, C * 2])
        w_sb = m.sb("w", [128, 2 * KC, C])
        cb, gf, bf, gl, bl = (m.sb(n, [R, C]) for n in ("cb", "gf", "bf", "gl", "bl"))
        xin = m.sb("xin", [R, 2, NT, 2 * C])
        xT = m.sb("xT", [128, 2, 2 * KC, R])
        y = m.sb("y", [R, 2, NT, C])
        sk = m.sb("sk", [R, 2, NT, C])
        st = m.sb("st", [R, 2, NT, 6])
        mv = m.sb("mv", [R, 2, NT, 2])
        ve = m.sb("ve", [R, 2, NT])
        rs = m.sb("rs", [R, 2, NT])
        st2 = m.sb("st2", [R, 2, NT, 6])
        mv2 = m.sb("mv2", [R, 2, NT, 2])
        ve2 = m.sb("ve2", [R, 2, NT])
        rs2 = m.sb("rs2", [R, 2, NT])
        p_wt = m.ps("p_wt", [128, 512])
        p_xt = [m.ps(f"p_xt{n}", [128, 2 * KC, 128]) for n in range(2)]
        p_y = [m.ps(f"p_y{n}", [128, 512]) for n in range(2)]
        (consts_in, wt_full, wt_evac, xt_full, xt_ready, y_full, y_added, stats1, aggr1, eps1, rstd1,
         scaled1, gained1, fused, skip_sum, summed, gelu_done, stats2, aggr2, eps2, rstd2, scaled2, gained2,
         final) = (m.sem(n) for n in (
             "consts_in", "wt_full", "wt_evac", "xt_full", "xt_ready", "y_full", "y_added", "stats1", "aggr1",
             "eps1", "rstd1", "scaled1", "gained1", "fused", "skip_sum", "summed", "gelu_done", "stats2", "aggr2",
             "eps2", "rstd2", "scaled2", "gained2", "final"))
        x_in = [m.sem(f"x_in{n}") for n in range(2)]
        x_rows = x.rearrange("b t c -> (b t c)").rearrange("(g r c) -> r g c", r=R, c=2 * C)
        cpar = m.sb("cpar", [128, 1])
        lpar = m.sb("lpar", [128, 1])
        thr = m.sb("thr", [128, 1])
        rel = m.sb("rel", [128, CAUSAL])
        pos = m.sb("pos", [128, NT])
        nd = m.sb("nd", [128, CAUSAL])
        w1c = m.sb("w1c", [128, 1])
        b1c = m.sb("b1c", [128, 1])
        b2c = m.sb("b2c", [G * H, 1])
        w2g = m.sb("w2g", [128, G * H])
        nd_w = m.sb("nd_w", [128, 2, CH])
        hidden = m.sb("hidden", [128, 2, CH])
        outb = m.sb("outb", [G * H, 2, CH])
        pb = [m.ps(f"pb{n}", [G * H, 512]) for n in range(NMM)]
        (params_in, zeroed, w2_in, iota_done, rel_abs, rel_log, pos_max, pos_abs, pos_log, pos_eps, pos_inv, thr_done,
         nd_done, nd_out, hidden_done, mm_done, out_done) = (m.sem(n) for n in (
             "params_in", "zeroed", "w2_in", "iota_done", "rel_abs", "rel_log", "pos_max", "pos_abs", "pos_log",
             "pos_eps", "pos_inv", "thr_done", "nd_done", "nd_out", "hidden_done", "mm_done", "out_done"))
        nd_in = [m.sem(f"nd_in{n}") for n in range(2)]
        stored = [m.sem(f"stored{n}") for n in range(2)]

        block = ctx.enter_context(nc.Block())

        @block.sync
        def _(sp):
            def load(b, par):
                wait_alone(sp, (xt_full, count(b, NT, -NT)),
                               (skip_sum, count(b, 1, -1)))
                sp.dma_start(xin[:, par, :, :], x_rows[:, rows(b, 0, NT), :]).then_inc(x_in[par], 16)

            def chunk_load(c, par):
                wait_alone(sp, (hidden_done, count(c, 1, -1)))
                for g in range(G):
                    r0 = count(c, STEP, g * PR)
                    r_ = slice(r0, r0 + STEP) if isinstance(r0, int) else bass.ds(r0, STEP)
                    src = nd_dram[r_, :].rearrange("(a r) c -> a (r c)", a=1)
                    sp.dma_start(nd_w[g * W:(g + 1) * W, par, :], src.to_broadcast([W, CH])).then_inc(nd_in[par], 16)

            def chunk_store(c, par):
                wait_alone(sp, (out_done, count(c, NMM, NMM)))
                for g in range(G):
                    r0 = count(c, STEP, g * PR)
                    r_ = slice(r0, r0 + STEP) if isinstance(r0, int) else bass.ds(r0, STEP)
                    sp.dma_start(bias_dram[:, r_, :].rearrange("h r c -> h (r c)"), outb[g * H:(g + 1) * H, par, :]
                                 ).then_inc(stored[par], 16)

            def prelude():
                for g in range(G):
                    sp.dma_start(w1c[g * W:(g + 1) * W, :], w1.rearrange("a w -> w a")).then_inc(params_in, 16)
                    sp.dma_start(b1c[g * W:(g + 1) * W, :], b1.rearrange("(w a) -> w a", a=1)).then_inc(params_in, 16)
                    sp.dma_start(b2c[g * H:(g + 1) * H, :], b2.rearrange("(h a) -> h a", a=1)).then_inc(params_in, 16)
                sp.wait_ge(zeroed, 1)
                for g in range(G):
                    sp.dma_start(w2g[g * W:(g + 1) * W, g * H:(g + 1) * H], w2).then_inc(w2_in, 16)
                load((None, 1, 2), 1)
                sp.wait_ge(nd_done, NT)
                sp.dma_start(nd_dram, nd[:, :]).then_inc(nd_out, 16)
                sp.wait_ge(nd_out, 16)

            def load_later(b, par):
                if b[0] is not None or b[1] != 1:
                    load(b, par)

            sp.dma_start(w_in[:, :, :], conv_w.rearrange("(o p) c k -> p o (c k)", p=128)).then_inc(consts_in, 16)
            sp.dma_start(cpar[:, :], c_param.to_broadcast([128, 1])).then_inc(params_in, 16)
            sp.dma_start(lpar[:, :], l_mult.to_broadcast([128, 1])).then_inc(params_in, 16)
            for vec, sb in ((conv_b, cb), (g_fuse, gf), (b_fuse, bf), (g_fin, gl), (b_fin, bl)):
                sp.dma_start(sb[:, :], vec.rearrange("(a c) -> a c", a=1).to_broadcast([R, C])).then_inc(consts_in, 16)
            skewed(sp, [(0, load_later), (1, chunk_load), (3, chunk_store)], prelude)
            for n in range(2):
                sp.wait_ge(stored[n], 16 * G * B // 2)

        @block.tensor
        def _(pe):
            pe.wait_ge(consts_in, 96)
            w_ck = w_in[:, :, :].rearrange("p o (c k) -> p o c k", k=2)
            for k in range(2):
                for c in range(KC):
                    n = k * KC + c
                    if n:
                        pe.wait_ge(wt_evac, n)
                    for o in range(KC):
                        mm = pe.transpose(p_wt[:, o * 128:(o + 1) * 128],
                                          w_ck[:, o, c * 128:(c + 1) * 128, k], ident[:, :])
                    mm.then_inc(wt_full, 1)
            pe.wait_ge(wt_evac, 2 * KC)

            def convolve(b, par):
                wait(pe, x_in[par], lane_count(b, 16, 16))

                def transpose(j):
                    wait(pe, xt_ready, count(b, NT, j - 1))
                    for k in range(2 * KC):
                        mm = pe.transpose(p_xt[(par * NT + j) % 2][:, k, 0:R], xin[:, par, j, k * 128:(k + 1) * 128],
                                          ident[0:R, 0:R])
                    mm.then_inc(xt_full, 1)

                transpose(0)
                for j in range(NT):
                    q = (par * NT + j) % 2
                    if j + 1 < NT:
                        transpose(j + 1)
                    wait(pe, xt_ready, count(b, NT, j + 1))
                    wait(pe, y_added, count(b, NT, j - 1))
                    for k in range(2 * KC):
                        mm = pe.matmul(p_y[q][0:R, 0:C], xT[:, q, k, :], w_sb[:, k, :],
                                       start=(k == 0), stop=(k == 2 * KC - 1))
                    mm.then_inc(y_full, 1)

            def chunk_products(c, par):
                wait(pe, hidden_done, count(c, 1, 1))
                for k in range(NMM):
                    wait(pe, out_done, count(c, NMM, k + 1 - NMM))
                    pe.matmul(pb[k][:, 0:500], w2g[:, :], hidden[:, par, k * 500:(k + 1) * 500],
                              start=True, stop=True).then_inc(mm_done, 1)

            def prelude():
                pe.wait_ge(w2_in, 16 * G)

            skewed(pe, [(0, convolve), (1, chunk_products)], prelude)

        @block.scalar
        def _(act):
            for n in range(2 * KC):
                act.wait_ge(wt_full, n + 1)
                act.activation(w_sb[:, n, :], p_wt[:, 0:C], ACT.Copy).then_inc(wt_evac, 1)

            def frames_back(b, par):
                for j in range(NT):
                    q = (par * NT + j) % 2
                    wait(act, xt_full, count(b, NT, j + 1))
                    wait(act, y_full, count(b, NT, j - 1))
                    act.activation(xT[:, q, :, :], p_xt[q][:, :, 0:R], ACT.Copy).then_inc(xt_ready, 1)

            def gelu(b, par):
                wait(act, summed, count(b, 1, 1))
                act.activation(sk[:, par, :, :], sk[:, par, :, :], ACT.Gelu).then_inc(gelu_done, 1)

            def chunk_hidden(c, par):
                wait(act, nd_in[par], lane_count(c, 16 * G, 16 * G))
                wait(act, mm_done, count(c, NMM, -NMM))
                act.activation(hidden[:, par, :], nd_w[:, par, :], ACT.Relu, bias=b1c[:, 0:1],
                               scale=w1c[:, 0:1]).then_inc(hidden_done, 1)

            def chunk_out(c, par):
                wait(act, stored[par], lane_count(c, 16 * G, 0))
                for k in range(NMM):
                    wait(act, mm_done, count(c, NMM, k + 1))
                    act.activation(outb[:, par, k * 500:(k + 1) * 500], pb[k][:, 0:500], ACT.Identity,
                                   bias=b2c[:, 0:1]).then_inc(out_done, 1)

            def prelude():
                act.wait_ge(params_in, 16 * (2 + 3 * G))
                act.wait_ge(iota_done, 1)
                act.activation(thr[:, :], lpar[:, :], ACT.Abs, scale=INIT_L).then_inc(thr_done, 1)
                act.activation(rel[:, :], rel[:, :], ACT.Abs, scale=cpar[:, 0:1]).then_inc(rel_abs, 1)
                act.wait_ge(rel_abs, 1)
                act.activation(rel[:, :], rel[:, :], ACT.Ln, bias=1.0).then_inc(rel_log, 1)
                act.wait_ge(pos_max, 1)
                act.activation(pos[:, :], pos[:, :], ACT.Abs, scale=cpar[:, 0:1]).then_inc(pos_abs, 1)
                act.wait_ge(pos_abs, 1)
                act.activation(pos[:, :], pos[:, :], ACT.Ln, bias=1.0).then_inc(pos_log, 1)

            skewed(act, [(0, frames_back), (2, gelu), (2, chunk_out), (1, chunk_hidden)], prelude)

        @block.vector
        def _(dve):
            def norm1_stats(b, par):
                for j in range(NT):
                    q = (par * NT + j) % 2
                    wait(dve, y_full, count(b, NT, j + 1))
                    wait(dve, summed, count(b, 1, -1))
                    dve.tensor_tensor(y[:, par, j, :], p_y[q][0:R, 0:C], cb[:, :], ALU.add).then_inc(y_added, 1)
                for j in range(NT):
                    wait(dve, y_added, count(b, NT, j + 1))
                    dve.bn_stats(st[:, par, j, :], y[:, par, j, :]).then_inc(stats1, 1)
                for j in range(NT):
                    wait_alone(dve, (stats1, count(b, NT, j + 1)))
                    dve.bn_aggr(mv[:, par, j, :], st[:, par, j, :]).then_inc(aggr1, 1)

            def norm1_scale(b, par):
                wait(dve, rstd1, count(b, 1, 1))
                for j in range(NT):
                    dve.tensor_scalar(y[:, par, j, :], y[:, par, j, :], mv[:, par, j, 0:1], rs[:, par, j:j + 1],
                                      ALU.subtract, ALU.mult).then_inc(scaled1, 1)

            def frames_sum(b, par):
                wait(dve, x_in[par], lane_count(b, 16, 16))
                wait(dve, scaled2, count(b, NT, -NT))
                dve.tensor_tensor(sk[:, par, :, :], xin[:, par, :, 0:C], xin[:, par, :, C:2 * C],
                                  ALU.add).then_inc(skip_sum, 1)

            def add_skip(b, par):
                wait(dve, fused, count(b, 1, 1))
                wait(dve, skip_sum, count(b, 1, 1))
                dve.scalar_tensor_tensor(out=sk[:, par, :, :], in0=sk[:, par, :, :], scalar=0.5,
                                         in1=y[:, par, :, :], op0=ALU.mult, op1=ALU.add).then_inc(summed, 1)

            def norm2_stats(b, par):
                wait(dve, gelu_done, count(b, 1, 1))
                for j in range(NT):
                    dve.bn_stats(st2[:, par, j, :], sk[:, par, j, :]).then_inc(stats2, 1)
                for j in range(NT):
                    wait_alone(dve, (stats2, count(b, NT, j + 1)))
                    dve.bn_aggr(mv2[:, par, j, :], st2[:, par, j, :]).then_inc(aggr2, 1)

            def norm2_scale(b, par):
                wait(dve, rstd2, count(b, 1, 1))
                for j in range(NT):
                    dve.tensor_scalar(hid[:, row(b, j), :], sk[:, par, j, :], mv2[:, par, j, 0:1],
                                      rs2[:, par, j:j + 1], ALU.subtract, ALU.mult).then_inc(scaled2, 1)

            def prelude():
                dve.wait_ge(thr_done, 1)
                dve.tensor_scalar(pos[:, :], pos[:, :], thr[:, 0:1], None, ALU.max).then_inc(pos_max, 1)
                dve.wait_ge(pos_log, 1)
                dve.tensor_scalar(pos[:, :], pos[:, :], BIAS_EPS, None, ALU.add).then_inc(pos_eps, 1)
                dve.wait_ge(pos_eps, 1)
                dve.reciprocal(pos[:, :], pos[:, :]).then_inc(pos_inv, 1)
                dve.wait_ge(pos_inv, 1)
                dve.wait_ge(rel_log, 1)
                for i in range(NT):
                    dve.tensor_scalar(nd[:, SEG[i]:SEG[i + 1]], rel[:, SEG[i]:SEG[i + 1]], pos[:, i:i + 1], None,
                                      ALU.mult).then_inc(nd_done, 1)

            dve.wait_ge(consts_in, 96)
            skewed(dve, [(1, norm1_scale), (0, norm1_stats), (2, norm2_stats), (1, add_skip), (2, norm2_scale),
                         (0, frames_sum)], prelude)

        @block.gpsimd
        def _(pool):
            def over_tiles(v):
                return v[:, :].rearrange("p (a c) -> p a c", a=1).to_broadcast([R, NT, C])

            def root(mv, ve, rs, aggr, eps_done, rstd_done):
                def step(b, par):
                    wait_alone(pool, (aggr, count(b, NT, NT)))
                    pool.tensor_tensor(ve[:, par, :], mv[:, par, :, 1], eps[0:R, :], ALU.add).then_inc(eps_done, 1)
                    wait_alone(pool, (eps_done, count(b, 1, 1)))
                    pool.tensor_tensor(rs[:, par, :], ve[:, par, :], neghalf[0:R, :], ALU.pow).then_inc(rstd_done, 1)
                return step

            def norm1_gain(b, par):
                wait_alone(pool, (scaled1, count(b, NT, NT)))
                pool.tensor_tensor(y[:, par, :, :], y[:, par, :, :], over_tiles(gf), ALU.mult).then_inc(gained1, 1)
                wait_alone(pool, (gained1, count(b, 1, 1)))
                pool.tensor_tensor(y[:, par, :, :], y[:, par, :, :], over_tiles(bf), ALU.add).then_inc(fused, 1)

            def norm2_gain(b, par):
                wait_alone(pool, (scaled2, count(b, NT, NT)))
                hb = hid[:, rows(b, 0, NT), :]
                pool.tensor_tensor(hb, hb, over_tiles(gl), ALU.mult).then_inc(gained2, 1)
                wait_alone(pool, (gained2, count(b, 1, 1)))
                pool.tensor_tensor(hb, hb, over_tiles(bl), ALU.add).then_inc(final, 1)

            for i in range(NT):
                pool.iota(rel[:, SEG[i]:SEG[i + 1]], [[-1, R * (i + 1)]], base=R * i, channel_multiplier=1,
                          allow_small_or_imprecise_dtypes=True)
                pool.iota(pos[:, i:i + 1], [[0, 1]], base=R * i, channel_multiplier=1,
                          allow_small_or_imprecise_dtypes=True)
            pool.memset(w2g[:, :], 0.0).then_inc(zeroed, 1)
            pool.wait_ge(zeroed, 1)
            pool.nop().then_inc(iota_done, 1)
            pool.wait_ge(consts_in, 96)
            skewed(pool, [(1, norm1_gain), (0, root(mv, ve, rs, aggr1, eps1, rstd1)),
                          (2, root(mv2, ve2, rs2, aggr2, eps2, rstd2)), (2, norm2_gain)])


def attention(nc, ident, neghalf, eps, hid, first, wq_in, wk_in, wv_in, scale, bias, tail):
    tag = "a" if first else "f"
    with ExitStack() as ctx:
        m = Memory(nc, ctx, tag)
        XW = NT * R
        wqk = m.sb("wqk", [128, KC, 2 * C])
        wv = m.sb("wv", [128, KC, C])
        wo = m.sb("wo", [128, KC, C]) if first else None
        wg = None if first else m.sb("wg", [128, KC, E])
        qkb = m.sb("qkb", [128, 2 * KC])
        vb = m.sb("vb", [R, C])
        ob = m.sb("ob", [R, C])
        ob2 = None if first else m.sb("ob2", [R, C])
        st = m.sb("st", [R, NT, 6])
        mv = m.sb("mv", [R, NT, 2])
        ve = m.sb("ve", [R, NT])
        rs = m.sb("rs", [R, NT])
        xn = m.sb("xn", [R, NT, C])
        xr = None if first else m.sb("xr", [R, 2, NT, C])
        xT = m.sb("xT", [128, KC, XW])
        f = m.sb("f", [128, 2, XW])
        w_stage = [v[:, :, :].rearrange("p a t -> p (a t)") for v in (f, xT)]
        part = [m.sb(f"part{n}", [128, 2 * KC, XW], BF16) for n in range(3)]
        qs = [m.sb(f"qs{n}", [STACK, H, XW], BF16) for n in range(2)]
        ks = [m.sb(f"ks{n}", [STACK, H, XW], BF16) for n in range(2)]
        VW = HD + 1
        OR = 32
        vx = [m.sb(f"vx{n}", [R, NT, H, VW]) for n in range(2)]
        sc = m.sb("sc", [R, 2, CAUSAL])
        nmx = m.sb("nmx", [R, 2, NT])
        pr = m.sb("pr", [R, 2, CAUSAL])
        pT = m.sb("pT", [R, 2, CAUSAL])
        oT = m.sb("oT", [128, XW])
        rden = m.sb("rden", [R, NT, 4])
        y = m.sb("y", [R, 2, NT, C])
        yT = xT if first else m.sb("yT", [128, KC, XW])
        p_s = [[m.ps(f"p_s{n}{u}", [128, 512]) for u in range(2)] for n in range(2)]
        p_t = [m.ps(f"p_t{u}", [128, 512]) for u in range(2)]
        p_o = m.ps("p_o", [128, 512])
        p_m = m.ps("p_m", [128, 512])
        S = {n: m.sem(n) for n in (
            "consts_in", "ones_set", "gaps_zeroed", "table_ready", "no_bias", "wqk_ready", "bias_scaled", "stats", "aggr", "eps_added", "rstd", "normed", "xt_full", "xt_ready",
            "qk_full", "f_ready", "part0", "residual1", "part1", "part2", "v_full", "v_ready", "scored", "biased",
            "exped", "pt_full", "ptx_ready", "pty_ready", "weighed", "o_evac", "o_back", "recip", "y_ready",
            "yt_full", "yt_ready", "out_full", "out_added", "tail_done")}
        S2 = {} if first else {n: m.sem(n) for n in ("stats_y", "aggr_y", "eps_y", "rstd_y", "normed_y", "gained",
                                                     "shifted", "summed", "resid_added", "ids_set",
                                                     "empty_set")}
        stacked = [m.sem(f"stacked{n}") for n in range(2)]
        table_in = [m.sem(f"table_in{n}") for n in range(4)] if first else None
        y_out = [m.sem(f"y_out{n}") for n in range(2)]
        h_out = [m.sem(f"h_out{n}") for n in range(2)]
        if not first:
            empty = m.sb("empty", [SLOT, 2, CLEAR, ROWW])
            id_step = m.sb("id_step", [SLOT, CLEAR], I32)
            cleared = [m.sem(f"cleared{n}") for n in range(2)]
            y_st, y_mv = m.sb("y_st", [R, NT, 6]), m.sb("y_mv", [R, NT, 2])
            y_ve, y_rs = m.sb("y_ve", [R, NT]), m.sb("y_rs", [R, NT])

        N_CONST = tail["n_const"]
        PAIRS = [range(j, min(j + 2, NT)) for j in range(0, NT, 2)]
        NP = len(PAIRS)
        block = ctx.enter_context(nc.Block())

        @block.sync
        def _(sp):
            for k in range(KC):
                for n, w_ in enumerate((wq_in, wk_in, wv_in)):
                    dst = wv[:, k, :] if n == 2 else w_stage[k][:, n * C:(n + 1) * C]
                    if not first:
                        dst = dst.rearrange("p (h d) -> p h d", d=HD)
                    sp.dma_start(dst, w_(k)).then_inc(S["consts_in"], 16)
            tail["load"](sp, qkb, vb, ob, ob2, wo, wg, S["consts_in"])
            if first:
                tail["load_table"](sp, table_in)

            def stacks(b, par):
                for blk in range(2 * KC):
                    n = blk % 2
                    wait_alone(sp, (S["part2"], count(b, 2 * KC, blk + 1)),
                                   (S["scored"], count(b, 2 * H, -2 * H)))
                    to, parts = (qs, Q_PARTS) if blk < KC else (ks, K_PARTS)
                    at = blk % KC * (H // KC)
                    for r, c in enumerate(parts):
                        sp.dma_start(to[par][r * HD:(r + 1) * HD, at:at + H // KC, :],
                                     part[c][:, blk, :]).then_inc(stacked[n], 16)

            def clear(b, par):
                wait_alone(sp, (S2["ids_set"], count(b, 1, 1)))
                at = count(b, CLEAR, 0)
                at = slice(at, at + CLEAR) if isinstance(at, int) else bass.ds(at, CLEAR)
                sp.dma_start(tail["slot_rows"][:, at, :], empty[:, par, :, :]).then_inc(cleared[par], 16)

            def body(b, par, prologue, epilogue):
                if not first:
                    clear(b, par)
                if prologue:
                    stacks(after(b), 1 - par)
                if epilogue and not first:
                    pb = before(b)
                    wait_alone(sp, (S2["summed"], count(pb, 1, 1)))
                    sp.dma_start(tail["y_rows"][:, rows(pb, 0, NT), :], y[:, 1 - par, :, :]).then_inc(y_out[1 - par], 16)
                    wait_alone(sp, (S2["resid_added"], count(pb, 1, 1)))
                    sp.dma_start(tail["h_rows"][:, rows(pb, 0, NT), :], hid[:, rows(pb, 0, NT), :]
                                 ).then_inc(h_out[1 - par], 16)

            run_batches(sp, lambda: stacks((None, 0, 2), 0), body)
            if not first:
                sp.wait_ge(S2["summed"], B)
                sp.dma_start(tail["y_rows"][:, (B - 1) * NT:B * NT, :], y[:, 1, :, :]).then_inc(y_out[1], 16)
                sp.wait_ge(S2["resid_added"], B)
                sp.dma_start(tail["h_rows"][:, (B - 1) * NT:B * NT, :],
                             hid[:, (B - 1) * NT:B * NT, :]).then_inc(h_out[1], 16)
                for n in range(2):
                    sp.wait_ge(y_out[n], 16 * B // 2)
                    sp.wait_ge(h_out[n], 16 * B // 2)
                    sp.wait_ge(cleared[n], 16 * B // 2)

        @block.tensor
        def _(pe):
            shared = {}

            def take_bank():
                if "by" in shared:
                    wait(pe, *shared["by"])

            def x_transpose(b, par, k):
                take_bank()
                wait(pe, S["normed"], count(b, NT, NT))
                wait(pe, S["v_full"], count(b, NP, 0))
                for j in range(NT):
                    mm = pe.transpose(p_m[:, j * R:(j + 1) * R], xn[:, j, k * 128:(k + 1) * 128], ident[0:R, 0:R])
                mm.then_inc(S["xt_full"], 1)
                shared["by"] = (S["xt_ready"], count(b, KC, k + 1))

            def qk_project(b, par, blk):
                take_bank()
                wait(pe, S["xt_ready"], count(b, KC, KC))
                for k in range(KC):
                    mm = pe.matmul(p_m[:, 0:XW], wqk[:, k, blk * 128:(blk + 1) * 128], xT[:, k, :],
                                   start=(k == 0), stop=(k == KC - 1))
                mm.then_inc(S["qk_full"], 1)
                shared["by"] = (S["f_ready"], count(b, 2 * KC, blk + 1))

            def v_project(b, par, p):
                take_bank()
                for n, j in enumerate(PAIRS[p]):
                    for k in range(KC):
                        mm = pe.matmul(p_m[0:R, n * C:(n + 1) * C], xT[:, k, j * R:(j + 1) * R], wv[:, k, :],
                                       start=(k == 0), stop=(k == KC - 1))
                mm.then_inc(S["v_full"], 1)
                shared["by"] = (S["v_ready"], count(b, NP, p + 1))

            def score(b, par, h):
                if h == 0:
                    for n in range(2):
                        wait(pe, stacked[n], count(b, 16 * KC * STACK // HD, 16 * KC * STACK // HD))
                for u, tiles in enumerate(((0, 1), (2,))):
                    wait(pe, S["biased"], count(b, H * NT, NT * (h - 2) + tiles[-1] + 1))
                    for i in tiles:
                        o = SEG[i] if u == 0 else 0
                        mm = pe.matmul(p_s[h % 2][u][0:R, o:o + R * (i + 1)], qs[par][:, h, i * R:(i + 1) * R],
                                       ks[par][:, h, 0:R * (i + 1)], start=True, stop=True)
                    mm.then_inc(S["scored"], 1)

            def transpose_probs(b, par, h):
                if h < 0:
                    b, par, h = before(b), 1 - par, h + H
                    if b[0] is None and b[1] < 0:
                        return
                wait(pe, S["exped"], count(b, H * NT, NT * h + NT))
                wait(pe, S["ptx_ready"], count(b, H, h))
                for i in range(NT):
                    mm = pe.transpose(p_t[0][0:R, i * R:(i + 1) * R], pr[:, h % 2, SEG[i]:SEG[i] + R], ident[0:R, 0:R])
                mm.then_inc(S["pt_full"], 1)
                wait(pe, S["pty_ready"], count(b, H, h))
                for o, (i, s) in enumerate(((1, 1), (2, 1), (2, 2))):
                    mm = pe.transpose(p_t[1][0:R, o * R:(o + 1) * R], pr[:, h % 2, SEG[i] + s * R:SEG[i] + (s + 1) * R],
                                      ident[0:R, 0:R])
                mm.then_inc(S["pt_full"], 1)

            def weigh(b, par, h):
                if h < 0:
                    b, par, h = before(b), 1 - par, h + H
                    if b[0] is None and b[1] < 0:
                        return
                q = h % 4
                if q == 0:
                    wait(pe, S["o_evac"], count(b, H // 4, h // 4))
                if h == 0:
                    wait(pe, S["v_ready"], count(b, NP, NP))
                wait(pe, S["ptx_ready"], count(b, H, h + 1))
                wait(pe, S["pty_ready"], count(b, H, h + 1))
                for s in range(NT):
                    at = (0, XW, 2 * XW - R)[s]
                    mm = pe.matmul(p_o[q * OR:q * OR + VW, s * R:XW], vx[par][:, s, h, :],
                                   pT[:, h % 2, at:at + XW - s * R], start=(s == 0), stop=(s == NT - 1))
                mm.then_inc(S["weighed"], 1)

            def outputs_back(b, par, g):
                take_bank()
                wait(pe, S["o_evac"], count(b, H // 4, g + 1))
                for j in range(NT):
                    mm = pe.transpose(p_m[0:R, j * 128:(j + 1) * 128], oT[:, j * R:(j + 1) * R], ident[:, :])
                mm.then_inc(S["o_back"], 1)
                shared["by"] = (S["y_ready"], count(b, H // 4, g + 1))

            def y_transpose(b, par, k):
                take_bank()
                if first:
                    wait(pe, S["y_ready"], count(b, H // 4, H // 4))
                else:
                    wait(pe, S2["summed"], count(b, 1, 1))
                for j in range(NT):
                    mm = pe.transpose(p_m[:, j * R:(j + 1) * R], y[:, par, j, k * 128:(k + 1) * 128], ident[0:R, 0:R])
                mm.then_inc(S["yt_full"], 1)
                shared["by"] = (S["yt_ready"], count(b, KC, k + 1))

            def out_project(b, par, p):
                take_bank()
                wait(pe, S["yt_ready"], count(b, KC, KC))
                for n, j in enumerate(PAIRS[p]):
                    for k in range(KC):
                        mm = pe.matmul(p_m[0:R, n * C:(n + 1) * C], yT[:, k, j * R:(j + 1) * R], wo[:, k, :],
                                       start=(k == 0), stop=(k == KC - 1))
                mm.then_inc(S["out_full"], 1)
                shared["by"] = (S["out_added"], count(b, NP, p + 1))

            def gate(b, par, _):
                take_bank()
                wait(pe, S["yt_ready"], count(b, KC, KC))
                for j in range(NT):
                    for k in range(KC):
                        mm = pe.matmul(p_m[0:R, j * E:(j + 1) * E], yT[:, k, j * R:(j + 1) * R], wg[:, k, :],
                                       start=(k == 0), stop=(k == KC - 1))
                mm.then_inc(S["out_full"], 1)
                shared["by"] = (S["out_added"], count(b, 1, 1))

            def own(n):
                return {6: [(outputs_back, 0)], 10: [(outputs_back, 1)], 14: [(outputs_back, 2)]}.get(n, [])

            pro = {0: [(x_transpose, 0)], 1: [(x_transpose, 1)], 3: [(qk_project, 0)], 4: [(qk_project, 1)],
                   5: [(v_project, 0)], 7: [(qk_project, 2)], 8: [(qk_project, 3)], 9: [(v_project, 1)]}
            epi = {11: [(y_transpose, 0)], 12: [(y_transpose, 1)], 13: [(out_project if first else gate, 0)]}
            if first:
                epi[15] = [(out_project, 1)]

            def body(b, par, prologue, epilogue):
                if b[0] is not None:
                    shared["by"] = (S["out_added"], count(before(b, 2), NP if first else 1, NP if first else 1))
                for n in range(H):
                    transpose_probs(b, par, n - 1)
                    if n + 1 < H:
                        score(b, par, n + 1)
                    elif prologue:
                        score(after(b), 1 - par, 0)
                    weigh(b, par, n - 2)
                    if epilogue:
                        if n == 2:
                            outputs_back(before(b), 1 - par, 3)
                        for step, arg in epi.get(n, []):
                            step(before(b), 1 - par, arg)
                    for step, arg in own(n):
                        step(b, par, arg)
                    if prologue:
                        for step, arg in pro.get(n, []):
                            step(after(b), 1 - par, arg)

            def start():
                pe.wait_ge(S["consts_in"], 16 * N_CONST)
                pe.wait_ge(S["wqk_ready"], 2 * KC * KC)
                pe.wait_ge(S["gaps_zeroed"], 1)
                for n in range(H):
                    for step, arg in pro.get(n, []):
                        step((None, 0, 2), 0, arg)
                score((None, 0, 2), 0, 0)

            run_batches(pe, start, body)
            b, par = (None, B - 1, 2), 1
            transpose_probs(b, par, H - 1)
            weigh(b, par, H - 2)
            weigh(b, par, H - 1)
            outputs_back(b, par, 3)
            for n in range(H):
                for step, arg in epi.get(n, []):
                    step(b, par, arg)

        @block.vector
        def _(dve):
            def norm_stats(b, par, _):
                for j in range(NT):
                    dve.bn_stats(st[:, j, :], hid[:, row(b, j), :]).then_inc(S["stats"], 1)
                for j in range(NT):
                    wait_alone(dve, (S["stats"], count(b, NT, j + 1)))
                    dve.bn_aggr(mv[:, j, :], st[:, j, :]).then_inc(S["aggr"], 1)

            def norm_scale(b, par, _):
                wait(dve, S["rstd"], count(b, 1, 1))
                wait(dve, S["xt_full"], count(b, KC, 0))
                if not first:
                    wait(dve, S2["shifted"], count(b, 1, 0))
                for j in range(NT):
                    dve.tensor_scalar(xn[:, j, :], hid[:, row(b, j), :], mv[:, j, 0:1], rs[:, j:j + 1],
                                      ALU.subtract, ALU.mult).then_inc(S["normed"], 1)

            def first_part(b, par, blk):
                n = blk % 2
                wait(dve, S["f_ready"], count(b, 2 * KC, blk + 1))
                free_part(dve, b, blk)
                dve.tensor_copy(part[0][:, blk, :], f[:, n, :]).then_inc(S["part0"], 1)

            def second_part(b, par, blk):
                n = blk % 2
                wait(dve, S["residual1"], count(b, 2 * KC, blk + 1))
                free_part(dve, b, blk)
                dve.tensor_copy(part[1][:, blk, :], f[:, n, :]).then_inc(S["part1"], 1)

            def values(b, par, p):
                wait(dve, S["v_full"], count(b, NP, p + 1))
                wait(dve, S["weighed"], count(b, H, -H))
                k = len(PAIRS[p])
                dve.tensor_tensor(vx[par][:, PAIRS[p][0]:PAIRS[p][0] + k, :, 0:HD],
                                  p_m[0:R, 0:k * C].rearrange("p (j h d) -> p j h d", h=H, d=HD),
                                  vb[:, :].rearrange("p (a h d) -> p a h d", a=1, d=HD).to_broadcast([R, k, H, HD]),
                                  ALU.add).then_inc(S["v_ready"], 1)

            def add_bias(b, par, h):
                for i in range(NT):
                    u, o = (0, SEG[i]) if i < 2 else (1, 0)
                    if i != 1:
                        wait_alone(dve, (S["scored"], count(b, 2 * H, 2 * h + u + 1)))
                    if i == 0:
                        wait_alone(dve, (S["exped"], count(b, NT * H, NT * (h - 1))))
                    dve.tensor_tensor_reduce(out=sc[:, h % 2, SEG[i]:SEG[i + 1]],
                                             in0=p_s[h % 2][u][0:R, o:o + R * (i + 1)], in1=bias(h, i),
                                             scale=-1.0, scalar=BIG, op0=ALU.add, op1=ALU.min,
                                             accum_out=nmx[:, h % 2, i:i + 1]).then_inc(S["biased"], 1)

            def probs_back(b, par, h):
                if h < 0:
                    b, par, h = before(b), 1 - par, h + H
                    if b[0] is None and b[1] < 0:
                        return
                wait(dve, S["pt_full"], count(b, 2 * H, 2 * h + 1))
                wait(dve, S["weighed"], count(b, H, h - 1))
                dve.tensor_copy(pT[:, h % 2, 0:XW], p_t[0][0:R, 0:XW]).then_inc(S["ptx_ready"], 1)

            def normalize(b, par, g):
                wait(dve, S["o_back"], count(b, H // 4, g + 1))
                o = p_m[0:R, 0:NT * 128].rearrange("p (j q v) -> p j q v", j=NT, q=4)
                wait(dve, S["y_ready"], count(b, H // 4, g))
                dve.reciprocal(rden[:, :, :], o[:, :, :, HD]).then_inc(S["recip"], 1)
                wait(dve, S["recip"], count(b, H // 4, g + 1))
                if first:
                    wait(dve, S["yt_full"], count(b, KC, -KC))
                else:
                    wait(dve, S["yt_full"], count(b, KC, -KC))
                    wait(dve, S2["resid_added"], count(b, 1, -1))
                    wait(dve, y_out[par], lane_count(b, 16, 0))
                dst = y[:, par, :, g * 4 * HD:(g + 1) * 4 * HD].rearrange("p j (q d) -> p j q d", q=4)
                dve.tensor_tensor(dst, o[:, :, :, 0:HD],
                                  rden[:, :, :].rearrange("p j (q a) -> p j q a", a=1).to_broadcast([R, NT, 4, HD]),
                                  ALU.mult).then_inc(S["y_ready"], 1)

            def add_output(b, par, p):
                k = len(PAIRS[p])
                hb = hid[:, rows(b, PAIRS[p][0], k), :]
                wait(dve, S["out_full"], count(b, NP, p + 1))
                dve.tensor_tensor(hb, p_m[0:R, 0:k * C].rearrange("p (j c) -> p j c", c=C), hb,
                                  ALU.add).then_inc(S["out_added"], 1)

            def y_stats(b, par, _):
                wait(dve, S["y_ready"], count(b, H // 4, H // 4))
                for j in range(NT):
                    dve.bn_stats(y_st[:, j, :], y[:, par, j, :]).then_inc(S2["stats_y"], 1)
                for j in range(NT):
                    wait_alone(dve, (S2["stats_y"], count(b, NT, j + 1)))
                    dve.bn_aggr(y_mv[:, j, :], y_st[:, j, :]).then_inc(S2["aggr_y"], 1)

            def y_scale(b, par, _):
                wait(dve, S2["rstd_y"], count(b, 1, 1))
                for j in range(NT):
                    dve.tensor_scalar(y[:, par, j, :], y[:, par, j, :], y_mv[:, j, 0:1], y_rs[:, j:j + 1],
                                      ALU.subtract, ALU.mult).then_inc(S2["normed_y"], 1)

            def keep_logits(b, par, _):
                wait(dve, S["out_full"], count(b, 1, 1))
                dve.tensor_copy(tail["logits"][:, rows(b, 0, NT), :],
                                p_m[0:R, 0:NT * E].rearrange("p (j e) -> p j e", e=E)).then_inc(S["out_added"], 1)

            epi_mid = {3: [(normalize, 3)], 14: [(add_output if first else keep_logits, 0)]}
            epi = {} if first else {3: [(y_stats, 0)], 5: [(y_scale, 0)]}
            own = {7: [(normalize, 0)], 11: [(normalize, 1)], 15: [(normalize, 2)]}
            pro_mid = {6: [(values, 0)], 10: [(values, 1)]}
            pro = {4: [(first_part, 0)], 5: [(second_part, 0), (first_part, 1)], 6: [(second_part, 1)],
                   8: [(first_part, 2)], 9: [(second_part, 2), (first_part, 3)], 10: [(second_part, 3)]}
            norm_ahead = {12: [(norm_stats, 0)], 13: [(norm_scale, 0)]}

            def body(b, par, prologue, epilogue):
                nxt, last = after(b), before(b)

                def steps(table, at, p):
                    for step, arg in table:
                        step(at, p, arg)

                for n in range(H):
                    add_bias(b, par, n)
                    if first and n == 0 and (b[0] is not None or b[1] >= 2):
                        add_output(before(b, 2), par, 1)
                    if prologue:
                        steps(pro_mid.get(n, []), nxt, 1 - par)
                    if epilogue:
                        steps(epi_mid.get(n, []), last, 1 - par)
                    steps(own.get(n, []), b, par)
                    if b[0] is not None or b[1] < B - 2:
                        steps(norm_ahead.get(n, []), after(nxt), par)
                    probs_back(b, par, n - 1)
                    if epilogue:
                        steps(epi.get(n, []), last, 1 - par)
                    if prologue:
                        steps(pro.get(n, []), nxt, 1 - par)

            def start():
                dve.wait_ge(S["consts_in"], 16 * N_CONST)
                for k in range(KC):
                    for n in range(2 * KC):
                        dve.tensor_copy(wqk[:, k, n * 128:(n + 1) * 128].rearrange("p (d h) -> p d h", d=HD),
                                        w_stage[k][:, n * 128:(n + 1) * 128].rearrange("p (h d) -> p d h", d=HD)
                                        ).then_inc(S["wqk_ready"], 1)
                if not first:
                    dve.wait_ge(S["no_bias"], 2)
                dve.tensor_scalar(qkb[:, 0:KC], qkb[:, 0:KC], scale, None, ALU.mult).then_inc(S["bias_scaled"], 1)
                dve.memset(p_o[:, :], 0.0).then_inc(S["gaps_zeroed"], 1)
                dve.wait_ge(S["ones_set"], 2)
                norm_stats((None, 0, 2), 0, 0)
                norm_scale((None, 0, 2), 0, 0)
                for n in range(H):
                    for step, arg in pro_mid.get(n, []) + pro.get(n, []):
                        step((None, 0, 2), 0, arg)
                norm_stats((None, 1, 2), 1, 0)
                norm_scale((None, 1, 2), 1, 0)
                if first:
                    dve.wait_ge(S["table_ready"], 4 * NT)

            def free_part(eng, b, blk):
                wait(eng, stacked[blk % 2], count(b, 16 * KC * STACK // HD, 0))

            run_batches(dve, start, body)
            b, par = (None, B - 1, 2), 1
            probs_back(b, par, H - 1)
            if first:
                add_output(before(b), 1 - par, 1)
            for n in range(H):
                for step, arg in epi_mid.get(n, []) + epi.get(n, []):
                    step(b, par, arg)
            if first:
                add_output(b, par, 1)

        @block.scalar
        def _(act):
            def x_back(b, par, k):
                wait(act, S["xt_full"], count(b, KC, k + 1))
                if first:
                    wait(act, S["out_full"], count(b, NP, -2 * NP))
                wait(act, S["v_full"], count(b, NP, 0))
                act.activation(xT[:, k, :], p_m[:, 0:XW], ACT.Copy).then_inc(S["xt_ready"], 1)

            def qk_back(b, par, blk):
                n = blk % 2
                wait(act, S["qk_full"], count(b, 2 * KC, blk + 1))
                wait(act, S["part2"], count(b, 2 * KC, blk - 1))
                act.activation(f[:, n, :], p_m[:, 0:XW], ACT.Identity, bias=qkb[:, blk:blk + 1],
                               scale=(scale if blk < KC else 1.0)).then_inc(S["f_ready"], 1)

            def exponentiate(b, par, h):
                for i in range(NT):
                    wait(act, S["biased"], count(b, NT * H, NT * h + i + 1))
                    if i == 0:
                        wait(act, S["pt_full"], count(b, 2 * H, 2 * (h - 1)))
                    act.activation(pr[:, h % 2, SEG[i]:SEG[i + 1]], sc[:, h % 2, SEG[i]:SEG[i + 1]], ACT.Exp,
                                   bias=nmx[:, h % 2, i:i + 1], scale=-1.0).then_inc(S["exped"], 1)

            def probs_back(b, par, h):
                if h < 0:
                    b, par, h = before(b), 1 - par, h + H
                    if b[0] is None and b[1] < 0:
                        return
                wait(act, S["pt_full"], count(b, 2 * H, 2 * h + 2))
                wait(act, S["weighed"], count(b, H, h - 1))
                act.activation(pT[:, h % 2, XW:2 * XW], p_t[1][0:R, 0:XW], ACT.Copy).then_inc(S["pty_ready"], 1)

            def outputs_out(b, par, g):
                wait(act, S["weighed"], count(b, H, 4 * g + 4))
                wait(act, S["o_back"], count(b, H // 4, g))
                act.activation(oT[:, :], p_o[:, 0:XW], ACT.Copy).then_inc(S["o_evac"], 1)

            def y_back(b, par, k):
                wait(act, S["yt_full"], count(b, KC, k + 1))
                wait(act, S["out_full"], count(b, NP if first else 1, 0))
                if first and (b[0] is not None or b[1] < B - 2):
                    wait(act, S["v_full"], count(b, NP, 3 * NP))
                act.activation(yT[:, k, :], p_m[:, 0:XW], ACT.Copy).then_inc(S["yt_ready"], 1)

            epi = {2: [(outputs_out, 3)], 12: [(y_back, 0)], 13: [(y_back, 1)]}
            own = {6: [(outputs_out, 0)], 10: [(outputs_out, 1)], 14: [(outputs_out, 2)]}
            pro = {1: [(x_back, 0)], 2: [(x_back, 1)], 4: [(qk_back, 0)], 5: [(qk_back, 1)], 8: [(qk_back, 2)],
                   9: [(qk_back, 3)]}

            def body(b, par, prologue, epilogue):
                for n in range(H):
                    if epilogue:
                        for step, arg in epi.get(n, []):
                            step(before(b), 1 - par, arg)
                    for step, arg in own.get(n, []):
                        step(b, par, arg)
                    if prologue:
                        for step, arg in pro.get(n, []):
                            step(after(b), 1 - par, arg)
                    exponentiate(b, par, n)
                    probs_back(b, par, n - 1)

            def start():
                act.wait_ge(S["bias_scaled"], 1)
                act.wait_ge(S["wqk_ready"], 2 * KC * KC)
                for n in range(H):
                    for step, arg in pro.get(n, []):
                        step((None, 0, 2), 0, arg)

            run_batches(act, start, body)
            b, par = (None, B - 1, 2), 1
            probs_back(b, par, H - 1)
            for n in range(H):
                for step, arg in epi.get(n, []):
                    step(b, par, arg)

        @block.gpsimd
        def _(pool):
            def root(b, par, _):
                wait_alone(pool, (S["aggr"], count(b, NT, NT)))
                pool.tensor_tensor(ve[:, :], mv[:, :, 1], eps[0:R, :], ALU.add).then_inc(S["eps_added"], 1)
                wait_alone(pool, (S["eps_added"], count(b, 1, 1)),
                                 (S["normed"], count(b, NT, 0)))
                pool.tensor_tensor(rs[:, :], ve[:, :], neghalf[0:R, :], ALU.pow).then_inc(S["rstd"], 1)

            def residual(b, par, blk):
                n = blk % 2
                wait_alone(pool, (S["part0"], count(b, 2 * KC, blk + 1)))
                pool.tensor_tensor(f[:, n, :], f[:, n, :], part[0][:, blk, :], ALU.subtract).then_inc(S["residual1"], 1)

            def third_part(b, par, blk):
                n = blk % 2
                wait_alone(pool, (S["part1"], count(b, 2 * KC, blk + 1)),
                                 (stacked[n], count(b, 16 * KC * STACK // HD, 0)))
                pool.tensor_tensor(part[2][:, blk, :], f[:, n, :], part[1][:, blk, :],
                                   ALU.subtract).then_inc(S["part2"], 1)

            def over_tiles(v):
                return v[:, :].rearrange("p (a c) -> p a c", a=1).to_broadcast([R, NT, C])

            def output_bias(b, par, _):
                wait_alone(pool, (S["out_added"], count(b, NP, NP)))
                hb = hid[:, rows(b, 0, NT), :]
                pool.tensor_tensor(hb, hb, over_tiles(ob), ALU.add).then_inc(S["tail_done"], 1)

            def root_y(b, par, _):
                wait_alone(pool, (S2["aggr_y"], count(b, NT, NT)))
                pool.tensor_tensor(y_ve[:, :], y_mv[:, :, 1], eps[0:R, :], ALU.add).then_inc(S2["eps_y"], 1)
                wait_alone(pool, (S2["eps_y"], count(b, 1, 1)),
                                 (S2["normed_y"], count(b, NT, 0)))
                pool.tensor_tensor(y_rs[:, :], y_ve[:, :], neghalf[0:R, :], ALU.pow).then_inc(S2["rstd_y"], 1)

            def shift(b, par, _):
                wait_alone(pool, (S["normed"], count(b, NT, NT)),
                                 (S2["summed"], count(b, 1, -1)))
                pool.tensor_tensor(xr[:, par, :, :], xn[:, :, :], over_tiles(ob2), ALU.add).then_inc(S2["shifted"], 1)

            def number(b, par):
                ids = empty[:, par, :, C].bitcast(I32)
                wait_alone(pool, (S2["ids_set"], count(b, 1, 2)),
                                 (cleared[par], lane_count(b, 16, 16)))
                pool.tensor_tensor(ids, ids, id_step[:, :], ALU.add).then_inc(S2["ids_set"], 1)

            def gain(b, par, _):
                yb = y[:, par, :, :]
                wait_alone(pool, (S2["normed_y"], count(b, NT, NT)))
                pool.tensor_tensor(yb, yb, over_tiles(ob), ALU.mult).then_inc(S2["gained"], 1)
                wait_alone(pool, (S2["gained"], count(b, 1, 1)))
                pool.tensor_tensor(yb, yb, xr[:, par, :, :], ALU.add).then_inc(S2["summed"], 1)

            def add_residual(b, par, _):
                wait_alone(pool, (S2["summed"], count(b, 1, 1)))
                hb = hid[:, rows(b, 0, NT), :]
                pool.tensor_tensor(hb, hb, y[:, par, :, :], ALU.add).then_inc(S2["resid_added"], 1)

            epi = {15: [(output_bias, 0)]} if first else {3: [(root_y, 0)], 6: [(gain, 0)], 11: [(add_residual, 0)]}
            pro = {4: [(residual, 0)], 5: [(third_part, 0), (residual, 1)], 6: [(third_part, 1)],
                   8: [(residual, 2)], 9: [(third_part, 2), (residual, 3)], 10: [(third_part, 3)]}
            if not first:
                pro[11] = [(shift, 0)]

            def body(b, par, prologue, epilogue):
                ahead = b[0] is not None or b[1] < B - 2
                for n in range(H):
                    if prologue:
                        for step, arg in pro.get(n, []):
                            step(after(b), 1 - par, arg)
                    if epilogue:
                        for step, arg in epi.get(n, []):
                            step(before(b), 1 - par, arg)
                    if ahead and n == 12:
                        root(before(b, -2), par, 0)
                if not first and ahead:
                    number(b, par)

            def start():
                if not first:
                    pool.memset(qkb[:, :], 0.0).then_inc(S["no_bias"], 1)
                    pool.memset(vb[:, :], 0.0).then_inc(S["no_bias"], 1)
                    pool.memset(empty[:, :, :, 0:C], 0.0).then_inc(S2["empty_set"], 1)
                    pool.iota(id_step[:, :], [[0, CLEAR]], base=2 * CLEAR * SLOT, channel_multiplier=0
                              ).then_inc(S2["empty_set"], 1)
                    pool.wait_ge(S2["empty_set"], 2)
                    for n in range(2):
                        pool.iota(empty[:, n, :, C].bitcast(I32), [[SLOT, CLEAR]], base=DUMP + n * CLEAR * SLOT,
                                  channel_multiplier=1).then_inc(S2["ids_set"], 1)
                for n in range(2):
                    pool.memset(vx[n][:, :, :, HD:VW], 1.0).then_inc(S["ones_set"], 1)
                pool.wait_ge(S["consts_in"], 16 * N_CONST)
                root((None, 0, 2), 0, 0)
                for n in range(H):
                    for step, arg in pro.get(n, []):
                        step((None, 0, 2), 0, arg)
                root((None, 1, 2), 1, 0)
                if first:
                    tail["mask_table"](pool, table_in, S["table_ready"])

            run_batches(pool, start, body)
            for n in range(H):
                for step, arg in epi.get(n, []):
                    step((None, B - 1, 2), 1, arg)


def run_batches(eng, start, body):
    start()
    body((None, 0, 2), 0, True, False)
    body((None, 1, 2), 1, True, True)
    with eng.Fori(0, (B - 4) // 2) as i:
        for par in range(2):
            body((i, 2 + par, 2), par, True, True)
    body((None, B - 2, 2), 0, True, True)
    body((None, B - 1, 2), 1, False, True)


def attend(nc, ident, neghalf, eps, hid, bias_dram, wqkv, bqkv, wproj, bproj):
    with ExitStack() as ctx:
        bias = Memory(nc, ctx, "held").sb("bias", [R, H, CAUSAL])
        attend_with(nc, ident, neghalf, eps, hid, bias, bias_dram, wqkv, bqkv, wproj, bproj)


def attend_with(nc, ident, neghalf, eps, hid, bias, bias_dram, wqkv, bqkv, wproj, bproj):
    def load_table(sp, table_in):
        for q in range(4):
            sp.dma_start(bias[:, q * 4:(q + 1) * 4, :], bias_dram[q * 4:(q + 1) * 4, 0:R, :].rearrange("h r c -> r h c")
                         ).then_inc(table_in[q], 16)

    def mask_table(pool, table_in, table_ready):
        for q in range(4):
            pool.wait_ge(table_in[q], 16)
            for i in range(NT):
                diag = bias[:, q * 4:(q + 1) * 4, SEG[i] + R * i:SEG[i + 1]]
                pool.affine_select(out=diag, in_=diag, compare_op=ALU.is_ge, fill=NEG, base=0,
                                   pattern=[[0, 4], [-1, R]], channel_multiplier=1).then_inc(table_ready, 1)

    def load(sp, qkb, vb, ob, ob2, wo, wg, consts_in):
        for n in range(2 * KC):
            sp.dma_start(qkb[:, n:n + 1], bqkv[n * 128:(n + 1) * 128].rearrange("(h d a) -> d h a", d=HD, a=1),
                         allow_slow_non_contiguous=True).then_inc(consts_in, 16)
        for vec, sb in ((bqkv[2 * C:3 * C], vb), (bproj, ob)):
            sp.dma_start(sb[:, :], vec.rearrange("(a c) -> a c", a=1).to_broadcast([R, C])).then_inc(consts_in, 16)
        sp.dma_start(wo[:, :, :], wproj.rearrange("(k p) n -> p k n", p=128)).then_inc(consts_in, 16)

    cols = [lambda k, n=n: wqkv[k * 128:(k + 1) * 128, n * C:(n + 1) * C] for n in range(3)]
    attention(nc, ident, neghalf, eps, hid, True, *cols, float(HD) ** -0.5,
              lambda h, i: bias[:, h, SEG[i]:SEG[i + 1]],
              {"load": load, "n_const": 5 * KC + 3, "load_table": load_table, "mask_table": mask_table})


def attend_in_ffn(nc, ident, neghalf, eps, hid, logits, y_dram, h_dram, slots_dram, wq, wk, wv, gate_w, g1, b1):
    with ExitStack() as ctx:
        m = Memory(nc, ctx, "mask")
        mask = m.sb("mask", [R, CAUSAL])
        zeroed, masked = m.sem("zeroed"), m.sem("masked")
        with nc.Block() as block:

            @block.gpsimd
            def _(pool):
                pool.memset(mask[:, :], 0.0).then_inc(zeroed, 1)
                pool.wait_ge(zeroed, 1)
                for i in range(NT):
                    diag = mask[:, SEG[i] + R * i:SEG[i + 1]]
                    pool.affine_select(out=diag, in_=diag, compare_op=ALU.is_ge, fill=NEG, base=0,
                                       pattern=[[-1, R]], channel_multiplier=1).then_inc(masked, 1)

        def load(sp, qkb, vb, ob, ob2, wo, wg, consts_in):
            for vec, sb in ((g1, ob), (b1, ob2)):
                sp.dma_start(sb[:, :], vec.rearrange("(a c) -> a c", a=1).to_broadcast([R, C])).then_inc(consts_in, 16)
            sp.dma_start(wg[:, :, :], gate_w.rearrange("(k p) n -> p k n", p=128)).then_inc(consts_in, 16)

        cols = [lambda k, w=w: w[:, k * 128:(k + 1) * 128, :].rearrange("h p d -> p h d") for w in (wq, wk, wv)]
        attention(nc, ident, neghalf, eps, hid, False, *cols, float(C) ** -0.5,
                  lambda h, i: mask[:, SEG[i]:SEG[i + 1]],
                  {"load": load, "n_const": 3 * KC + 3, "logits": logits,
                   "y_rows": y_dram.rearrange("(g r) c -> r g c", r=R),
                   "h_rows": h_dram.rearrange("(g r) c -> r g c", r=R),
                   "slot_rows": slots_dram.rearrange("(t p) c -> p t c", p=SLOT)})


N_TOK = B * T
SLOT = 128
SLOT_TILES = (2 * N_TOK + E * (SLOT - 1)) // SLOT
ROWW = C + 1
DUMP = 2 * N_TOK
N_RES = DUMP + SLOT_TILES * SLOT
CLEAR = -(-SLOT_TILES // B)


def route(nc, logits, weights, expert_of, y_dram, slots_dram, load_weights):
    with ExitStack() as ctx:
        m = Memory(nc, ctx, "route")
        GE = TILES * E
        NC_ = -(-N_TOK // SLOT)
        eid = m.sb("eid", [R, TILES, E])
        upper = m.sb("upper", [R, 128])
        ones = m.sb("ones", [R, 128])
        top = m.sb("top", [R, 2, TILES])
        lg2 = m.sb("lg2", [R, TILES, E])
        eq = m.sb("eq", [R, TILES, E])
        idx = m.sb("idx", [R, 2, TILES])
        hot = m.sb("hot", [R, 2, TILES, E])
        both = m.sb("both", [R, TILES, E])
        ediff = m.sb("ediff", [R, TILES])
        esum = m.sb("esum", [R, TILES])
        total = m.sb("total", [128, TILES, E])
        incl = m.sb("incl", [128, TILES, E])
        onesg = m.sb("onesg", [128, TILES])
        steps = m.sb("steps", [128, E, NC_])
        over = m.sb("over", [128, E, NC_])
        ntile = m.sb("ntile", [128, E])
        tend = m.sb("tend", [128, E])
        base = m.sb("base", [128, E])
        slot = m.sb("slot", [R, TILES, E])
        picked = m.sb("picked", [R, TILES, E])
        slotf = m.sb("slotf", [R, 2, TILES])
        sloti = m.sb("sloti", [R, 2, TILES], U32)
        dest = m.sb("dest", [R, 2, TILES], I32)
        tid = m.sb("tid", [1, SLOT_TILES, E])
        past = m.sb("past", [1, SLOT_TILES, E])
        texp = m.sb("texp", [1, SLOT_TILES])
        NB = 4
        ybuf = [m.sb(f"ybuf{n}", [R, ROWW]) for n in range(2 * NB)]
        p_rank = m.ps("p_rank", [128, GE])
        p_total = m.ps("p_total", [128, GE])
        dve_step, pool_set, chosen, ranked, exp_done, slots_ready, dest_set = (m.sem(n) for n in (
            "dve_step", "pool_set", "chosen", "ranked", "exp_done", "slots_ready", "dest_set"))
        y_in = [m.sem(f"y_in{n}") for n in range(2 * NB)]
        sent = [m.sem(f"sent{n}") for n in range(2 * NB)]
        y_rows = y_dram.rearrange("(g r) c -> g r c", r=R)
        block = ctx.enter_context(nc.Block())

        def over_experts(v):
            return v.rearrange("p (g a) -> p g a", a=1).to_broadcast([v.shape[0], v.shape[1], E])

        @block.sync
        def _(sp):
            for g in range(TILES):
                for c in range(2):
                    n = 2 * (g % NB) + c
                    if g >= NB:
                        sp.wait_ge(sent[n], 16 * (g // NB))
                    sp.dma_start(ybuf[n][:, 0:C], y_rows[g]).then_inc(y_in[n], 16)
            load_weights(sp)

        @block.gpsimd
        def _(pool):
            pool.iota(eid[:, :, :], [[0, TILES], [1, E]], base=-E, channel_multiplier=0,
                      allow_small_or_imprecise_dtypes=True).then_inc(pool_set, 1)
            pool.memset(upper[:, :], 1.0).then_inc(pool_set, 1)
            pool.memset(ones[:, :], 1.0).then_inc(pool_set, 1)
            pool.memset(onesg[:, :], 1.0).then_inc(pool_set, 1)
            pool.iota(steps[:, :, :], [[0, E], [SLOT, NC_]], base=0, channel_multiplier=0,
                      allow_small_or_imprecise_dtypes=True).then_inc(pool_set, 1)
            pool.iota(tid[:, :, :], [[1, SLOT_TILES], [0, E]], base=0, channel_multiplier=0,
                      allow_small_or_imprecise_dtypes=True).then_inc(pool_set, 1)
            pool.iota(dest[:, :, :], [[N_TOK, 2], [R, TILES]], base=0, channel_multiplier=1).then_inc(pool_set, 1)
            pool.wait_ge(pool_set, 7)
            pool.affine_select(out=upper[:, :], in_=upper[:, :], compare_op=ALU.is_gt, fill=0.0, base=0,
                               pattern=[[1, 128]], channel_multiplier=-1).then_inc(pool_set, 1)
            pool.wait_ge(slots_ready, 1)
            for g in range(TILES):
                for c in range(2):
                    n = 2 * (g % NB) + c
                    pool.wait_ge(dest_set, 2 * g + c + 1)
                    pool.wait_ge(y_in[n], 16 * (g // NB + 1))
                    pool.indirect_dma_start(out=slots_dram, out_offset=bass.IndirectOffsetOnAxis(
                        ap=sloti[:, c, g:g + 1], axis=0), in_=ybuf[n][:, :], in_offset=None).then_inc(sent[n], 16)
            for n in range(2 * NB):
                pool.wait_ge(sent[n], 16 * (TILES // NB))

        @block.scalar
        def _(act):
            act.wait_ge(chosen, 2)
            act.activation(ediff[:, :], ediff[:, :], ACT.Exp).then_inc(exp_done, 1)

        @block.tensor
        def _(pe):
            pe.wait_ge(chosen, 1)
            pe.wait_ge(pool_set, 8)
            b2 = both[:, :, :].rearrange("p g e -> p (g e)")
            pe.matmul(p_rank[:, :], upper[:, :], b2, start=True, stop=True)
            pe.matmul(p_total[:, :], ones[:, :], b2, start=True, stop=True).then_inc(ranked, 1)

        @block.vector
        def _(dve):
            n_steps = [0]

            def step(ins):
                ins.then_inc(dve_step, 1)
                n_steps[0] += 1
                dve.wait_ge(dve_step, n_steps[0])

            dve.wait_ge(pool_set, 8)
            src = logits[:, :, :]
            for c in range(2):
                step(dve.tensor_reduce(top[:, c, :], src, axis=AX_X, op=ALU.max))
                step(dve.tensor_tensor(eq[:, :, :], src, over_experts(top[:, c, :]), ALU.is_equal))
                step(dve.tensor_tensor(eq[:, :, :], eq[:, :, :], eid[:, :, :], ALU.mult))
                step(dve.tensor_reduce(idx[:, c, :], eq[:, :, :], axis=AX_X, op=ALU.min))
                step(dve.tensor_tensor(hot[:, c, :, :], eid[:, :, :], over_experts(idx[:, c, :]), ALU.is_equal))
                if c == 0:
                    step(dve.scalar_tensor_tensor(out=lg2[:, :, :], in0=hot[:, 0, :, :], scalar=-BIG,
                                                  in1=src, op0=ALU.mult, op1=ALU.add))
                    src = lg2[:, :, :]
            dve.tensor_tensor(both[:, :, :], hot[:, 0, :, :], hot[:, 1, :, :], ALU.add).then_inc(chosen, 1)
            dve.tensor_tensor(ediff[:, :], top[:, 1, :], top[:, 0, :], ALU.subtract).then_inc(chosen, 1)
            dve.wait_ge(exp_done, 1)
            step(dve.tensor_scalar(esum[:, :], ediff[:, :], 1.0, None, ALU.add))
            step(dve.reciprocal(weights[:, 0, :], esum[:, :]))
            step(dve.tensor_tensor(weights[:, 1, :], ediff[:, :], weights[:, 0, :], ALU.mult))
            dve.wait_ge(ranked, 1)
            step(dve.tensor_copy(total[:, :, :], p_total[:, :].rearrange("p (g e) -> p g e", e=E)))
            for e in range(E):
                scan = dve.tensor_tensor_scan(incl[:, :, e], onesg[:, :], total[:, :, e], 0.0, ALU.mult, ALU.add)
            step(scan)
            step(dve.tensor_tensor(over[:, :, :], incl[:, TILES - 1, :].rearrange("p (e a) -> p e a", a=1)
                                   .to_broadcast([128, E, NC_]), steps[:, :, :], ALU.is_gt))
            step(dve.tensor_reduce(ntile[:, :], over[:, :, :], axis=AX_X, op=ALU.add))
            step(dve.tensor_tensor_scan(tend[:, :], onesg[:, 0:E], ntile[:, :], 0.0, ALU.mult, ALU.add))
            step(dve.tensor_tensor(base[:, :], tend[:, :], ntile[:, :], ALU.subtract))
            step(dve.tensor_scalar(base[:, :], base[:, :], float(SLOT), None, ALU.mult))
            step(dve.tensor_tensor(incl[:, :, :], incl[:, :, :], total[:, :, :], ALU.subtract))
            step(dve.tensor_tensor(slot[:, :, :], p_rank[0:R, :].rearrange("p (g e) -> p g e", e=E),
                                   incl[0:R, :, :], ALU.add))
            step(dve.tensor_tensor(slot[:, :, :], slot[:, :, :], base[0:R, :].rearrange("p (a e) -> p a e", a=1)
                                   .to_broadcast([R, TILES, E]), ALU.add))
            for c in range(2):
                step(dve.tensor_tensor(picked[:, :, :], hot[:, c, :, :], slot[:, :, :], ALU.mult))
                step(dve.tensor_reduce(slotf[:, c, :], picked[:, :, :], axis=AX_X, op=ALU.add))
            dve.tensor_copy(sloti[:, :, :], slotf[:, :, :]).then_inc(slots_ready, 1)
            step(dve.tensor_tensor(past[:, :, :], tid[:, :, :], tend[0:1, :].rearrange("p (a e) -> p a e", a=1)
                                   .to_broadcast([1, SLOT_TILES, E]), ALU.is_ge))
            step(dve.tensor_reduce(texp[:, :], past[:, :, :], axis=AX_X, op=ALU.add))
            step(dve.tensor_scalar(expert_of[:, :], texp[:, :], float(E - 1), None, ALU.min))
            for g in range(TILES):
                for c in range(2):
                    n = 2 * (g % NB) + c
                    if g >= NB:
                        dve.wait_ge(sent[n], 16 * (g // NB))
                    dve.tensor_copy(ybuf[n][:, C:ROWW].bitcast(I32), dest[:, c, g:g + 1]).then_inc(dest_set, 1)


def split_biases(nc, b1, b2, b1s, b2s, ones3):
    with ExitStack() as ctx:
        m = Memory(nc, ctx, "bsp")
        WID = FF + C
        raw = m.sb("raw", [E, WID])
        part = [m.sb(f"part{n}", [E, WID], BF16) for n in range(3)]
        loaded, cut, rest, ones_set, moved = (m.sem(n) for n in ("loaded", "cut", "rest", "ones_set", "moved"))
        with nc.Block() as block:

            @block.sync
            def _(sp):
                sp.dma_start(raw[:, 0:FF], b1).then_inc(loaded, 16)
                sp.dma_start(raw[:, FF:WID], b2).then_inc(loaded, 16)
                sp.wait_ge(cut, 3)
                for n in range(3):
                    sp.dma_start(b1s[n:n + 1, :], part[n][:, 0:FF]).then_inc(moved, 16)
                    sp.dma_start(b2s[n:n + 1, :], part[n][:, FF:WID]).then_inc(moved, 16)
                sp.wait_ge(moved, 96)

            @block.vector
            def _(dve):
                dve.memset(ones3[:, :], 1.0).then_inc(ones_set, 1)
                dve.wait_ge(loaded, 32)
                for n in range(3):
                    dve.tensor_copy(part[n][:, :], raw[:, :]).then_inc(cut, 1)
                    dve.wait_ge(cut, n + 1)
                    if n < 2:
                        dve.tensor_tensor(raw[:, :], raw[:, :], part[n][:, :], ALU.subtract).then_inc(rest, 1)
                        dve.wait_ge(rest, n + 1)


def slot_tiles(eng, body):
    first, last = 2, 1 + (SLOT_TILES - 3) % 2
    for n in range(first):
        body((None, n, 2), n % 2, False)
    with eng.Fori(0, (SLOT_TILES - first - last) // 2) as i:
        for par in range(2):
            body((i, first + par, 2), par, False)
    for n in range(SLOT_TILES - last, SLOT_TILES):
        body((None, n, 2), n % 2, n == SLOT_TILES - 1)


def experts(nc, ident, w1, w2, b1s, b2s, ones3, expert_of, slots_dram, out_dram, weights_in, n_weights):
    FT = FF // 128
    HALF = FF // 2
    with ExitStack() as ctx:
        m = Memory(nc, ctx, "moe")
        xin = m.sb("xin", [SLOT, 2, ROWW])
        ids = m.sb("ids", [SLOT, 2], I32)
        xT = m.sb("xT", [128, 2, KC, SLOT])
        hid = m.sb("hid", [SLOT, 2, FF])
        hT = m.sb("hT", [128, 2, FT, SLOT])
        res = m.sb("res", [SLOT, 2, C])
        p_x = m.ps("p_x", [128, 512])
        p_h = [m.ps(f"p_h{n}", [128, 512]) for n in range(2)]
        p_t = [m.ps(f"p_t{n}", [128, 512]) for n in range(2)]
        p_y = [m.ps(f"p_y{n}", [128, 512]) for n in range(2)]
        xt_full, xt_ready, h_full, h_ready, ht_full, ht0_ready, ht1_ready, y_full, y_ready, ids_ready = (
            m.sem(n) for n in ("xt_full", "xt_ready", "h_full", "h_ready", "ht_full", "ht0_ready", "ht1_ready",
                               "y_full", "y_ready", "ids_ready"))
        x_in = [m.sem(f"x_in{n}") for n in range(2)]
        sent = [m.sem(f"sent{n}") for n in range(2)]
        x_rows = slots_dram.rearrange("(t p) c -> p t c", p=SLOT)
        block = ctx.enter_context(nc.Block())

        def at(b, width=1, per=1):
            v = count(b, per, 0)
            return slice(v, v + width) if isinstance(v, int) else bass.ds(v, width)

        @block.sync
        def _(sp):
            def load(t, par, is_last):
                wait_alone(sp, (xt_full, count(t, 1, -1)),
                               (ids_ready, count(t, 1, -1)))
                sp.dma_start(xin[:, par, :], x_rows[:, at(t), :]).then_inc(x_in[par], 16)

            slot_tiles(sp, load)

        @block.tensor
        def _(pe):
            def expert(t):
                return pe.value_load(expert_of[0:1, at(t)], min_val=0, max_val=E - 1)

            def transpose_x(t, par):
                wait(pe, x_in[par], lane_count(t, 16, 16))
                wait(pe, xt_ready, count(t, 1, 0))
                for k in range(KC):
                    mm = pe.transpose(p_x[:, k * 128:(k + 1) * 128], xin[:, par, k * 128:(k + 1) * 128], ident[:, :])
                mm.then_inc(xt_full, 1)

            def layer1(t, par):
                e = expert(t)
                wait(pe, xt_ready, count(t, 1, 1))
                for n in range(2):
                    wait(pe, h_ready, count(t, 2, n - 1))
                    for k in range(KC):
                        pe.matmul(p_h[n][:, :], xT[:, par, k, :], w1[:, k, bass.ds(e * FF + n * HALF, HALF)],
                                  start=(k == 0), stop=False)
                    pe.matmul(p_h[n][:, :], ones3[:, :], b1s[:, bass.ds(e * FF + n * HALF, HALF)],
                              start=False, stop=True).then_inc(h_full, 1)

            def transpose_h(t, par):
                for n, evac in enumerate((ht0_ready, ht1_ready)):
                    wait(pe, h_ready, count(t, 2, n + 1))
                    wait(pe, evac, count(t, 1, 0))
                    for f in range(FT // 2):
                        at_ = (n * FT // 2 + f) * 128
                        mm = pe.transpose(p_t[n][:, f * 128:(f + 1) * 128], hid[:, par, at_:at_ + 128], ident[:, :])
                    mm.then_inc(ht_full, 1)

            def layer2(t, par):
                e = expert(t)
                wait(pe, y_ready, count(t, 1, -1))
                for f in range(FT):
                    if f == 0:
                        wait(pe, ht0_ready, count(t, 1, 1))
                    if f == FT // 2:
                        wait(pe, ht1_ready, count(t, 1, 1))
                    pe.matmul(p_y[par][:, 0:C], hT[:, par, f, :], w2[:, bass.ds((e * FT + f) * C, C)],
                              start=(f == 0), stop=False)
                pe.matmul(p_y[par][:, 0:C], ones3[:, :], b2s[:, bass.ds(e * C, C)],
                          start=False, stop=True).then_inc(y_full, 1)

            def body(t, par, is_last):
                layer1(t, par)
                if not is_last:
                    transpose_x(after(t), 1 - par)
                if t[0] is not None or t[1] > 0:
                    layer2(before(t), 1 - par)
                transpose_h(t, par)

            pe.wait_ge(weights_in, n_weights)
            transpose_x((None, 0, 2), 0)
            slot_tiles(pe, body)
            layer2((None, SLOT_TILES - 1, 2), (SLOT_TILES - 1) % 2)

        @block.scalar
        def _(act):
            def body(t, par, is_last):
                for n in range(2):
                    wait(act, h_full, count(t, 2, n + 1))
                    wait(act, ht_full, count(t, 2, -2))
                    act.activation(hid[:, par, n * HALF:(n + 1) * HALF], p_h[n][:, :], ACT.Relu).then_inc(h_ready, 1)
                wait(act, ht_full, count(t, 2, 2))
                wait(act, y_full, count(t, 1, -1))
                act.activation(hT[:, par, FT // 2:FT, :].rearrange("p f s -> p (f s)"), p_t[1][:, :],
                               ACT.Copy).then_inc(ht1_ready, 1)

            slot_tiles(act, body)

        @block.vector
        def _(dve):
            def keep_ids(t, par):
                wait(dve, x_in[par], lane_count(t, 16, 16))
                wait(dve, sent[par], lane_count(t, 16, 0))
                dve.tensor_copy(ids[:, par:par + 1], xin[:, par, C:ROWW].bitcast(I32)).then_inc(ids_ready, 1)

            def x_back(t, par):
                wait(dve, xt_full, count(t, 1, 1))
                wait(dve, h_full, count(t, 2, -2))
                dve.tensor_copy(xT[:, par, :, :].rearrange("p k s -> p (k s)"), p_x[:, 0:C]).then_inc(xt_ready, 1)

            def result(t, par):
                wait(dve, y_full, count(t, 1, 1))
                wait(dve, sent[par], lane_count(t, 16, 0))
                dve.tensor_copy(res[:, par, :], p_y[par][:, 0:C]).then_inc(y_ready, 1)

            def body(t, par, is_last):
                if t[0] is not None or t[1] > 0:
                    result(before(t), 1 - par)
                if not is_last:
                    x_back(after(t), 1 - par)
                wait(dve, ht_full, count(t, 2, 1))
                wait(dve, y_full, count(t, 1, -1))
                dve.tensor_copy(hT[:, par, 0:FT // 2, :].rearrange("p f s -> p (f s)"), p_t[0][:, :]).then_inc(ht0_ready, 1)
                if not is_last:
                    keep_ids(after(t), 1 - par)

            keep_ids((None, 0, 2), 0)
            x_back((None, 0, 2), 0)
            slot_tiles(dve, body)
            result((None, SLOT_TILES - 1, 2), (SLOT_TILES - 1) % 2)

        @block.gpsimd
        def _(pool):
            def send(t, par, is_last):
                wait_alone(pool, (y_ready, count(t, 1, 1)),
                                 (ids_ready, count(t, 1, 1)))
                pool.indirect_dma_start(out=out_dram, out_offset=bass.IndirectOffsetOnAxis(
                    ap=ids[:, par:par + 1].bitcast(U32), axis=0), in_=res[:, par, :], in_offset=None
                    ).then_inc(sent[par], 16)

            slot_tiles(pool, send)
            for n in range(2):
                pool.wait_ge(sent[n], 16 * ((SLOT_TILES + 1 - n) // 2))


def combine(nc, neghalf, eps, weights, moe_dram, h_dram, out, g2, b2):
    with ExitStack() as ctx:
        m = Memory(nc, ctx, "comb")
        gain, shift = m.sb("gain", [R, C]), m.sb("shift", [R, C])
        WAYS = 4
        eo = m.sb("eo", [R, WAYS, 2, NT, C])
        hy = m.sb("hy", [R, WAYS, NT, C])
        acc = m.sb("acc", [R, WAYS, NT, C])
        st, mv = m.sb("st", [R, WAYS, NT, 6]), m.sb("mv", [R, WAYS, NT, 2])
        ve, rs = m.sb("ve", [R, WAYS, NT]), m.sb("rs", [R, WAYS, NT])
        consts_in, weighted, mixed, stats, aggr, eps_added, rstd, normed, gained, shifted, summed = (
            m.sem(n) for n in ("consts_in", "weighted", "mixed", "stats", "aggr", "eps_added", "rstd", "normed",
                               "gained", "shifted", "summed"))
        x_in = [m.sem(f"x_in{n}") for n in range(WAYS)]
        out_done = [m.sem(f"out_done{n}") for n in range(WAYS)]
        e_rows = moe_dram[0:2 * N_TOK, :].rearrange("(c g r) d -> r c g d", c=2, r=R)
        h_rows = h_dram.rearrange("(g r) c -> r g c", r=R)
        o_rows = out.rearrange("b t c -> (b t) c").rearrange("(g r) c -> r g c", r=R)
        block = ctx.enter_context(nc.Block())

        @block.sync
        def _(sp):
            for vec, sb in ((g2, gain), (b2, shift)):
                sp.dma_start(sb[:, :], vec.rearrange("(a c) -> a c", a=1).to_broadcast([R, C])).then_inc(consts_in, 16)

            def load(b, lane):
                wait_alone(sp, (summed, count(b, 1, 1 - WAYS)))
                for c in range(2):
                    sp.dma_start(eo[:, lane, c, :, :], e_rows[:, c, rows(b, 0, NT), :]).then_inc(x_in[lane], 16)
                sp.dma_start(hy[:, lane, :, :], h_rows[:, rows(b, 0, NT), :]).then_inc(x_in[lane], 16)

            skewed(sp, [(0, load)], ways=WAYS)

        @block.scalar
        def _(act):
            def store(b, lane):
                wait(act, summed, count(b, 1, 1))
                act.dma_start(o_rows[:, rows(b, 0, NT), :], acc[:, lane, :, :]).then_inc(out_done[lane], 16)

            skewed(act, [(0, store)], ways=WAYS)
            for n in range(WAYS):
                act.wait_ge(out_done[n], 16 * B // WAYS)

        @block.vector
        def _(dve):
            def mix(b, lane):
                wait(dve, x_in[lane], lane_count(b, 48, 48))
                wait(dve, out_done[lane], lane_count(b, 16, 0))
                for c, done in ((0, weighted), (1, mixed)):
                    for j in range(NT):
                        w = weights[:, c, row(b, j):row(b, j) + 1] if b[0] is None else weights[:, c, bass.ds(row(b, j), 1)]
                        if c == 0:
                            dve.tensor_scalar(acc[:, lane, j, :], eo[:, lane, 0, j, :], w, None, ALU.mult).then_inc(done, 1)
                        else:
                            wait(dve, weighted, count(b, NT, j + 1))
                            dve.scalar_tensor_tensor(out=acc[:, lane, j, :], in0=eo[:, lane, 1, j, :], scalar=w,
                                                     in1=acc[:, lane, j, :], op0=ALU.mult, op1=ALU.add).then_inc(done, 1)
                for j in range(NT):
                    wait_alone(dve, (mixed, count(b, NT, j + 1)))
                    dve.bn_stats(st[:, lane, j, :], acc[:, lane, j, :]).then_inc(stats, 1)
                for j in range(NT):
                    wait_alone(dve, (stats, count(b, NT, j + 1)))
                    dve.bn_aggr(mv[:, lane, j, :], st[:, lane, j, :]).then_inc(aggr, 1)

            def scale(b, lane):
                wait(dve, rstd, count(b, 1, 1))
                for j in range(NT):
                    dve.tensor_scalar(acc[:, lane, j, :], acc[:, lane, j, :], mv[:, lane, j, 0:1], rs[:, lane, j:j + 1],
                                      ALU.subtract, ALU.mult).then_inc(normed, 1)

            def residual(b, lane):
                wait(dve, shifted, count(b, 1, 1))
                dve.tensor_tensor(acc[:, lane, :, :], acc[:, lane, :, :], hy[:, lane, :, :], ALU.add).then_inc(summed, 1)

            skewed(dve, [(1, scale), (0, mix), (1, residual)], ways=WAYS)

        @block.gpsimd
        def _(pool):
            def over_tiles(v):
                return v[:, :].rearrange("p (a c) -> p a c", a=1).to_broadcast([R, NT, C])

            def root(b, lane):
                wait_alone(pool, (aggr, count(b, NT, NT)))
                pool.tensor_tensor(ve[:, lane, :], mv[:, lane, :, 1], eps[0:R, :], ALU.add).then_inc(eps_added, 1)
                wait_alone(pool, (eps_added, count(b, 1, 1)))
                pool.tensor_tensor(rs[:, lane, :], ve[:, lane, :], neghalf[0:R, :], ALU.pow).then_inc(rstd, 1)

            def affine(b, lane):
                ab = acc[:, lane, :, :]
                wait_alone(pool, (normed, count(b, NT, NT)))
                pool.tensor_tensor(ab, ab, over_tiles(gain), ALU.mult).then_inc(gained, 1)
                wait_alone(pool, (gained, count(b, 1, 1)))
                pool.tensor_tensor(ab, ab, over_tiles(shift), ALU.add).then_inc(shifted, 1)

            pool.wait_ge(consts_in, 32)
            skewed(pool, [(1, affine), (0, root)], ways=WAYS)


def mixture(nc, ctx, ident, neghalf, eps, logits, y_dram, h_dram, slots_dram, moe_dram, out, w1, b1, w2, b2, g2, be2):
    m = Memory(nc, ctx, "mix")
    FT = FF // 128
    weights = m.sb("weights", [R, 2, TILES])
    expert_of = m.sb("expert_of", [1, SLOT_TILES], I32)
    with ExitStack() as inner:
        m = Memory(nc, inner, "mixw")
        w1s = m.sb("w1s", [128, KC, E * FF])
        w2s = m.sb("w2s", [128, E * FT * C])
        b1s = m.sb("b1s", [3, E * FF], BF16)
        b2s = m.sb("b2s", [3, E * C], BF16)
        ones3 = m.sb("ones3", [3, SLOT], BF16)
        weights_in = m.sem("weights_in")

        def load_weights(sp):
            for e in range(E):
                sp.dma_start(w1s[:, :, e * FF:(e + 1) * FF], w1[e].rearrange("(k p) f -> p k f", p=128)
                             ).then_inc(weights_in, 16)
                sp.dma_start(w2s[:, e * FT * C:(e + 1) * FT * C].rearrange("p (f c) -> p f c", c=C),
                             w2[e].rearrange("(f p) c -> p f c", p=128)).then_inc(weights_in, 16)

        split_biases(nc, b1, b2, b1s, b2s, ones3)
        route(nc, logits, weights, expert_of, y_dram, slots_dram, load_weights)
        experts(nc, ident, w1s, w2s, b1s, b2s, ones3, expert_of, slots_dram, moe_dram, weights_in, 32 * E)
    combine(nc, neghalf, eps, weights, moe_dram, h_dram, out, g2, be2)


def build(nc, x, conv_w, conv_b, fuse_w, fuse_b, fin_w, fin_b, a_wqkv, a_bqkv, a_wproj, a_bproj, a_w1, a_b1, a_w2, a_b2,
          a_c, a_l, f_wq, f_wk, f_wv, f_gate, f_w1, f_b1, f_w2, f_b2, f_g1, f_be1, f_g2, f_be2, out):
    def dram(name, shape):
        return nc.dram_tensor(name, shape, F32, kind="Internal").ap()

    nd_dram = dram("nd_scratch", (128, CAUSAL))
    bias_dram = dram("bias_scratch", (H, 128, CAUSAL))
    y_dram = dram("y_scratch", (N_TOK, C))
    h_dram = dram("h_scratch", (N_TOK, C))
    slots_dram = dram("slots_scratch", (B * CLEAR * SLOT, ROWW))
    moe_dram = dram("moe_scratch", (N_RES, C))
    with ExitStack() as ctx:
        m = Memory(nc, ctx, "all")
        logits = m.sb("logits", [R, TILES, E])
        ident, neghalf, eps = constants(nc, m)
        with ExitStack() as held:
            hid = Memory(nc, held, "held").sb("hid", [R, TILES, C])
            tokenize(nc, ident, neghalf, eps, hid, nd_dram, bias_dram, x, conv_w, conv_b, fuse_w, fuse_b, fin_w, fin_b,
                     a_w1, a_b1, a_w2, a_b2, a_c, a_l)
            attend(nc, ident, neghalf, eps, hid, bias_dram, a_wqkv, a_bqkv, a_wproj, a_bproj)
            attend_in_ffn(nc, ident, neghalf, eps, hid, logits, y_dram, h_dram, slots_dram, f_wq, f_wk, f_wv, f_gate, f_g1, f_be1)
        mixture(nc, ctx, ident, neghalf, eps, logits, y_dram, h_dram, slots_dram, moe_dram, out,
                f_w1, f_b1, f_w2, f_b2, f_g2, f_be2)


_INS = ["x", "L0_tok_conv_w", "L0_tok_conv_b", "L0_tok_fusion_ln_w", "L0_tok_fusion_ln_b", "L0_tok_final_ln_w",
        "L0_tok_final_ln_b", "L0_attn_Wqkv", "L0_attn_bqkv", "L0_attn_Wproj", "L0_attn_bproj", "L0_attn_w1",
        "L0_attn_b1", "L0_attn_w2", "L0_attn_b2", "L0_attn_c_param", "L0_attn_L_multiplier", "L0_ffn_Wq", "L0_ffn_Wk",
        "L0_ffn_Wv", "L0_ffn_gate_W", "L0_ffn_W1", "L0_ffn_b1", "L0_ffn_W2", "L0_ffn_b2", "L0_ffn_ln1_g",
        "L0_ffn_ln1_b", "L0_ffn_ln2_g", "L0_ffn_ln2_b"]


def kernel(**inputs):
    import numpy as _np
    import concourse.bacc as _bacc
    from concourse import mybir as _mybir
    from concourse.bass_utils import run_bass_kernel_spmd as _run

    nc = _bacc.Bacc("TRN2", target_bir_lowering=False, num_devices=1)
    arrays, args = {}, []
    for name in _INS:
        a = _np.ascontiguousarray(inputs[name])
        if name in ("L0_attn_c_param", "L0_attn_L_multiplier"):
            a = a.reshape(1, 1)
        arrays[f"in_{name}"] = a
        args.append(nc.dram_tensor(f"in_{name}", a.shape, _mybir.dt.from_np(a.dtype), kind="ExternalInput").ap())
    args.append(nc.dram_tensor("out_0", (B, T, C), F32, kind="ExternalOutput").ap())
    build(nc, *args)
    r = _run(nc, [arrays], core_ids=[0])
    return r.results[0]["out_0"]
```

```python
import concourse.bass as bass
from concourse import mybir
from concourse.alu_op_type import AluOpType as ALU
from contextlib import ExitStack

F32 = mybir.dt.float32
BF16 = mybir.dt.bfloat16
I32 = mybir.dt.int32
U32 = mybir.dt.uint32
ACT = mybir.ActivationFunctionType
AX_X = mybir.AxisListType.X

B, T_IN, C = 16, 750, 256
T = T_IN // 2
R = 125
NT = T // R
TILES = B * NT
KC = C // 128
H = 16
HD = C // H
W = 32
E = 8
FF = 4 * C
SEG = [R * i * (i + 1) // 2 for i in range(NT + 1)]
CAUSAL = SEG[NT]
BIG = 3.0e38
NEG = -1.0e30
INIT_L, BIAS_EPS, LN_EPS = 512.0, 1e-6, 1e-5
Q_PARTS = [0, 0, 0, 1, 1, 2]
K_PARTS = [0, 1, 2, 0, 1, 0]
STACK = len(Q_PARTS) * HD


def count(b, per, c):
    i, off, ways = b
    const = off * per + c
    return const if i is None else i * (ways * per) + const


def wait(eng, sem, value):
    if not isinstance(value, int) or value > 0:
        eng.wait_ge(sem, value)


def wait_alone(eng, *pairs):
    pairs = [(sem, value) for sem, value in pairs if not isinstance(value, int) or value > 0]
    if any(not isinstance(value, int) for _, value in pairs):
        pairs = [(sem, value if isinstance(value, int) else eng.to_reg(value)) for sem, value in pairs]
        eng.wait_ge(pairs[0][0], 1)
    for sem, value in pairs:
        eng.wait_ge(sem, value)


def skewed(eng, steps, prelude=None, ways=2):
    def body(b, lane):
        for k, step in steps:
            if b[0] is not None or 0 <= b[1] - k < B:
                step(before(b, k), (lane - k) % ways)

    body((None, 0, ways), 0)
    if prelude:
        prelude()
    for n in range(1, 4):
        body((None, n, ways), n % ways)
    with eng.Fori(0, (B - 4) // ways) as i:
        for lane in range(ways):
            body((i, 4 + lane, ways), lane)
    for n in range(B, B + max(k for k, _ in steps)):
        body((None, n, ways), n % ways)


def lane_count(b, per, c):
    i, off, ways = b
    const = off // ways * per + c
    return const if i is None else i * per + const


def before(b, n=1):
    return (b[0], b[1] - n, b[2])


def after(b):
    return before(b, -1)


def rows(b, j=0, n=1):
    at = count(b, NT, j)
    return slice(at, at + n) if isinstance(at, int) else bass.ds(at, n)


def row(b, j):
    at = count(b, NT, j)
    return at


class Memory:

    def __init__(self, nc, ctx, tag):
        self.nc, self.ctx, self.tag, self.sems = nc, ctx, tag, []
        ctx.callback(self.close)

    def close(self):
        if self.sems:
            self.nc.clear_and_free_semaphores(self.sems)
            self.nc.all_engine_barrier()

    def sb(self, name, shape, dt=F32):
        return self.ctx.enter_context(self.nc.sbuf_tensor(f"{self.tag}_{name}", shape, dt))

    def ps(self, name, shape, dt=F32):
        return self.ctx.enter_context(self.nc.psum_tensor(f"{self.tag}_{name}", shape, dt))

    def sem(self, name):
        self.sems.append(self.nc.alloc_semaphore(f"{self.tag}_{name}"))
        return self.sems[-1]


def constants(nc, mem):
    ident = mem.sb("ident", [128, 128])
    neghalf = mem.sb("neghalf", [128, NT])
    eps = mem.sb("eps", [128, NT])
    set_done, sel_done = mem.sem("set_done"), mem.sem("sel_done")
    with nc.Block() as block:

        @block.gpsimd
        def _(pool):
            pool.memset(neghalf[:, :], -0.5)
            pool.memset(eps[:, :], LN_EPS)
            pool.memset(ident[:, :], 0.0).then_inc(set_done, 1)
            pool.wait_ge(set_done, 1)
            pool.affine_select(out=ident[:, :], in_=ident[:, :], compare_op=ALU.not_equal, fill=1.0,
                               base=0, pattern=[[-1, 128]], channel_multiplier=1).then_inc(sel_done, 1)
    return ident, neghalf, eps


def tokenize(nc, ident, neghalf, eps, hid, nd_dram, bias_dram, x, conv_w, conv_b, g_fuse, b_fuse, g_fin, b_fin,
             w1, b1, w2, b2, c_param, l_mult):
    G = 4
    PR = 128 // G
    STEP = PR // B
    CH = STEP * CAUSAL
    NMM = CH // 500
    with ExitStack() as ctx:
        m = Memory(nc, ctx, "tok")
        w_in = m.sb("w_in", [128, KC, C * 2])
        w_sb = m.sb("w", [128, 2 * KC, C])
        cb, gf, bf, gl, bl = (m.sb(n, [R, C]) for n in ("cb", "gf", "bf", "gl", "bl"))
        xin = m.sb("xin", [R, 2, NT, 2 * C])
        xT = m.sb("xT", [128, 2, 2 * KC, R])
        y = m.sb("y", [R, 2, NT, C])
        sk = m.sb("sk", [R, 2, NT, C])
        st = m.sb("st", [R, 2, NT, 6])
        mv = m.sb("mv", [R, 2, NT, 2])
        ve = m.sb("ve", [R, 2, NT])
        rs = m.sb("rs", [R, 2, NT])
        st2 = m.sb("st2", [R, 2, NT, 6])
        mv2 = m.sb("mv2", [R, 2, NT, 2])
        ve2 = m.sb("ve2", [R, 2, NT])
        rs2 = m.sb("rs2", [R, 2, NT])
        p_wt = m.ps("p_wt", [128, 512])
        p_xt = [m.ps(f"p_xt{n}", [128, 2 * KC, 128]) for n in range(2)]
        p_y = [m.ps(f"p_y{n}", [128, 512]) for n in range(2)]
        (consts_in, wt_full, wt_evac, xt_full, xt_ready, y_full, y_added, stats1, aggr1, eps1, rstd1,
         scaled1, gained1, fused, skip_sum, summed, gelu_done, stats2, aggr2, eps2, rstd2, scaled2, gained2,
         final) = (m.sem(n) for n in (
             "consts_in", "wt_full", "wt_evac", "xt_full", "xt_ready", "y_full", "y_added", "stats1", "aggr1",
             "eps1", "rstd1", "scaled1", "gained1", "fused", "skip_sum", "summed", "gelu_done", "stats2", "aggr2",
             "eps2", "rstd2", "scaled2", "gained2", "final"))
        x_in = [m.sem(f"x_in{n}") for n in range(2)]
        x_rows = x.rearrange("b t c -> (b t c)").rearrange("(g r c) -> r g c", r=R, c=2 * C)
        cpar = m.sb("cpar", [128, 1])
        lpar = m.sb("lpar", [128, 1])
        thr = m.sb("thr", [128, 1])
        rel = m.sb("rel", [128, CAUSAL])
        pos = m.sb("pos", [128, NT])
        nd = m.sb("nd", [128, CAUSAL])
        w1c = m.sb("w1c", [128, 1])
        b1c = m.sb("b1c", [128, 1])
        b2c = m.sb("b2c", [G * H, 1])
        w2g = m.sb("w2g", [128, G * H])
        nd_w = m.sb("nd_w", [128, 2, CH])
        hidden = m.sb("hidden", [128, 2, CH])
        outb = m.sb("outb", [G * H, 2, CH])
        pb = [m.ps(f"pb{n}", [G * H, 512]) for n in range(NMM)]
        (params_in, zeroed, w2_in, iota_done, rel_abs, rel_log, pos_max, pos_abs, pos_log, pos_eps, pos_inv, thr_done,
         nd_done, nd_out, hidden_done, mm_done, out_done) = (m.sem(n) for n in (
             "params_in", "zeroed", "w2_in", "iota_done", "rel_abs", "rel_log", "pos_max", "pos_abs", "pos_log",
             "pos_eps", "pos_inv", "thr_done", "nd_done", "nd_out", "hidden_done", "mm_done", "out_done"))
        nd_in = [m.sem(f"nd_in{n}") for n in range(2)]
        stored = [m.sem(f"stored{n}") for n in range(2)]

        block = ctx.enter_context(nc.Block())

        @block.sync
        def _(sp):
            def load(b, par):
                wait_alone(sp, (xt_full, count(b, NT, -NT)),
                               (skip_sum, count(b, 1, -1)))
                sp.dma_start(xin[:, par, :, :], x_rows[:, rows(b, 0, NT), :]).then_inc(x_in[par], 16)

            def chunk_load(c, par):
                wait_alone(sp, (hidden_done, count(c, 1, -1)))
                for g in range(G):
                    r0 = count(c, STEP, g * PR)
                    r_ = slice(r0, r0 + STEP) if isinstance(r0, int) else bass.ds(r0, STEP)
                    src = nd_dram[r_, :].rearrange("(a r) c -> a (r c)", a=1)
                    sp.dma_start(nd_w[g * W:(g + 1) * W, par, :], src.to_broadcast([W, CH])).then_inc(nd_in[par], 16)

            def chunk_store(c, par):
                wait_alone(sp, (out_done, count(c, NMM, NMM)))
                for g in range(G):
                    r0 = count(c, STEP, g * PR)
                    r_ = slice(r0, r0 + STEP) if isinstance(r0, int) else bass.ds(r0, STEP)
                    sp.dma_start(bias_dram[:, r_, :].rearrange("h r c -> h (r c)"), outb[g * H:(g + 1) * H, par, :]
                                 ).then_inc(stored[par], 16)

            def prelude():
                for g in range(G):
                    sp.dma_start(w1c[g * W:(g + 1) * W, :], w1.rearrange("a w -> w a")).then_inc(params_in, 16)
                    sp.dma_start(b1c[g * W:(g + 1) * W, :], b1.rearrange("(w a) -> w a", a=1)).then_inc(params_in, 16)
                    sp.dma_start(b2c[g * H:(g + 1) * H, :], b2.rearrange("(h a) -> h a", a=1)).then_inc(params_in, 16)
                sp.wait_ge(zeroed, 1)
                for g in range(G):
                    sp.dma_start(w2g[g * W:(g + 1) * W, g * H:(g + 1) * H], w2).then_inc(w2_in, 16)
                load((None, 1, 2), 1)
                sp.wait_ge(nd_done, NT)
                sp.dma_start(nd_dram, nd[:, :]).then_inc(nd_out, 16)
                sp.wait_ge(nd_out, 16)

            def load_later(b, par):
                if b[0] is not None or b[1] != 1:
                    load(b, par)

            sp.dma_start(w_in[:, :, :], conv_w.rearrange("(o p) c k -> p o (c k)", p=128)).then_inc(consts_in, 16)
            sp.dma_start(cpar[:, :], c_param.to_broadcast([128, 1])).then_inc(params_in, 16)
            sp.dma_start(lpar[:, :], l_mult.to_broadcast([128, 1])).then_inc(params_in, 16)
            for vec, sb in ((conv_b, cb), (g_fuse, gf), (b_fuse, bf), (g_fin, gl), (b_fin, bl)):
                sp.dma_start(sb[:, :], vec.rearrange("(a c) -> a c", a=1).to_broadcast([R, C])).then_inc(consts_in, 16)
            skewed(sp, [(0, load_later), (1, chunk_load), (3, chunk_store)], prelude)
            for n in range(2):
                sp.wait_ge(stored[n], 16 * G * B // 2)

        @block.tensor
        def _(pe):
            pe.wait_ge(consts_in, 96)
            w_ck = w_in[:, :, :].rearrange("p o (c k) -> p o c k", k=2)
            for k in range(2):
                for c in range(KC):
                    n = k * KC + c
                    if n:
                        pe.wait_ge(wt_evac, n)
                    for o in range(KC):
                        mm = pe.transpose(p_wt[:, o * 128:(o + 1) * 128],
                                          w_ck[:, o, c * 128:(c + 1) * 128, k], ident[:, :])
                    mm.then_inc(wt_full, 1)
            pe.wait_ge(wt_evac, 2 * KC)

            def convolve(b, par):
                wait(pe, x_in[par], lane_count(b, 16, 16))

                def transpose(j):
                    wait(pe, xt_ready, count(b, NT, j - 1))
                    for k in range(2 * KC):
                        mm = pe.transpose(p_xt[(par * NT + j) % 2][:, k, 0:R], xin[:, par, j, k * 128:(k + 1) * 128],
                                          ident[0:R, 0:R])
                    mm.then_inc(xt_full, 1)

                transpose(0)
                for j in range(NT):
                    q = (par * NT + j) % 2
                    if j + 1 < NT:
                        transpose(j + 1)
                    wait(pe, xt_ready, count(b, NT, j + 1))
                    wait(pe, y_added, count(b, NT, j - 1))
                    for k in range(2 * KC):
                        mm = pe.matmul(p_y[q][0:R, 0:C], xT[:, q, k, :], w_sb[:, k, :],
                                       start=(k == 0), stop=(k == 2 * KC - 1))
                    mm.then_inc(y_full, 1)

            def chunk_products(c, par):
                wait(pe, hidden_done, count(c, 1, 1))
                for k in range(NMM):
                    wait(pe, out_done, count(c, NMM, k + 1 - NMM))
                    pe.matmul(pb[k][:, 0:500], w2g[:, :], hidden[:, par, k * 500:(k + 1) * 500],
                              start=True, stop=True).then_inc(mm_done, 1)

            def prelude():
                pe.wait_ge(w2_in, 16 * G)

            skewed(pe, [(0, convolve), (1, chunk_products)], prelude)

        @block.scalar
        def _(act):
            for n in range(2 * KC):
                act.wait_ge(wt_full, n + 1)
                act.activation(w_sb[:, n, :], p_wt[:, 0:C], ACT.Copy).then_inc(wt_evac, 1)

            def frames_back(b, par):
                for j in range(NT):
                    q = (par * NT + j) % 2
                    wait(act, xt_full, count(b, NT, j + 1))
                    wait(act, y_full, count(b, NT, j - 1))
                    act.activation(xT[:, q, :, :], p_xt[q][:, :, 0:R], ACT.Copy).then_inc(xt_ready, 1)

            def gelu(b, par):
                wait(act, summed, count(b, 1, 1))
                act.activation(sk[:, par, :, :], sk[:, par, :, :], ACT.Gelu).then_inc(gelu_done, 1)

            def chunk_hidden(c, par):
                wait(act, nd_in[par], lane_count(c, 16 * G, 16 * G))
                wait(act, mm_done, count(c, NMM, -NMM))
                act.activation(hidden[:, par, :], nd_w[:, par, :], ACT.Relu, bias=b1c[:, 0:1],
                               scale=w1c[:, 0:1]).then_inc(hidden_done, 1)

            def chunk_out(c, par):
                wait(act, stored[par], lane_count(c, 16 * G, 0))
                for k in range(NMM):
                    wait(act, mm_done, count(c, NMM, k + 1))
                    act.activation(outb[:, par, k * 500:(k + 1) * 500], pb[k][:, 0:500], ACT.Identity,
                                   bias=b2c[:, 0:1]).then_inc(out_done, 1)

            def prelude():
                act.wait_ge(params_in, 16 * (2 + 3 * G))
                act.wait_ge(iota_done, 1)
                act.activation(thr[:, :], lpar[:, :], ACT.Abs, scale=INIT_L).then_inc(thr_done, 1)
                act.activation(rel[:, :], rel[:, :], ACT.Abs, scale=cpar[:, 0:1]).then_inc(rel_abs, 1)
                act.wait_ge(rel_abs, 1)
                act.activation(rel[:, :], rel[:, :], ACT.Ln, bias=1.0).then_inc(rel_log, 1)
                act.wait_ge(pos_max, 1)
                act.activation(pos[:, :], pos[:, :], ACT.Abs, scale=cpar[:, 0:1]).then_inc(pos_abs, 1)
                act.wait_ge(pos_abs, 1)
                act.activation(pos[:, :], pos[:, :], ACT.Ln, bias=1.0).then_inc(pos_log, 1)

            skewed(act, [(0, frames_back), (1, chunk_hidden), (2, gelu), (2, chunk_out)], prelude)

        @block.vector
        def _(dve):
            def norm1_stats(b, par):
                for j in range(NT):
                    q = (par * NT + j) % 2
                    wait(dve, y_full, count(b, NT, j + 1))
                    wait(dve, summed, count(b, 1, -1))
                    dve.tensor_tensor(y[:, par, j, :], p_y[q][0:R, 0:C], cb[:, :], ALU.add).then_inc(y_added, 1)
                for j in range(NT):
                    wait(dve, y_added, count(b, NT, j + 1))
                    dve.bn_stats(st[:, par, j, :], y[:, par, j, :]).then_inc(stats1, 1)
                for j in range(NT):
                    wait_alone(dve, (stats1, count(b, NT, j + 1)))
                    dve.bn_aggr(mv[:, par, j, :], st[:, par, j, :]).then_inc(aggr1, 1)

            def norm1_scale(b, par):
                wait(dve, rstd1, count(b, 1, 1))
                for j in range(NT):
                    dve.tensor_scalar(y[:, par, j, :], y[:, par, j, :], mv[:, par, j, 0:1], rs[:, par, j:j + 1],
                                      ALU.subtract, ALU.mult).then_inc(scaled1, 1)

            def frames_sum(b, par):
                wait(dve, x_in[par], lane_count(b, 16, 16))
                wait(dve, scaled2, count(b, NT, -NT))
                dve.tensor_tensor(sk[:, par, :, :], xin[:, par, :, 0:C], xin[:, par, :, C:2 * C],
                                  ALU.add).then_inc(skip_sum, 1)

            def add_skip(b, par):
                wait(dve, fused, count(b, 1, 1))
                wait(dve, skip_sum, count(b, 1, 1))
                dve.scalar_tensor_tensor(out=sk[:, par, :, :], in0=sk[:, par, :, :], scalar=0.5,
                                         in1=y[:, par, :, :], op0=ALU.mult, op1=ALU.add).then_inc(summed, 1)

            def norm2_stats(b, par):
                wait(dve, gelu_done, count(b, 1, 1))
                for j in range(NT):
                    dve.bn_stats(st2[:, par, j, :], sk[:, par, j, :]).then_inc(stats2, 1)
                for j in range(NT):
                    wait_alone(dve, (stats2, count(b, NT, j + 1)))
                    dve.bn_aggr(mv2[:, par, j, :], st2[:, par, j, :]).then_inc(aggr2, 1)

            def norm2_scale(b, par):
                wait(dve, rstd2, count(b, 1, 1))
                for j in range(NT):
                    dve.tensor_scalar(hid[:, row(b, j), :], sk[:, par, j, :], mv2[:, par, j, 0:1],
                                      rs2[:, par, j:j + 1], ALU.subtract, ALU.mult).then_inc(scaled2, 1)

            def prelude():
                dve.wait_ge(thr_done, 1)
                dve.tensor_scalar(pos[:, :], pos[:, :], thr[:, 0:1], None, ALU.max).then_inc(pos_max, 1)
                dve.wait_ge(pos_log, 1)
                dve.tensor_scalar(pos[:, :], pos[:, :], BIAS_EPS, None, ALU.add).then_inc(pos_eps, 1)
                dve.wait_ge(pos_eps, 1)
                dve.reciprocal(pos[:, :], pos[:, :]).then_inc(pos_inv, 1)
                dve.wait_ge(pos_inv, 1)
                dve.wait_ge(rel_log, 1)
                for i in range(NT):
                    dve.tensor_scalar(nd[:, SEG[i]:SEG[i + 1]], rel[:, SEG[i]:SEG[i + 1]], pos[:, i:i + 1], None,
                                      ALU.mult).then_inc(nd_done, 1)

            dve.wait_ge(consts_in, 96)
            skewed(dve, [(1, norm1_scale), (0, norm1_stats), (2, norm2_stats), (2, norm2_scale), (0, frames_sum),
                         (1, add_skip)], prelude)

        @block.gpsimd
        def _(pool):
            def over_tiles(v):
                return v[:, :].rearrange("p (a c) -> p a c", a=1).to_broadcast([R, NT, C])

            def root(mv, ve, rs, aggr, eps_done, rstd_done):
                def step(b, par):
                    wait_alone(pool, (aggr, count(b, NT, NT)))
                    pool.tensor_tensor(ve[:, par, :], mv[:, par, :, 1], eps[0:R, :], ALU.add).then_inc(eps_done, 1)
                    wait_alone(pool, (eps_done, count(b, 1, 1)))
                    pool.tensor_tensor(rs[:, par, :], ve[:, par, :], neghalf[0:R, :], ALU.pow).then_inc(rstd_done, 1)
                return step

            def norm1_gain(b, par):
                wait_alone(pool, (scaled1, count(b, NT, NT)))
                pool.tensor_tensor(y[:, par, :, :], y[:, par, :, :], over_tiles(gf), ALU.mult).then_inc(gained1, 1)
                wait_alone(pool, (gained1, count(b, 1, 1)))
                pool.tensor_tensor(y[:, par, :, :], y[:, par, :, :], over_tiles(bf), ALU.add).then_inc(fused, 1)

            def norm2_gain(b, par):
                wait_alone(pool, (scaled2, count(b, NT, NT)))
                hb = hid[:, rows(b, 0, NT), :]
                pool.tensor_tensor(hb, hb, over_tiles(gl), ALU.mult).then_inc(gained2, 1)
                wait_alone(pool, (gained2, count(b, 1, 1)))
                pool.tensor_tensor(hb, hb, over_tiles(bl), ALU.add).then_inc(final, 1)

            for i in range(NT):
                pool.iota(rel[:, SEG[i]:SEG[i + 1]], [[-1, R * (i + 1)]], base=R * i, channel_multiplier=1,
                          allow_small_or_imprecise_dtypes=True)
                pool.iota(pos[:, i:i + 1], [[0, 1]], base=R * i, channel_multiplier=1,
                          allow_small_or_imprecise_dtypes=True)
            pool.memset(w2g[:, :], 0.0).then_inc(zeroed, 1)
            pool.wait_ge(zeroed, 1)
            pool.nop().then_inc(iota_done, 1)
            pool.wait_ge(consts_in, 96)
            skewed(pool, [(1, norm1_gain), (0, root(mv, ve, rs, aggr1, eps1, rstd1)),
                          (2, root(mv2, ve2, rs2, aggr2, eps2, rstd2)), (2, norm2_gain)])


def attention(nc, ident, neghalf, eps, hid, first, wq_in, wk_in, wv_in, scale, bias, tail):
    tag = "a" if first else "f"
    with ExitStack() as ctx:
        m = Memory(nc, ctx, tag)
        XW = NT * R
        wqk = m.sb("wqk", [128, KC, 2 * C])
        wv = m.sb("wv", [128, KC, C])
        wo = m.sb("wo", [128, KC, C]) if first else None
        wg = None if first else m.sb("wg", [128, KC, E])
        qkb = m.sb("qkb", [128, 2 * KC])
        vb = m.sb("vb", [R, C])
        ob = m.sb("ob", [R, C])
        ob2 = None if first else m.sb("ob2", [R, C])
        st = m.sb("st", [R, NT, 6])
        mv = m.sb("mv", [R, NT, 2])
        ve = m.sb("ve", [R, NT])
        rs = m.sb("rs", [R, NT])
        ms = m.sb("ms", [R, NT])
        zeros = m.sb("zeros", [R, NT])
        xn = m.sb("xn", [R, NT, C])
        xr = None if first else m.sb("xr", [R, 2, NT, C])
        xT = m.sb("xT", [128, KC, XW])
        f = m.sb("f", [128, 2, XW])
        w_stage = [v[:, :, :].rearrange("p a t -> p (a t)") for v in (f, xT)]
        part = [m.sb(f"part{n}", [128, 2 * KC, XW], BF16) for n in range(3)]
        qs = [m.sb(f"qs{n}", [STACK, H, XW], BF16) for n in range(2)]
        ks = [m.sb(f"ks{n}", [STACK, H, XW], BF16) for n in range(2)]
        VW = HD + 1
        OR = 32
        vx = [m.sb(f"vx{n}", [R, NT, H, VW]) for n in range(2)]
        sc = m.sb("sc", [R, 2, CAUSAL])
        nmx = m.sb("nmx", [R, 2, NT])
        pr = m.sb("pr", [R, 2, CAUSAL])
        pT = m.sb("pT", [R, 2, CAUSAL])
        oT = m.sb("oT", [128, XW])
        rden = m.sb("rden", [R, NT, 4])
        y = m.sb("y", [R, 2, NT, C])
        yT = xT if first else m.sb("yT", [128, KC, XW])
        p_s = [[m.ps(f"p_s{n}{u}", [128, 512]) for u in range(2)] for n in range(2)]
        p_t = [m.ps(f"p_t{u}", [128, 512]) for u in range(2)]
        p_o = m.ps("p_o", [128, 512])
        p_m = m.ps("p_m", [128, 512])
        S = {n: m.sem(n) for n in (
            "consts_in", "ones_set", "gaps_zeroed", "table_ready", "zeros_set", "mean_scaled", "shift_made", "no_bias", "wqk_ready", "bias_scaled", "stats", "aggr", "eps_added", "rstd", "normed", "xt_full", "xt_ready",
            "qk_full", "f_ready", "part0", "residual1", "part1", "part2", "v_full", "v_ready", "scored", "biased",
            "exped", "pt_full", "ptx_ready", "pty_ready", "weighed", "o_evac", "o_back", "recip", "y_ready",
            "yt_full", "yt_ready", "out_full", "out_added", "tail_done")}
        S2 = {} if first else {n: m.sem(n) for n in ("stats_y", "aggr_y", "eps_y", "rstd_y", "normed_y", "gained",
                                                     "shifted", "summed", "resid_added")}
        stacked = [m.sem(f"stacked{n}") for n in range(2)]
        table_in = [m.sem(f"table_in{n}") for n in range(4)] if first else None
        y_out = [m.sem(f"y_out{n}") for n in range(2)]
        h_out = [m.sem(f"h_out{n}") for n in range(2)]
        if not first:
            y_st, y_mv = m.sb("y_st", [R, NT, 6]), m.sb("y_mv", [R, NT, 2])
            y_ve, y_rs = m.sb("y_ve", [R, NT]), m.sb("y_rs", [R, NT])

        N_CONST = tail["n_const"]
        PAIRS = [range(j, min(j + 2, NT)) for j in range(0, NT, 2)]
        NP = len(PAIRS)
        block = ctx.enter_context(nc.Block())

        @block.sync
        def _(sp):
            for k in range(KC):
                for n, w_ in enumerate((wq_in, wk_in, wv_in)):
                    dst = wv[:, k, :] if n == 2 else w_stage[k][:, n * C:(n + 1) * C]
                    if not first:
                        dst = dst.rearrange("p (h d) -> p h d", d=HD)
                    sp.dma_start(dst, w_(k)).then_inc(S["consts_in"], 16)
            tail["load"](sp, qkb, vb, ob, ob2, wo, wg, S["consts_in"])
            if first:
                tail["load_table"](sp, table_in)

            def stacks(b, par):
                for blk in range(2 * KC):
                    n = blk % 2
                    wait_alone(sp, (S["part2"], count(b, 2 * KC, blk + 1)),
                                   (S["scored"], count(b, 2 * H, -2 * H)))
                    to, parts = (qs, Q_PARTS) if blk < KC else (ks, K_PARTS)
                    at = blk % KC * (H // KC)
                    for r, c in enumerate(parts):
                        sp.dma_start(to[par][r * HD:(r + 1) * HD, at:at + H // KC, :],
                                     part[c][:, blk, :]).then_inc(stacked[n], 16)

            def body(b, par, prologue, epilogue):
                if prologue:
                    stacks(after(b), 1 - par)
                if epilogue and not first:
                    pb = before(b)
                    wait_alone(sp, (S2["summed"], count(pb, 1, 1)))
                    sp.dma_start(tail["y_rows"][:, rows(pb, 0, NT), :], y[:, 1 - par, :, :]).then_inc(y_out[1 - par], 16)
                    wait_alone(sp, (S2["resid_added"], count(pb, 1, 1)))
                    sp.dma_start(tail["h_rows"][:, rows(pb, 0, NT), :], hid[:, rows(pb, 0, NT), :]
                                 ).then_inc(h_out[1 - par], 16)

            run_batches(sp, lambda: stacks((None, 0, 2), 0), body)
            if not first:
                sp.wait_ge(S2["summed"], B)
                sp.dma_start(tail["y_rows"][:, (B - 1) * NT:B * NT, :], y[:, 1, :, :]).then_inc(y_out[1], 16)
                sp.wait_ge(S2["resid_added"], B)
                sp.dma_start(tail["h_rows"][:, (B - 1) * NT:B * NT, :],
                             hid[:, (B - 1) * NT:B * NT, :]).then_inc(h_out[1], 16)
                for n in range(2):
                    sp.wait_ge(y_out[n], 16 * B // 2)
                    sp.wait_ge(h_out[n], 16 * B // 2)

        @block.tensor
        def _(pe):
            shared = {}

            def take_bank():
                if "by" in shared:
                    wait(pe, *shared["by"])

            def x_transpose(b, par, k):
                take_bank()
                wait(pe, S["normed"], count(b, NT, NT))
                wait(pe, S["v_full"], count(b, NP, 0))
                for j in range(NT):
                    mm = pe.transpose(p_m[:, j * R:(j + 1) * R], xn[:, j, k * 128:(k + 1) * 128], ident[0:R, 0:R])
                mm.then_inc(S["xt_full"], 1)
                shared["by"] = (S["xt_ready"], count(b, KC, k + 1))

            def qk_project(b, par, blk):
                take_bank()
                wait(pe, S["xt_ready"], count(b, KC, KC))
                for k in range(KC):
                    mm = pe.matmul(p_m[:, 0:XW], wqk[:, k, blk * 128:(blk + 1) * 128], xT[:, k, :],
                                   start=(k == 0), stop=(k == KC - 1))
                mm.then_inc(S["qk_full"], 1)
                shared["by"] = (S["f_ready"], count(b, 2 * KC, blk + 1))

            def v_project(b, par, p):
                take_bank()
                for n, j in enumerate(PAIRS[p]):
                    for k in range(KC):
                        mm = pe.matmul(p_m[0:R, n * C:(n + 1) * C], xT[:, k, j * R:(j + 1) * R], wv[:, k, :],
                                       start=(k == 0), stop=(k == KC - 1))
                mm.then_inc(S["v_full"], 1)
                shared["by"] = (S["v_ready"], count(b, NP, p + 1))

            def score(b, par, h):
                if h == 0:
                    for n in range(2):
                        wait(pe, stacked[n], count(b, 16 * KC * STACK // HD, 16 * KC * STACK // HD))
                for u, tiles in enumerate(((0, 1), (2,))):
                    wait(pe, S["biased"], count(b, H * NT, NT * (h - 2) + tiles[-1] + 1))
                    for i in tiles:
                        o = SEG[i] if u == 0 else 0
                        mm = pe.matmul(p_s[h % 2][u][0:R, o:o + R * (i + 1)], qs[par][:, h, i * R:(i + 1) * R],
                                       ks[par][:, h, 0:R * (i + 1)], start=True, stop=True)
                    mm.then_inc(S["scored"], 1)

            def transpose_probs(b, par, h):
                if h < 0:
                    b, par, h = before(b), 1 - par, h + H
                    if b[0] is None and b[1] < 0:
                        return
                wait(pe, S["exped"], count(b, H * NT, NT * h + NT))
                wait(pe, S["ptx_ready"], count(b, H, h))
                for i in range(NT):
                    mm = pe.transpose(p_t[0][0:R, i * R:(i + 1) * R], pr[:, h % 2, SEG[i]:SEG[i] + R], ident[0:R, 0:R])
                mm.then_inc(S["pt_full"], 1)
                wait(pe, S["pty_ready"], count(b, H, h))
                for o, (i, s) in enumerate(((1, 1), (2, 1), (2, 2))):
                    mm = pe.transpose(p_t[1][0:R, o * R:(o + 1) * R], pr[:, h % 2, SEG[i] + s * R:SEG[i] + (s + 1) * R],
                                      ident[0:R, 0:R])
                mm.then_inc(S["pt_full"], 1)

            def weigh(b, par, h):
                if h < 0:
                    b, par, h = before(b), 1 - par, h + H
                    if b[0] is None and b[1] < 0:
                        return
                q = h % 4
                if q == 0:
                    wait(pe, S["o_evac"], count(b, H // 4, h // 4))
                if h == 0:
                    wait(pe, S["v_ready"], count(b, NP, NP))
                wait(pe, S["ptx_ready"], count(b, H, h + 1))
                wait(pe, S["pty_ready"], count(b, H, h + 1))
                for s in range(NT):
                    at = (0, XW, 2 * XW - R)[s]
                    mm = pe.matmul(p_o[q * OR:q * OR + VW, s * R:XW], vx[par][:, s, h, :],
                                   pT[:, h % 2, at:at + XW - s * R], start=(s == 0), stop=(s == NT - 1))
                mm.then_inc(S["weighed"], 1)

            def outputs_back(b, par, g):
                take_bank()
                wait(pe, S["o_evac"], count(b, H // 4, g + 1))
                for j in range(NT):
                    mm = pe.transpose(p_m[0:R, j * 128:(j + 1) * 128], oT[:, j * R:(j + 1) * R], ident[:, :])
                mm.then_inc(S["o_back"], 1)
                shared["by"] = (S["y_ready"], count(b, H // 4, g + 1))

            def y_transpose(b, par, k):
                take_bank()
                if first:
                    wait(pe, S["y_ready"], count(b, H // 4, H // 4))
                else:
                    wait(pe, S2["summed"], count(b, 1, 1))
                for j in range(NT):
                    mm = pe.transpose(p_m[:, j * R:(j + 1) * R], y[:, par, j, k * 128:(k + 1) * 128], ident[0:R, 0:R])
                mm.then_inc(S["yt_full"], 1)
                shared["by"] = (S["yt_ready"], count(b, KC, k + 1))

            def out_project(b, par, p):
                take_bank()
                wait(pe, S["yt_ready"], count(b, KC, KC))
                for n, j in enumerate(PAIRS[p]):
                    for k in range(KC):
                        mm = pe.matmul(p_m[0:R, n * C:(n + 1) * C], yT[:, k, j * R:(j + 1) * R], wo[:, k, :],
                                       start=(k == 0), stop=(k == KC - 1))
                mm.then_inc(S["out_full"], 1)
                shared["by"] = (S["out_added"], count(b, NP, p + 1))

            def gate(b, par, _):
                take_bank()
                wait(pe, S["yt_ready"], count(b, KC, KC))
                for j in range(NT):
                    for k in range(KC):
                        mm = pe.matmul(p_m[0:R, j * E:(j + 1) * E], yT[:, k, j * R:(j + 1) * R], wg[:, k, :],
                                       start=(k == 0), stop=(k == KC - 1))
                mm.then_inc(S["out_full"], 1)
                shared["by"] = (S["out_added"], count(b, 1, 1))

            def own(n):
                return {6: [(outputs_back, 0)], 10: [(outputs_back, 1)], 14: [(outputs_back, 2)]}.get(n, [])

            pro = {0: [(x_transpose, 0)], 1: [(x_transpose, 1)], 3: [(qk_project, 0)], 4: [(qk_project, 1)],
                   5: [(v_project, 0)], 7: [(qk_project, 2)], 8: [(qk_project, 3)], 9: [(v_project, 1)]}
            epi = {11: [(y_transpose, 0)], 12: [(y_transpose, 1)], 13: [(out_project if first else gate, 0)]}
            if first:
                epi[15] = [(out_project, 1)]

            def body(b, par, prologue, epilogue):
                if b[0] is not None:
                    shared["by"] = (S["out_added"], count(before(b, 2), NP if first else 1, NP if first else 1))
                for n in range(H):
                    transpose_probs(b, par, n - 1)
                    if n + 1 < H:
                        score(b, par, n + 1)
                    elif prologue:
                        score(after(b), 1 - par, 0)
                    weigh(b, par, n - 2)
                    if epilogue:
                        if n == 2:
                            outputs_back(before(b), 1 - par, 3)
                        for step, arg in epi.get(n, []):
                            step(before(b), 1 - par, arg)
                    for step, arg in own(n):
                        step(b, par, arg)
                    if prologue:
                        for step, arg in pro.get(n, []):
                            step(after(b), 1 - par, arg)

            def start():
                x_transpose((None, 0, 2), 0, 0)
                pe.wait_ge(S["consts_in"], 16 * N_CONST)
                pe.wait_ge(S["wqk_ready"], 2 * KC * KC)
                pe.wait_ge(S["gaps_zeroed"], 1)
                for n in range(1, H):
                    for step, arg in pro.get(n, []):
                        step((None, 0, 2), 0, arg)
                score((None, 0, 2), 0, 0)

            run_batches(pe, start, body)
            b, par = (None, B - 1, 2), 1
            transpose_probs(b, par, H - 1)
            weigh(b, par, H - 2)
            weigh(b, par, H - 1)
            outputs_back(b, par, 3)
            for n in range(H):
                for step, arg in epi.get(n, []):
                    step(b, par, arg)

        @block.vector
        def _(dve):
            def norm_stats(b, par, _):
                for j in range(NT):
                    dve.bn_stats(st[:, j, :], hid[:, row(b, j), :]).then_inc(S["stats"], 1)
                for j in range(NT):
                    wait_alone(dve, (S["stats"], count(b, NT, j + 1)),
                                    (S["shift_made"], count(b, 1, 0)))
                    dve.bn_aggr(mv[:, j, :], st[:, j, :]).then_inc(S["aggr"], 1)

            def first_part(b, par, blk):
                n = blk % 2
                wait(dve, S["f_ready"], count(b, 2 * KC, blk + 1))
                free_part(dve, b, blk)
                dve.tensor_copy(part[0][:, blk, :], f[:, n, :]).then_inc(S["part0"], 1)

            def second_part(b, par, blk):
                n = blk % 2
                wait(dve, S["residual1"], count(b, 2 * KC, blk + 1))
                free_part(dve, b, blk)
                dve.tensor_copy(part[1][:, blk, :], f[:, n, :]).then_inc(S["part1"], 1)

            def values(b, par, p):
                wait(dve, S["v_full"], count(b, NP, p + 1))
                wait(dve, S["weighed"], count(b, H, -H))
                k = len(PAIRS[p])
                dve.tensor_tensor(vx[par][:, PAIRS[p][0]:PAIRS[p][0] + k, :, 0:HD],
                                  p_m[0:R, 0:k * C].rearrange("p (j h d) -> p j h d", h=H, d=HD),
                                  vb[:, :].rearrange("p (a h d) -> p a h d", a=1, d=HD).to_broadcast([R, k, H, HD]),
                                  ALU.add).then_inc(S["v_ready"], 1)

            def add_bias(b, par, h):
                for i in range(NT):
                    u, o = (0, SEG[i]) if i < 2 else (1, 0)
                    if i != 1:
                        wait_alone(dve, (S["scored"], count(b, 2 * H, 2 * h + u + 1)))
                    if i == 0:
                        wait_alone(dve, (S["exped"], count(b, NT * H, NT * (h - 1))))
                    dve.tensor_tensor_reduce(out=sc[:, h % 2, SEG[i]:SEG[i + 1]],
                                             in0=p_s[h % 2][u][0:R, o:o + R * (i + 1)], in1=bias(h, i),
                                             scale=-1.0, scalar=BIG, op0=ALU.add, op1=ALU.min,
                                             accum_out=nmx[:, h % 2, i:i + 1]).then_inc(S["biased"], 1)

            def probs_back(b, par, h):
                if h < 0:
                    b, par, h = before(b), 1 - par, h + H
                    if b[0] is None and b[1] < 0:
                        return
                wait(dve, S["pt_full"], count(b, 2 * H, 2 * h + 1))
                wait(dve, S["weighed"], count(b, H, h - 1))
                dve.tensor_copy(pT[:, h % 2, 0:XW], p_t[0][0:R, 0:XW]).then_inc(S["ptx_ready"], 1)

            def normalize(b, par, g):
                wait(dve, S["o_back"], count(b, H // 4, g + 1))
                o = p_m[0:R, 0:NT * 128].rearrange("p (j q v) -> p j q v", j=NT, q=4)
                wait(dve, S["y_ready"], count(b, H // 4, g))
                dve.reciprocal(rden[:, :, :], o[:, :, :, HD]).then_inc(S["recip"], 1)
                wait(dve, S["recip"], count(b, H // 4, g + 1))
                if first:
                    wait(dve, S["yt_full"], count(b, KC, -KC))
                else:
                    wait(dve, S["yt_full"], count(b, KC, -KC))
                    wait(dve, S2["resid_added"], count(b, 1, -1))
                    wait(dve, y_out[par], lane_count(b, 16, 0))
                dst = y[:, par, :, g * 4 * HD:(g + 1) * 4 * HD].rearrange("p j (q d) -> p j q d", q=4)
                dve.tensor_tensor(dst, o[:, :, :, 0:HD],
                                  rden[:, :, :].rearrange("p j (q a) -> p j q a", a=1).to_broadcast([R, NT, 4, HD]),
                                  ALU.mult).then_inc(S["y_ready"], 1)

            def add_output(b, par, p):
                k = len(PAIRS[p])
                hb = hid[:, rows(b, PAIRS[p][0], k), :]
                wait(dve, S["out_full"], count(b, NP, p + 1))
                dve.tensor_tensor(hb, p_m[0:R, 0:k * C].rearrange("p (j c) -> p j c", c=C), hb,
                                  ALU.add).then_inc(S["out_added"], 1)

            def y_stats(b, par, _):
                wait(dve, S["y_ready"], count(b, H // 4, H // 4))
                for j in range(NT):
                    dve.bn_stats(y_st[:, j, :], y[:, par, j, :]).then_inc(S2["stats_y"], 1)
                for j in range(NT):
                    wait_alone(dve, (S2["stats_y"], count(b, NT, j + 1)))
                    dve.bn_aggr(y_mv[:, j, :], y_st[:, j, :]).then_inc(S2["aggr_y"], 1)

            def y_scale(b, par, _):
                wait(dve, S2["rstd_y"], count(b, 1, 1))
                for j in range(NT):
                    dve.tensor_scalar(y[:, par, j, :], y[:, par, j, :], y_mv[:, j, 0:1], y_rs[:, j:j + 1],
                                      ALU.subtract, ALU.mult).then_inc(S2["normed_y"], 1)

            def keep_logits(b, par, _):
                wait(dve, S["out_full"], count(b, 1, 1))
                dve.tensor_copy(tail["logits"][:, rows(b, 0, NT), :],
                                p_m[0:R, 0:NT * E].rearrange("p (j e) -> p j e", e=E)).then_inc(S["out_added"], 1)

            epi_mid = {3: [(normalize, 3)], 14: [(add_output if first else keep_logits, 0)]}
            epi = {} if first else {4: [(y_stats, 0)], 6: [(y_scale, 0)]}
            own = {7: [(normalize, 0)], 11: [(normalize, 1)], 15: [(normalize, 2)]}
            pro_mid = {6: [(values, 0)], 10: [(values, 1)]}
            pro = {4: [(first_part, 0)], 5: [(second_part, 0), (first_part, 1)], 6: [(second_part, 1)],
                   8: [(first_part, 2)], 9: [(second_part, 2), (first_part, 3)], 10: [(second_part, 3)]}
            norm_ahead = {13: [(norm_stats, 0)]}

            def body(b, par, prologue, epilogue):
                nxt, last = after(b), before(b)

                def steps(table, at, p):
                    for step, arg in table:
                        step(at, p, arg)

                for n in range(H):
                    add_bias(b, par, n)
                    if first and n == 0 and (b[0] is not None or b[1] >= 2):
                        add_output(before(b, 2), par, 1)
                    if prologue:
                        steps(pro_mid.get(n, []), nxt, 1 - par)
                    if epilogue:
                        steps(epi_mid.get(n, []), last, 1 - par)
                    steps(own.get(n, []), b, par)
                    if b[0] is not None or b[1] < B - 2:
                        steps(norm_ahead.get(n, []), after(nxt), par)
                    probs_back(b, par, n - 1)
                    if epilogue:
                        steps(epi.get(n, []), last, 1 - par)
                    if prologue:
                        steps(pro.get(n, []), nxt, 1 - par)

            def start():
                norm_stats((None, 0, 2), 0, 0)
                dve.wait_ge(S["consts_in"], 16 * N_CONST)
                for k in range(KC):
                    for n in range(2 * KC):
                        dve.tensor_copy(wqk[:, k, n * 128:(n + 1) * 128].rearrange("p (d h) -> p d h", d=HD),
                                        w_stage[k][:, n * 128:(n + 1) * 128].rearrange("p (h d) -> p d h", d=HD)
                                        ).then_inc(S["wqk_ready"], 1)
                if not first:
                    dve.wait_ge(S["no_bias"], 2)
                dve.tensor_scalar(qkb[:, 0:KC], qkb[:, 0:KC], scale, None, ALU.mult).then_inc(S["bias_scaled"], 1)
                dve.memset(p_o[:, :], 0.0).then_inc(S["gaps_zeroed"], 1)
                dve.wait_ge(S["ones_set"], 2)
                for n in range(H):
                    for step, arg in pro_mid.get(n, []) + pro.get(n, []):
                        step((None, 0, 2), 0, arg)
                norm_stats((None, 1, 2), 1, 0)
                if first:
                    dve.wait_ge(S["table_ready"], 4 * NT)

            def free_part(eng, b, blk):
                wait(eng, stacked[blk % 2], count(b, 16 * KC * STACK // HD, 0))

            run_batches(dve, start, body)
            b, par = (None, B - 1, 2), 1
            probs_back(b, par, H - 1)
            if first:
                add_output(before(b), 1 - par, 1)
            for n in range(H):
                for step, arg in epi_mid.get(n, []) + epi.get(n, []):
                    step(b, par, arg)
            if first:
                add_output(b, par, 1)

        @block.scalar
        def _(act):
            def norm_scale(b, par, _):
                wait(act, S["shift_made"], count(b, 1, 1))
                wait(act, S["xt_full"], count(b, KC, 0))
                if not first:
                    wait(act, S2["shifted"], count(b, 1, 0))
                for j in range(NT):
                    hb = hid[:, row(b, j), :]
                    act.activation(xn[:, j, :], hb, ACT.Identity, bias=ms[:, j:j + 1], scale=rs[:, j:j + 1]
                                   ).then_inc(S["normed"], 1)

            def x_back(b, par, k):
                wait(act, S["xt_full"], count(b, KC, k + 1))
                if first:
                    wait(act, S["out_full"], count(b, NP, -2 * NP))
                wait(act, S["v_full"], count(b, NP, 0))
                act.activation(xT[:, k, :], p_m[:, 0:XW], ACT.Copy).then_inc(S["xt_ready"], 1)

            def qk_back(b, par, blk):
                n = blk % 2
                wait(act, S["qk_full"], count(b, 2 * KC, blk + 1))
                wait(act, S["part2"], count(b, 2 * KC, blk - 1))
                act.activation(f[:, n, :], p_m[:, 0:XW], ACT.Identity, bias=qkb[:, blk:blk + 1],
                               scale=(scale if blk < KC else 1.0)).then_inc(S["f_ready"], 1)

            def exponentiate(b, par, h):
                for i in range(NT):
                    wait(act, S["biased"], count(b, NT * H, NT * h + i + 1))
                    if i == 0:
                        wait(act, S["pt_full"], count(b, 2 * H, 2 * (h - 1)))
                    act.activation(pr[:, h % 2, SEG[i]:SEG[i + 1]], sc[:, h % 2, SEG[i]:SEG[i + 1]], ACT.Exp,
                                   bias=nmx[:, h % 2, i:i + 1], scale=-1.0).then_inc(S["exped"], 1)

            def probs_back(b, par, h):
                if h < 0:
                    b, par, h = before(b), 1 - par, h + H
                    if b[0] is None and b[1] < 0:
                        return
                wait(act, S["pt_full"], count(b, 2 * H, 2 * h + 2))
                wait(act, S["weighed"], count(b, H, h - 1))
                act.activation(pT[:, h % 2, XW:2 * XW], p_t[1][0:R, 0:XW], ACT.Copy).then_inc(S["pty_ready"], 1)

            def outputs_out(b, par, g):
                wait(act, S["weighed"], count(b, H, 4 * g + 4))
                wait(act, S["o_back"], count(b, H // 4, g))
                act.activation(oT[:, :], p_o[:, 0:XW], ACT.Copy).then_inc(S["o_evac"], 1)

            def y_back(b, par, k):
                wait(act, S["yt_full"], count(b, KC, k + 1))
                wait(act, S["out_full"], count(b, NP if first else 1, 0))
                if first and (b[0] is not None or b[1] < B - 2):
                    wait(act, S["v_full"], count(b, NP, 3 * NP))
                act.activation(yT[:, k, :], p_m[:, 0:XW], ACT.Copy).then_inc(S["yt_ready"], 1)

            epi = {2: [(outputs_out, 3)], 12: [(y_back, 0)], 13: [(y_back, 1)]}
            own = {6: [(outputs_out, 0)], 10: [(outputs_out, 1)], 14: [(outputs_out, 2)]}
            pro = {1: [(x_back, 0)], 2: [(x_back, 1)], 4: [(qk_back, 0)], 5: [(qk_back, 1)], 8: [(qk_back, 2)],
                   9: [(qk_back, 3)]}

            def body(b, par, prologue, epilogue):
                for n in range(H):
                    if epilogue:
                        for step, arg in epi.get(n, []):
                            step(before(b), 1 - par, arg)
                    for step, arg in own.get(n, []):
                        step(b, par, arg)
                    if prologue:
                        for step, arg in pro.get(n, []):
                            step(after(b), 1 - par, arg)
                    if n == 15 and (b[0] is not None or b[1] < B - 2):
                        norm_scale(before(b, -2), par, 0)
                    exponentiate(b, par, n)
                    probs_back(b, par, n - 1)

            def start():
                norm_scale((None, 0, 2), 0, 0)
                act.wait_ge(S["bias_scaled"], 1)
                act.wait_ge(S["wqk_ready"], 2 * KC * KC)
                for n in range(H):
                    for step, arg in pro.get(n, []):
                        step((None, 0, 2), 0, arg)
                norm_scale((None, 1, 2), 1, 0)

            run_batches(act, start, body)
            b, par = (None, B - 1, 2), 1
            probs_back(b, par, H - 1)
            for n in range(H):
                for step, arg in epi.get(n, []):
                    step(b, par, arg)

        @block.gpsimd
        def _(pool):
            def root(b, par, _):
                wait_alone(pool, (S["aggr"], count(b, NT, NT)))
                pool.tensor_tensor(ve[:, :], mv[:, :, 1], eps[0:R, :], ALU.add).then_inc(S["eps_added"], 1)
                wait_alone(pool, (S["eps_added"], count(b, 1, 1)),
                                 (S["normed"], count(b, NT, 0)))
                pool.tensor_tensor(rs[:, :], ve[:, :], neghalf[0:R, :], ALU.pow).then_inc(S["rstd"], 1)
                wait_alone(pool, (S["rstd"], count(b, 1, 1)))
                pool.tensor_tensor(ms[:, :], mv[:, :, 0], rs[:, :], ALU.mult).then_inc(S["mean_scaled"], 1)
                wait_alone(pool, (S["mean_scaled"], count(b, 1, 1)))
                pool.tensor_tensor(ms[:, :], zeros[:, :], ms[:, :], ALU.subtract).then_inc(S["shift_made"], 1)

            def residual(b, par, blk):
                n = blk % 2
                wait_alone(pool, (S["part0"], count(b, 2 * KC, blk + 1)))
                pool.tensor_tensor(f[:, n, :], f[:, n, :], part[0][:, blk, :], ALU.subtract).then_inc(S["residual1"], 1)

            def third_part(b, par, blk):
                n = blk % 2
                wait_alone(pool, (S["part1"], count(b, 2 * KC, blk + 1)),
                                 (stacked[n], count(b, 16 * KC * STACK // HD, 0)))
                pool.tensor_tensor(part[2][:, blk, :], f[:, n, :], part[1][:, blk, :],
                                   ALU.subtract).then_inc(S["part2"], 1)

            def over_tiles(v):
                return v[:, :].rearrange("p (a c) -> p a c", a=1).to_broadcast([R, NT, C])

            def output_bias(b, par, _):
                wait_alone(pool, (S["out_added"], count(b, NP, NP)))
                hb = hid[:, rows(b, 0, NT), :]
                pool.tensor_tensor(hb, hb, over_tiles(ob), ALU.add).then_inc(S["tail_done"], 1)

            def root_y(b, par, _):
                wait_alone(pool, (S2["aggr_y"], count(b, NT, NT)))
                pool.tensor_tensor(y_ve[:, :], y_mv[:, :, 1], eps[0:R, :], ALU.add).then_inc(S2["eps_y"], 1)
                wait_alone(pool, (S2["eps_y"], count(b, 1, 1)),
                                 (S2["normed_y"], count(b, NT, 0)))
                pool.tensor_tensor(y_rs[:, :], y_ve[:, :], neghalf[0:R, :], ALU.pow).then_inc(S2["rstd_y"], 1)

            def shift(b, par, _):
                wait_alone(pool, (S["normed"], count(b, NT, NT)),
                                 (S2["summed"], count(b, 1, -1)))
                pool.tensor_tensor(xr[:, par, :, :], xn[:, :, :], over_tiles(ob2), ALU.add).then_inc(S2["shifted"], 1)

            def gain(b, par, _):
                yb = y[:, par, :, :]
                wait_alone(pool, (S2["normed_y"], count(b, NT, NT)))
                pool.tensor_tensor(yb, yb, over_tiles(ob), ALU.mult).then_inc(S2["gained"], 1)
                wait_alone(pool, (S2["gained"], count(b, 1, 1)))
                pool.tensor_tensor(yb, yb, xr[:, par, :, :], ALU.add).then_inc(S2["summed"], 1)

            def add_residual(b, par, _):
                wait_alone(pool, (S2["summed"], count(b, 1, 1)))
                hb = hid[:, rows(b, 0, NT), :]
                pool.tensor_tensor(hb, hb, y[:, par, :, :], ALU.add).then_inc(S2["resid_added"], 1)

            epi = {15: [(output_bias, 0)]} if first else {4: [(root_y, 0)], 7: [(gain, 0)], 11: [(add_residual, 0)]}
            pro = {4: [(residual, 0)], 5: [(third_part, 0), (residual, 1)], 6: [(third_part, 1)],
                   8: [(residual, 2)], 9: [(third_part, 2), (residual, 3)], 10: [(third_part, 3)]}
            if not first:
                pro[11] = [(shift, 0)]

            def body(b, par, prologue, epilogue):
                ahead = b[0] is not None or b[1] < B - 2
                for n in range(H):
                    if prologue:
                        for step, arg in pro.get(n, []):
                            step(after(b), 1 - par, arg)
                    if epilogue:
                        for step, arg in epi.get(n, []):
                            step(before(b), 1 - par, arg)
                    if ahead and n == 13:
                        root(before(b, -2), par, 0)

            def start():
                if not first:
                    pool.memset(qkb[:, :], 0.0).then_inc(S["no_bias"], 1)
                    pool.memset(vb[:, :], 0.0).then_inc(S["no_bias"], 1)
                for n in range(2):
                    pool.memset(vx[n][:, :, :, HD:VW], 1.0).then_inc(S["ones_set"], 1)
                pool.memset(zeros[:, :], 0.0).then_inc(S["zeros_set"], 1)
                pool.wait_ge(S["zeros_set"], 1)
                root((None, 0, 2), 0, 0)
                pool.wait_ge(S["consts_in"], 16 * N_CONST)
                for n in range(H):
                    for step, arg in pro.get(n, []):
                        step((None, 0, 2), 0, arg)
                root((None, 1, 2), 1, 0)
                if first:
                    tail["mask_table"](pool, table_in, S["table_ready"])

            run_batches(pool, start, body)
            for n in range(H):
                for step, arg in epi.get(n, []):
                    step((None, B - 1, 2), 1, arg)


def run_batches(eng, start, body):
    start()
    body((None, 0, 2), 0, True, False)
    body((None, 1, 2), 1, True, True)
    with eng.Fori(0, (B - 4) // 2) as i:
        for par in range(2):
            body((i, 2 + par, 2), par, True, True)
    body((None, B - 2, 2), 0, True, True)
    body((None, B - 1, 2), 1, False, True)


def attend(nc, ident, neghalf, eps, hid, bias_dram, wqkv, bqkv, wproj, bproj):
    with ExitStack() as ctx:
        bias = Memory(nc, ctx, "held").sb("bias", [R, H, CAUSAL])
        attend_with(nc, ident, neghalf, eps, hid, bias, bias_dram, wqkv, bqkv, wproj, bproj)


def attend_with(nc, ident, neghalf, eps, hid, bias, bias_dram, wqkv, bqkv, wproj, bproj):
    def load_table(sp, table_in):
        for q in range(4):
            sp.dma_start(bias[:, q * 4:(q + 1) * 4, :], bias_dram[q * 4:(q + 1) * 4, 0:R, :].rearrange("h r c -> r h c")
                         ).then_inc(table_in[q], 16)

    def mask_table(pool, table_in, table_ready):
        for q in range(4):
            pool.wait_ge(table_in[q], 16)
            for i in range(NT):
                diag = bias[:, q * 4:(q + 1) * 4, SEG[i] + R * i:SEG[i + 1]]
                pool.affine_select(out=diag, in_=diag, compare_op=ALU.is_ge, fill=NEG, base=0,
                                   pattern=[[0, 4], [-1, R]], channel_multiplier=1).then_inc(table_ready, 1)

    def load(sp, qkb, vb, ob, ob2, wo, wg, consts_in):
        for n in range(2 * KC):
            sp.dma_start(qkb[:, n:n + 1], bqkv[n * 128:(n + 1) * 128].rearrange("(h d a) -> d h a", d=HD, a=1),
                         allow_slow_non_contiguous=True).then_inc(consts_in, 16)
        for vec, sb in ((bqkv[2 * C:3 * C], vb), (bproj, ob)):
            sp.dma_start(sb[:, :], vec.rearrange("(a c) -> a c", a=1).to_broadcast([R, C])).then_inc(consts_in, 16)
        sp.dma_start(wo[:, :, :], wproj.rearrange("(k p) n -> p k n", p=128)).then_inc(consts_in, 16)

    cols = [lambda k, n=n: wqkv[k * 128:(k + 1) * 128, n * C:(n + 1) * C] for n in range(3)]
    attention(nc, ident, neghalf, eps, hid, True, *cols, float(HD) ** -0.5,
              lambda h, i: bias[:, h, SEG[i]:SEG[i + 1]],
              {"load": load, "n_const": 5 * KC + 3, "load_table": load_table, "mask_table": mask_table})


def attend_in_ffn(nc, ident, neghalf, eps, hid, logits, y_dram, h_dram, wq, wk, wv, gate_w, g1, b1):
    with ExitStack() as ctx:
        m = Memory(nc, ctx, "mask")
        mask = m.sb("mask", [R, CAUSAL])
        zeroed, masked = m.sem("zeroed"), m.sem("masked")
        with nc.Block() as block:

            @block.gpsimd
            def _(pool):
                pool.memset(mask[:, :], 0.0).then_inc(zeroed, 1)
                pool.wait_ge(zeroed, 1)
                for i in range(NT):
                    diag = mask[:, SEG[i] + R * i:SEG[i + 1]]
                    pool.affine_select(out=diag, in_=diag, compare_op=ALU.is_ge, fill=NEG, base=0,
                                       pattern=[[-1, R]], channel_multiplier=1).then_inc(masked, 1)

        def load(sp, qkb, vb, ob, ob2, wo, wg, consts_in):
            for vec, sb in ((g1, ob), (b1, ob2)):
                sp.dma_start(sb[:, :], vec.rearrange("(a c) -> a c", a=1).to_broadcast([R, C])).then_inc(consts_in, 16)
            sp.dma_start(wg[:, :, :], gate_w.rearrange("(k p) n -> p k n", p=128)).then_inc(consts_in, 16)

        cols = [lambda k, w=w: w[:, k * 128:(k + 1) * 128, :].rearrange("h p d -> p h d") for w in (wq, wk, wv)]
        attention(nc, ident, neghalf, eps, hid, False, *cols, float(C) ** -0.5,
                  lambda h, i: mask[:, SEG[i]:SEG[i + 1]],
                  {"load": load, "n_const": 3 * KC + 3, "logits": logits,
                   "y_rows": y_dram.rearrange("(g r) c -> r g c", r=R),
                   "h_rows": h_dram.rearrange("(g r) c -> r g c", r=R)})


N_TOK = B * T
SLOT = 128
SLOT_TILES = (2 * N_TOK + E * (SLOT - 1)) // SLOT
DUMP = 2 * N_TOK
N_RES = DUMP + SLOT_TILES * SLOT


def route(nc, logits, weights, expert_of, src, dst, load_weights, load_biases):
    with ExitStack() as ctx:
        m = Memory(nc, ctx, "route")
        GE = TILES * E
        NC_ = -(-N_TOK // SLOT)
        eid = m.sb("eid", [R, TILES, E])
        upper = m.sb("upper", [R, 128])
        ones = m.sb("ones", [R, 128])
        top = m.sb("top", [R, 2, TILES])
        lg2 = m.sb("lg2", [R, TILES, E])
        eq = m.sb("eq", [R, TILES, E])
        idx = m.sb("idx", [R, 2, TILES])
        hot = m.sb("hot", [R, 2, TILES, E])
        both = m.sb("both", [R, TILES, E])
        ediff = m.sb("ediff", [R, TILES])
        esum = m.sb("esum", [R, TILES])
        total = m.sb("total", [128, TILES, E])
        incl = m.sb("incl", [128, TILES, E])
        onesg = m.sb("onesg", [128, TILES])
        steps = m.sb("steps", [128, E, NC_])
        over = m.sb("over", [128, E, NC_])
        ntile = m.sb("ntile", [128, E])
        tend = m.sb("tend", [128, E])
        base = m.sb("base", [128, E])
        slot, picked = lg2, eq
        slotf = m.sb("slotf", [R, 2, TILES])
        tile_of = m.sb("tile_of", [R, 2, TILES])
        row_of = m.sb("row_of", [R, 2, TILES])
        pair_id = m.sb("pair_id", [R, 2, TILES])
        row_no = m.sb("row_no", [R, SLOT])
        tile_no = m.sb("tile_no", [R, SLOT_TILES])
        unused = m.sb("unused", [SLOT, SLOT_TILES])
        found = m.sb("found", [SLOT, SLOT_TILES])
        other = m.sb("other", [SLOT, SLOT_TILES])
        source = m.sb("source", [SLOT, SLOT_TILES])
        NB = 8
        in_row = m.sb("in_row", [R, NB, SLOT])
        in_tile = m.sb("in_tile", [R, NB, SLOT_TILES])
        tid = m.sb("tid", [1, SLOT_TILES, E])
        past = tid
        texp = m.sb("texp", [1, SLOT_TILES])
        EARLY = 3
        p_rank = m.ps("p_rank", [128, GE])
        p_total = m.ps("p_total", [128, GE])
        p_ids = m.ps("p_ids", [SLOT, 512])
        dve_step, pool_set, chosen, ranked, exp_done, placed, added = (m.sem(n) for n in (
            "dve_step", "pool_set", "chosen", "ranked", "exp_done", "placed", "added"))
        block = ctx.enter_context(nc.Block())

        def over_experts(v):
            return v.rearrange("p (g a) -> p g a", a=1).to_broadcast([v.shape[0], v.shape[1], E])

        @block.gpsimd
        def _(pool):
            pool.iota(eid[:, :, :], [[0, TILES], [1, E]], base=-E, channel_multiplier=0,
                      allow_small_or_imprecise_dtypes=True).then_inc(pool_set, 1)
            pool.memset(upper[:, :], 1.0).then_inc(pool_set, 1)
            pool.memset(ones[:, :], 1.0).then_inc(pool_set, 1)
            pool.memset(onesg[:, :], 1.0).then_inc(pool_set, 1)
            pool.iota(steps[:, :, :], [[0, E], [SLOT, NC_]], base=0, channel_multiplier=0,
                      allow_small_or_imprecise_dtypes=True).then_inc(pool_set, 1)
            pool.iota(tid[:, :, :], [[1, SLOT_TILES], [0, E]], base=0, channel_multiplier=0,
                      allow_small_or_imprecise_dtypes=True).then_inc(pool_set, 1)
            pool.iota(pair_id[:, :, :], [[N_TOK, 2], [R, TILES]], base=1, channel_multiplier=1,
                      allow_small_or_imprecise_dtypes=True).then_inc(pool_set, 1)
            pool.iota(row_no[:, :], [[1, SLOT]], base=0, channel_multiplier=0,
                      allow_small_or_imprecise_dtypes=True).then_inc(pool_set, 1)
            pool.iota(tile_no[:, :], [[1, SLOT_TILES]], base=0, channel_multiplier=0,
                      allow_small_or_imprecise_dtypes=True).then_inc(pool_set, 1)
            pool.iota(unused[:, :], [[SLOT, SLOT_TILES]], base=DUMP + 1, channel_multiplier=1,
                      allow_small_or_imprecise_dtypes=True).then_inc(pool_set, 1)
            pool.wait_ge(pool_set, 10)
            pool.affine_select(out=upper[:, :], in_=upper[:, :], compare_op=ALU.is_gt, fill=0.0, base=0,
                               pattern=[[1, 128]], channel_multiplier=-1).then_inc(pool_set, 1)

        @block.scalar
        def _(act):
            load_weights(act, range(EARLY))
            act.wait_ge(chosen, 2)
            act.activation(ediff[:, :], ediff[:, :], ACT.Exp).then_inc(exp_done, 1)
            load_weights(act, range(EARLY, E))
            load_biases(act)

        @block.tensor
        def _(pe):
            pe.wait_ge(chosen, 1)
            pe.wait_ge(pool_set, 11)
            b2 = both[:, :, :].rearrange("p g e -> p (g e)")
            pe.matmul(p_rank[:, :], upper[:, :], b2, start=True, stop=True)
            pe.matmul(p_total[:, :], ones[:, :], b2, start=True, stop=True).then_inc(ranked, 1)
            for g in range(TILES):
                for c in range(2):
                    u = 2 * g + c
                    pe.wait_ge(placed, 2 * u + 2)
                    pe.matmul(p_ids[:, 0:SLOT_TILES], in_row[:, u % NB, :], in_tile[:, u % NB, :],
                              start=(u == 0), stop=(u == 2 * TILES - 1)).then_inc(added, 1)

        @block.vector
        def _(dve):
            n_steps = [0]

            def step(ins):
                ins.then_inc(dve_step, 1)
                n_steps[0] += 1
                dve.wait_ge(dve_step, n_steps[0])

            dve.wait_ge(pool_set, 11)
            left = logits[:, :, :]
            for c in range(2):
                step(dve.tensor_reduce(top[:, c, :], left, axis=AX_X, op=ALU.max))
                step(dve.tensor_tensor(eq[:, :, :], left, over_experts(top[:, c, :]), ALU.is_equal))
                step(dve.tensor_tensor(eq[:, :, :], eq[:, :, :], eid[:, :, :], ALU.mult))
                step(dve.tensor_reduce(idx[:, c, :], eq[:, :, :], axis=AX_X, op=ALU.min))
                step(dve.tensor_tensor(hot[:, c, :, :], eid[:, :, :], over_experts(idx[:, c, :]), ALU.is_equal))
                if c == 0:
                    step(dve.scalar_tensor_tensor(out=lg2[:, :, :], in0=hot[:, 0, :, :], scalar=-BIG,
                                                  in1=left, op0=ALU.mult, op1=ALU.add))
                    left = lg2[:, :, :]
            dve.tensor_tensor(both[:, :, :], hot[:, 0, :, :], hot[:, 1, :, :], ALU.add).then_inc(chosen, 1)
            dve.tensor_tensor(ediff[:, :], top[:, 1, :], top[:, 0, :], ALU.subtract).then_inc(chosen, 1)
            dve.wait_ge(exp_done, 1)
            step(dve.tensor_scalar(esum[:, :], ediff[:, :], 1.0, None, ALU.add))
            step(dve.reciprocal(weights[:, 0, :], esum[:, :]))
            step(dve.tensor_tensor(weights[:, 1, :], ediff[:, :], weights[:, 0, :], ALU.mult))
            dve.wait_ge(ranked, 1)
            step(dve.tensor_copy(total[:, :, :], p_total[:, :].rearrange("p (g e) -> p g e", e=E)))
            for e in range(E):
                scan = dve.tensor_tensor_scan(incl[:, :, e], onesg[:, :], total[:, :, e], 0.0, ALU.mult, ALU.add)
            step(scan)
            step(dve.tensor_tensor(over[:, :, :], incl[:, TILES - 1, :].rearrange("p (e a) -> p e a", a=1)
                                   .to_broadcast([128, E, NC_]), steps[:, :, :], ALU.is_gt))
            step(dve.tensor_reduce(ntile[:, :], over[:, :, :], axis=AX_X, op=ALU.add))
            step(dve.tensor_tensor_scan(tend[:, :], onesg[:, 0:E], ntile[:, :], 0.0, ALU.mult, ALU.add))
            step(dve.tensor_tensor(base[:, :], tend[:, :], ntile[:, :], ALU.subtract))
            step(dve.tensor_scalar(base[:, :], base[:, :], float(SLOT), None, ALU.mult))
            step(dve.tensor_tensor(incl[:, :, :], incl[:, :, :], total[:, :, :], ALU.subtract))
            step(dve.tensor_tensor(slot[:, :, :], p_rank[0:R, :].rearrange("p (g e) -> p g e", e=E),
                                   incl[0:R, :, :], ALU.add))
            step(dve.tensor_tensor(slot[:, :, :], slot[:, :, :], base[0:R, :].rearrange("p (a e) -> p a e", a=1)
                                   .to_broadcast([R, TILES, E]), ALU.add))
            for c in range(2):
                step(dve.tensor_tensor(picked[:, :, :], hot[:, c, :, :], slot[:, :, :], ALU.mult))
                step(dve.tensor_reduce(slotf[:, c, :], picked[:, :, :], axis=AX_X, op=ALU.add))
            step(dve.tensor_scalar(tile_of[:, :, :], slotf[:, :, :], 1.0 / SLOT, (0.5 - SLOT / 2) / SLOT,
                                   ALU.mult, ALU.add))
            step(dve.tensor_scalar(tile_of[:, :, :], tile_of[:, :, :], float(3 * 2 ** 22), None, ALU.add))
            step(dve.tensor_scalar(tile_of[:, :, :], tile_of[:, :, :], float(-3 * 2 ** 22), None, ALU.add))
            step(dve.scalar_tensor_tensor(out=row_of[:, :, :], in0=tile_of[:, :, :], scalar=float(-SLOT),
                                          in1=slotf[:, :, :], op0=ALU.mult, op1=ALU.add))
            for g in range(TILES):
                for c in range(2):
                    u = 2 * g + c
                    if u >= NB:
                        dve.wait_ge(added, u - NB + 1)
                    dve.tensor_scalar(in_row[:, u % NB, :], row_no[:, :], row_of[:, c, g:g + 1], None,
                                      ALU.is_equal).then_inc(placed, 1)
                    dve.tensor_scalar(in_tile[:, u % NB, :], tile_no[:, :], tile_of[:, c, g:g + 1],
                                      pair_id[:, c, g:g + 1], ALU.is_equal, ALU.mult).then_inc(placed, 1)
            step(dve.tensor_tensor(past[:, :, :], tid[:, :, :], tend[0:1, :].rearrange("p (a e) -> p a e", a=1)
                                   .to_broadcast([1, SLOT_TILES, E]), ALU.is_ge))
            step(dve.tensor_reduce(texp[:, :], past[:, :, :], axis=AX_X, op=ALU.add))
            step(dve.tensor_scalar(expert_of[:, :], texp[:, :], float(E - 1), None, ALU.min))
            dve.wait_ge(added, 2 * TILES)
            step(dve.tensor_copy(found[:, :], p_ids[:, 0:SLOT_TILES]))
            step(dve.scalar_tensor_tensor(out=other[:, :], in0=found[:, :], scalar=0.0, in1=unused[:, :],
                                          op0=ALU.is_equal, op1=ALU.mult))
            step(dve.tensor_tensor(other[:, :], other[:, :], found[:, :], ALU.add))
            step(dve.tensor_scalar(dst[:, :], other[:, :], -1.0, None, ALU.add))
            step(dve.tensor_scalar(source[:, :], found[:, :], N_TOK + 0.5, float(-N_TOK), ALU.is_gt, ALU.mult))
            step(dve.tensor_tensor(source[:, :], source[:, :], found[:, :], ALU.add))
            step(dve.tensor_scalar(src[:, :], source[:, :], -1.0, 0.0, ALU.add, ALU.max))


def slot_tiles(eng, body):
    first, last = 2, 3 + (SLOT_TILES - 5) % 2
    for n in range(first):
        body((None, n, 2), n % 2, SLOT_TILES - 1 - n)
    with eng.Fori(0, (SLOT_TILES - first - last) // 2) as i:
        for par in range(2):
            body((i, first + par, 2), par, last + 1 - par)
    for n in range(SLOT_TILES - last, SLOT_TILES):
        body((None, n, 2), n % 2, SLOT_TILES - 1 - n)


def experts(nc, ident, w1, w2, b1, b2, expert_of, src, dst, y_dram, out_dram, weights_in, n_weights, biases_in, n_biases):
    FT = FF // 128
    HALF = FF // 2
    with ExitStack() as ctx:
        m = Memory(nc, ctx, "moe")
        xin = m.sb("xin", [SLOT, 2, C])
        takes = m.sb("takes", [SLOT, 2], U32)
        goes = m.sb("goes", [SLOT, 2], U32)
        xT = m.sb("xT", [128, 2, KC, SLOT])
        hid = m.sb("hid", [SLOT, 2, FF])
        hT = m.sb("hT", [128, 2, FT, SLOT])
        res = m.sb("res", [SLOT, 2, C])
        p_x = m.ps("p_x", [128, 512])
        p_h = [m.ps(f"p_h{n}", [128, 512]) for n in range(2)]
        p_t = [m.ps(f"p_t{n}", [128, 512]) for n in range(2)]
        p_y = [m.ps(f"p_y{n}", [128, 512]) for n in range(2)]
        xt_full, xt_ready, h_full, h_ready, ht_full, ht0_ready, ht1_ready, y_full, y_ready, takes_ready, goes_ready = (
            m.sem(n) for n in ("xt_full", "xt_ready", "h_full", "h_ready", "ht_full", "ht0_ready", "ht1_ready",
                               "y_full", "y_ready", "takes_ready", "goes_ready"))
        x_in = [m.sem(f"x_in{n}") for n in range(2)]
        sent = [m.sem(f"sent{n}") for n in range(2)]
        block = ctx.enter_context(nc.Block())

        def at(b, width=1, per=1):
            v = count(b, per, 0)
            return slice(v, v + width) if isinstance(v, int) else bass.ds(v, width)

        def expert(eng, t):
            return eng.value_load(expert_of[0:1, at(t)], min_val=0, max_val=E - 1)

        @block.tensor
        def _(pe):
            def transpose_x(t, par):
                wait(pe, x_in[par], lane_count(t, 16, 16))
                wait(pe, xt_ready, count(t, 1, 0))
                for k in range(KC):
                    mm = pe.transpose(p_x[:, k * 128:(k + 1) * 128], xin[:, par, k * 128:(k + 1) * 128], ident[:, :])
                mm.then_inc(xt_full, 1)

            def layer1(t, par):
                e = expert(pe, t)
                wait(pe, xt_ready, count(t, 1, 1))
                for n in range(2):
                    wait(pe, h_ready, count(t, 2, n - 1))
                    for k in range(KC):
                        mm = pe.matmul(p_h[n][:, :], xT[:, par, k, :], w1[:, k, bass.ds(e * FF + n * HALF, HALF)],
                                       start=(k == 0), stop=(k == KC - 1))
                    mm.then_inc(h_full, 1)

            def transpose_h(t, par):
                for n, evac in enumerate((ht0_ready, ht1_ready)):
                    wait(pe, h_ready, count(t, 2, n + 1))
                    wait(pe, evac, count(t, 1, 0))
                    for f in range(FT // 2):
                        at_ = (n * FT // 2 + f) * 128
                        mm = pe.transpose(p_t[n][:, f * 128:(f + 1) * 128], hid[:, par, at_:at_ + 128], ident[:, :])
                    mm.then_inc(ht_full, 1)

            def layer2(t, par):
                e = expert(pe, t)
                wait(pe, y_ready, count(t, 1, -1))
                for f in range(FT):
                    if f == 0:
                        wait(pe, ht0_ready, count(t, 1, 1))
                    if f == FT // 2:
                        wait(pe, ht1_ready, count(t, 1, 1))
                    mm = pe.matmul(p_y[par][:, 0:C], hT[:, par, f, :], w2[:, bass.ds((e * FT + f) * C, C)],
                                   start=(f == 0), stop=(f == FT - 1))
                mm.then_inc(y_full, 1)

            def body(t, par, left):
                layer1(t, par)
                if left:
                    transpose_x(after(t), 1 - par)
                if t[0] is not None or t[1] > 0:
                    layer2(before(t), 1 - par)
                transpose_h(t, par)

            pe.wait_ge(weights_in, n_weights)
            transpose_x((None, 0, 2), 0)
            slot_tiles(pe, body)
            layer2((None, SLOT_TILES - 1, 2), (SLOT_TILES - 1) % 2)

        @block.scalar
        def _(act):
            def body(t, par, left):
                for n, done in enumerate((ht0_ready, ht1_ready)):
                    wait(act, ht_full, count(t, 2, n + 1))
                    wait(act, y_full, count(t, 1, -1))
                    act.activation(hT[:, par, n * FT // 2:(n + 1) * FT // 2, :].rearrange("p f s -> p (f s)"),
                                   p_t[n][:, :], ACT.Relu).then_inc(done, 1)

            slot_tiles(act, body)

        @block.vector
        def _(dve):
            def keep_takes(t, par):
                wait(dve, x_in[par], lane_count(t, 16, 0))
                dve.tensor_copy(takes[:, par:par + 1], src[:, at(t)]).then_inc(takes_ready, 1)

            def keep_goes(t, par):
                wait(dve, sent[par], lane_count(t, 16, 0))
                dve.tensor_copy(goes[:, par:par + 1], dst[:, at(t)]).then_inc(goes_ready, 1)

            def x_back(t, par):
                wait(dve, xt_full, count(t, 1, 1))
                wait(dve, h_full, count(t, 2, -2))
                dve.tensor_copy(xT[:, par, :, :].rearrange("p k s -> p (k s)"), p_x[:, 0:C]).then_inc(xt_ready, 1)

            def add_b1(t, par):
                e = expert(dve, t)
                for n in range(2):
                    wait(dve, h_full, count(t, 2, n + 1))
                    wait(dve, ht_full, count(t, 2, -2))
                    dve.tensor_tensor(hid[:, par, n * HALF:(n + 1) * HALF], p_h[n][:, :],
                                      b1[:, bass.ds(e * FF + n * HALF, HALF)], ALU.add).then_inc(h_ready, 1)

            def result(t, par):
                e = expert(dve, t)
                wait(dve, y_full, count(t, 1, 1))
                wait(dve, sent[par], lane_count(t, 16, 0))
                dve.tensor_tensor(res[:, par, :], p_y[par][:, 0:C], b2[:, bass.ds(e * C, C)],
                                  ALU.add).then_inc(y_ready, 1)

            def body(t, par, left):
                add_b1(t, par)
                if left:
                    x_back(after(t), 1 - par)
                if t[0] is not None or t[1] > 0:
                    result(before(t), 1 - par)
                if left >= 3:
                    keep_takes(before(t, -3), 1 - par)
                keep_goes(t, par)

            for n in range(3):
                keep_takes((None, n, 2), n % 2)
            dve.wait_ge(biases_in, n_biases)
            x_back((None, 0, 2), 0)
            slot_tiles(dve, body)
            result((None, SLOT_TILES - 1, 2), (SLOT_TILES - 1) % 2)

        @block.gpsimd
        def _(pool):
            def gather(t, par):
                wait_alone(pool, (takes_ready, count(t, 1, 1)),
                                 (xt_full, count(t, 1, -1)))
                pool.indirect_dma_start(out=xin[:, par, :], out_offset=None, in_=y_dram,
                                        in_offset=bass.IndirectOffsetOnAxis(ap=takes[:, par:par + 1], axis=0)
                                        ).then_inc(x_in[par], 16)

            def send(t, par):
                wait_alone(pool, (y_ready, count(t, 1, 1)),
                                 (goes_ready, count(t, 1, 1)))
                pool.indirect_dma_start(out=out_dram, out_offset=bass.IndirectOffsetOnAxis(
                    ap=goes[:, par:par + 1], axis=0), in_=res[:, par, :], in_offset=None).then_inc(sent[par], 16)

            def body(t, par, left):
                if left >= 2:
                    gather(before(t, -2), par)
                if t[0] is not None or t[1] > 0:
                    send(before(t), 1 - par)

            gather((None, 0, 2), 0)
            gather((None, 1, 2), 1)
            slot_tiles(pool, body)
            send((None, SLOT_TILES - 1, 2), (SLOT_TILES - 1) % 2)
            for n in range(2):
                pool.wait_ge(sent[n], 16 * ((SLOT_TILES + 1 - n) // 2))


def combine(nc, neghalf, eps, weights, moe_dram, h_dram, out, g2, b2):
    with ExitStack() as ctx:
        m = Memory(nc, ctx, "comb")
        gain, shift = m.sb("gain", [R, C]), m.sb("shift", [R, C])
        WAYS = 4
        eo = m.sb("eo", [R, WAYS, 2, NT, C])
        hy = m.sb("hy", [R, WAYS, NT, C])
        acc = m.sb("acc", [R, WAYS, NT, C])
        st, mv = m.sb("st", [R, WAYS, NT, 6]), m.sb("mv", [R, WAYS, NT, 2])
        ve, rs = m.sb("ve", [R, WAYS, NT]), m.sb("rs", [R, WAYS, NT])
        ms, zeros = m.sb("ms", [R, WAYS, NT]), m.sb("zeros", [R, NT])
        (consts_in, zeros_set, weighted, mixed, stats, aggr, eps_added, rstd, mean_scaled, shift_made, normed, gained,
         shifted, summed) = (m.sem(n) for n in (
             "consts_in", "zeros_set", "weighted", "mixed", "stats", "aggr", "eps_added", "rstd", "mean_scaled",
             "shift_made", "normed", "gained", "shifted", "summed"))
        x_in = [m.sem(f"x_in{n}") for n in range(WAYS)]
        out_done = [m.sem(f"out_done{n}") for n in range(WAYS)]
        e_rows = moe_dram[0:2 * N_TOK, :].rearrange("(c g r) d -> r c g d", c=2, r=R)
        h_rows = h_dram.rearrange("(g r) c -> r g c", r=R)
        o_rows = out.rearrange("b t c -> (b t) c").rearrange("(g r) c -> r g c", r=R)
        block = ctx.enter_context(nc.Block())

        @block.sync
        def _(sp):
            for vec, sb in ((g2, gain), (b2, shift)):
                sp.dma_start(sb[:, :], vec.rearrange("(a c) -> a c", a=1).to_broadcast([R, C])).then_inc(consts_in, 16)

            def load(b, lane):
                wait_alone(sp, (summed, count(b, 1, 1 - WAYS)))
                for c in range(2):
                    sp.dma_start(eo[:, lane, c, :, :], e_rows[:, c, rows(b, 0, NT), :]).then_inc(x_in[lane], 16)
                sp.dma_start(hy[:, lane, :, :], h_rows[:, rows(b, 0, NT), :]).then_inc(x_in[lane], 16)

            skewed(sp, [(0, load)], ways=WAYS)

        @block.scalar
        def _(act):
            def weigh_first(b, lane):
                wait(act, x_in[lane], lane_count(b, 48, 48))
                wait(act, out_done[lane], lane_count(b, 16, 0))
                for j in range(NT):
                    w = weights[:, 0, rows(b, j)]
                    act.activation(acc[:, lane, j, :], eo[:, lane, 0, j, :], ACT.Copy, scale=w).then_inc(weighted, 1)

            def norm(b, lane):
                wait(act, shift_made, count(b, 1, 1))
                for j in range(NT):
                    act.activation(acc[:, lane, j, :], acc[:, lane, j, :], ACT.Identity, bias=ms[:, lane, j:j + 1],
                                   scale=rs[:, lane, j:j + 1]).then_inc(normed, 1)

            def store(b, lane):
                wait(act, summed, count(b, 1, 1))
                act.dma_start(o_rows[:, rows(b, 0, NT), :], acc[:, lane, :, :]).then_inc(out_done[lane], 16)

            skewed(act, [(2, store), (0, weigh_first), (1, norm)], ways=WAYS)
            for n in range(WAYS):
                act.wait_ge(out_done[n], 16 * B // WAYS)

        @block.vector
        def _(dve):
            def mix(b, lane):
                for j in range(NT):
                    wait(dve, weighted, count(b, NT, j + 1))
                    dve.scalar_tensor_tensor(out=acc[:, lane, j, :], in0=eo[:, lane, 1, j, :],
                                             scalar=weights[:, 1, rows(b, j)], in1=acc[:, lane, j, :],
                                             op0=ALU.mult, op1=ALU.add).then_inc(mixed, 1)
                for j in range(NT):
                    wait_alone(dve, (mixed, count(b, NT, j + 1)))
                    dve.bn_stats(st[:, lane, j, :], acc[:, lane, j, :]).then_inc(stats, 1)
                for j in range(NT):
                    wait_alone(dve, (stats, count(b, NT, j + 1)))
                    dve.bn_aggr(mv[:, lane, j, :], st[:, lane, j, :]).then_inc(aggr, 1)

            def finish(b, lane):
                ab = acc[:, lane, :, :]
                wait(dve, normed, count(b, NT, NT))
                dve.tensor_tensor(ab, ab, gain[:, :].rearrange("p (a c) -> p a c", a=1).to_broadcast([R, NT, C]),
                                  ALU.mult).then_inc(gained, 1)
                wait(dve, gained, count(b, 1, 1))
                wait(dve, shifted, count(b, 1, 1))
                dve.tensor_tensor(ab, ab, hy[:, lane, :, :], ALU.add).then_inc(summed, 1)

            dve.wait_ge(consts_in, 32)
            skewed(dve, [(0, mix), (1, finish)], ways=WAYS)

        @block.gpsimd
        def _(pool):
            def over_tiles(v):
                return v[:, :].rearrange("p (a c) -> p a c", a=1).to_broadcast([R, NT, C])

            def shift_residual(b, lane):
                wait_alone(pool, (x_in[lane], lane_count(b, 48, 48)))
                pool.tensor_tensor(hy[:, lane, :, :], hy[:, lane, :, :], over_tiles(shift), ALU.add).then_inc(shifted, 1)

            def root(b, lane):
                wait_alone(pool, (aggr, count(b, NT, NT)))
                pool.tensor_tensor(ve[:, lane, :], mv[:, lane, :, 1], eps[0:R, :], ALU.add).then_inc(eps_added, 1)
                wait_alone(pool, (eps_added, count(b, 1, 1)))
                pool.tensor_tensor(rs[:, lane, :], ve[:, lane, :], neghalf[0:R, :], ALU.pow).then_inc(rstd, 1)
                wait_alone(pool, (rstd, count(b, 1, 1)))
                pool.tensor_tensor(ms[:, lane, :], mv[:, lane, :, 0], rs[:, lane, :], ALU.mult).then_inc(mean_scaled, 1)
                wait_alone(pool, (mean_scaled, count(b, 1, 1)))
                pool.tensor_tensor(ms[:, lane, :], zeros[:, :], ms[:, lane, :], ALU.subtract).then_inc(shift_made, 1)

            pool.memset(zeros[:, :], 0.0).then_inc(zeros_set, 1)
            pool.wait_ge(zeros_set, 1)
            pool.wait_ge(consts_in, 32)
            skewed(pool, [(0, shift_residual), (0, root)], ways=WAYS)


def mixture(nc, ctx, ident, neghalf, eps, logits, y_dram, h_dram, moe_dram, out, w1, b1, w2, b2, g2, be2):
    m = Memory(nc, ctx, "mix")
    FT = FF // 128
    weights = m.sb("weights", [R, 2, TILES])
    expert_of = m.sb("expert_of", [1, SLOT_TILES], I32)
    src = m.sb("src", [SLOT, SLOT_TILES], U32)
    dst = m.sb("dst", [SLOT, SLOT_TILES], U32)
    with ExitStack() as inner:
        m = Memory(nc, inner, "mixw")
        w1s = m.sb("w1s", [128, KC, E * FF])
        w2s = m.sb("w2s", [128, E * FT * C])
        b1s = m.sb("b1s", [SLOT, E * FF])
        b2s = m.sb("b2s", [SLOT, E * C])
        weights_in, biases_in = m.sem("weights_in"), m.sem("biases_in")

        def load_weights(queue, experts_):
            for e in experts_:
                queue.dma_start(w1s[:, :, e * FF:(e + 1) * FF], w1[e].rearrange("(k p) f -> p k f", p=128)
                             ).then_inc(weights_in, 16)
                queue.dma_start(w2s[:, e * FT * C:(e + 1) * FT * C].rearrange("p (f c) -> p f c", c=C),
                             w2[e].rearrange("(f p) c -> p f c", p=128)).then_inc(weights_in, 16)

        def load_biases(queue):
            for vec, sb in ((b1, b1s), (b2, b2s)):
                queue.dma_start(sb[:, :], vec.rearrange("(a e) f -> a (e f)", a=1).to_broadcast([SLOT, sb.shape[1]])
                             ).then_inc(biases_in, 16)

        route(nc, logits, weights, expert_of, src, dst, load_weights, load_biases)
        experts(nc, ident, w1s, w2s, b1s, b2s, expert_of, src, dst, y_dram, moe_dram, weights_in, 32 * E, biases_in, 32)
    combine(nc, neghalf, eps, weights, moe_dram, h_dram, out, g2, be2)


def build(nc, x, conv_w, conv_b, fuse_w, fuse_b, fin_w, fin_b, a_wqkv, a_bqkv, a_wproj, a_bproj, a_w1, a_b1, a_w2, a_b2,
          a_c, a_l, f_wq, f_wk, f_wv, f_gate, f_w1, f_b1, f_w2, f_b2, f_g1, f_be1, f_g2, f_be2, out):
    def dram(name, shape):
        return nc.dram_tensor(name, shape, F32, kind="Internal").ap()

    nd_dram = dram("nd_scratch", (128, CAUSAL))
    bias_dram = dram("bias_scratch", (H, 128, CAUSAL))
    y_dram = dram("y_scratch", (N_TOK, C))
    h_dram = dram("h_scratch", (N_TOK, C))
    moe_dram = dram("moe_scratch", (N_RES, C))
    with ExitStack() as ctx:
        m = Memory(nc, ctx, "all")
        logits = m.sb("logits", [R, TILES, E])
        ident, neghalf, eps = constants(nc, m)
        with ExitStack() as held:
            hid = Memory(nc, held, "held").sb("hid", [R, TILES, C])
            tokenize(nc, ident, neghalf, eps, hid, nd_dram, bias_dram, x, conv_w, conv_b, fuse_w, fuse_b, fin_w, fin_b,
                     a_w1, a_b1, a_w2, a_b2, a_c, a_l)
            attend(nc, ident, neghalf, eps, hid, bias_dram, a_wqkv, a_bqkv, a_wproj, a_bproj)
            attend_in_ffn(nc, ident, neghalf, eps, hid, logits, y_dram, h_dram, f_wq, f_wk, f_wv, f_gate, f_g1, f_be1)
        mixture(nc, ctx, ident, neghalf, eps, logits, y_dram, h_dram, moe_dram, out,
                f_w1, f_b1, f_w2, f_b2, f_g2, f_be2)


_INS = ["x", "L0_tok_conv_w", "L0_tok_conv_b", "L0_tok_fusion_ln_w", "L0_tok_fusion_ln_b", "L0_tok_final_ln_w",
        "L0_tok_final_ln_b", "L0_attn_Wqkv", "L0_attn_bqkv", "L0_attn_Wproj", "L0_attn_bproj", "L0_attn_w1",
        "L0_attn_b1", "L0_attn_w2", "L0_attn_b2", "L0_attn_c_param", "L0_attn_L_multiplier", "L0_ffn_Wq", "L0_ffn_Wk",
        "L0_ffn_Wv", "L0_ffn_gate_W", "L0_ffn_W1", "L0_ffn_b1", "L0_ffn_W2", "L0_ffn_b2", "L0_ffn_ln1_g",
        "L0_ffn_ln1_b", "L0_ffn_ln2_g", "L0_ffn_ln2_b"]


def kernel(**inputs):
    import numpy as _np
    import concourse.bacc as _bacc
    from concourse import mybir as _mybir
    from concourse.bass_utils import run_bass_kernel_spmd as _run

    nc = _bacc.Bacc("TRN2", target_bir_lowering=False, num_devices=1)
    arrays, args = {}, []
    for name in _INS:
        a = _np.ascontiguousarray(inputs[name])
        if name in ("L0_attn_c_param", "L0_attn_L_multiplier"):
            a = a.reshape(1, 1)
        arrays[f"in_{name}"] = a
        args.append(nc.dram_tensor(f"in_{name}", a.shape, _mybir.dt.from_np(a.dtype), kind="ExternalInput").ap())
    args.append(nc.dram_tensor("out_0", (B, T, C), F32, kind="ExternalOutput").ap())
    build(nc, *args)
    r = _run(nc, [arrays], core_ids=[0])
    return r.results[0]["out_0"]
```
